# Optimizing a Trainium2 kernel written in Bass

```python
import numpy as np
import jax
import jax.numpy as jnp

def _softmax(x, axis=-1):
    return jax.nn.softmax(x, axis=axis)

def _gelu(x):
    return jax.nn.gelu(x, approximate=True)

def _silu(x):
    return jax.nn.silu(x)

def _sigmoid(x):
    return jax.nn.sigmoid(x)

def _layernorm(x, axis=-1, eps=1e-05):
    m = jnp.mean(x, axis=axis, keepdims=True)
    v = jnp.var(x, axis=axis, keepdims=True)
    return (x - m) / jnp.sqrt(v + eps)

def _scatter_add(tgt, idx, src, axis=0):
    return tgt.at[idx].add(src)

def _segment_sum(src, seg, n):
    return jax.ops.segment_sum(src, seg, n)
kernel_name = 'mk_early_fusion_d1_tok_img512_r4_732556'

def setup_inputs(seed: int=0):
    np.random.seed(seed)
    _w = jnp.asarray

    def _rec_inputs():
        import jax
        import jax.numpy as jnp
        _rk = jax.random.key(seed)
        x = -0.000190493 + 0.999948 * jax.random.normal(jax.random.fold_in(_rk, 1), (16, 2, 104, 104), jnp.float32)
        txt = 0.000348801 + 0.506659 * jax.random.normal(jax.random.fold_in(_rk, 2), (16, 512, 128), jnp.float32)
        return (x, txt)
    x, txt = _rec_inputs()

    def _L0_tok_setup():
        import jax, jax.numpy as jnp
        import numpy as np
        HP = 4
        PATCH = 8
        EPS = 1e-07

        def _shifts(x):
            h, w = (x.shape[2], x.shape[3])
            pad2 = ((0, 0), (0, 0))
            left_up = jnp.pad(x[:, :, HP:, :w - HP], pad2 + ((0, HP), (HP, 0)))
            right_up = jnp.pad(x[:, :, HP:, HP:], pad2 + ((0, HP), (0, HP)))
            left_down = jnp.pad(x[:, :, :h - HP, :w - HP], pad2 + ((HP, 0), (HP, 0)))
            right_down = jnp.pad(x[:, :, :h - HP, HP:], pad2 + ((HP, 0), (0, HP)))
            return (left_up, right_up, left_down, right_down)
        key = jax.random.key(seed)
        k1, k2, k3, k4 = jax.random.split(key, 4)
        B, C, S = (128, 2, 104)
        embed_dim = 128
        x = jax.random.normal(k1, (B, C, S, S), dtype=jnp.float32)
        gamma = 1.0 + 0.05 * jax.random.normal(k2, (10, S, S), dtype=jnp.float32)
        beta = 0.05 * jax.random.normal(k3, (10, S, S), dtype=jnp.float32)
        W = 0.02 * jax.random.normal(k4, (embed_dim, 10, PATCH, PATCH), dtype=jnp.float32)
        b = jnp.zeros((embed_dim,), dtype=jnp.float32)
        return {'x': x, 'gamma': gamma, 'beta': beta, 'W': W, 'b': b}
    _L0_tok_all = _L0_tok_setup()
    _L0_tok_in = {k: v for k, v in _L0_tok_all.items() if k in ('gamma', 'beta', 'W', 'b')}
    del _L0_tok_all

    def _L0_attn_setup():
        import jax, jax.numpy as jnp
        import numpy as np
        B, T, C = (8, 1024, 128)
        key = jax.random.key(seed)
        k1, k2, k3 = jax.random.split(key, 3)
        return {'x': jax.random.normal(k1, (B, T, C), dtype=jnp.float32), 'log_decay': jax.random.normal(k2, (C,), dtype=jnp.float32), 'mix_w': jax.random.normal(k3, (C, C), dtype=jnp.float32) / np.sqrt(C).astype(np.float32), 'mix_b': jnp.zeros((C,), dtype=jnp.float32)}
    _L0_attn_all = _L0_attn_setup()
    _L0_attn_in = {k: v for k, v in _L0_attn_all.items() if k in ('log_decay', 'mix_w', 'mix_b')}
    del _L0_attn_all

    def _L0_ffn_setup():
        import jax, jax.numpy as jnp
        import numpy as np
        N_EXPERT = 8
        D_MODEL = 128
        D_HIDDEN = 256
        TOP_K = 2
        key = jax.random.key(seed)
        k_x, k_g, k_gu, k_d = jax.random.split(key, 4)
        b, t = (2, 256)
        s = 0.02
        x = jax.random.normal(k_x, (b, t, D_MODEL), dtype=jnp.float32)
        Wg = jax.random.normal(k_g, (D_MODEL, N_EXPERT), dtype=jnp.float32) * s
        Wgu = jax.random.normal(k_gu, (N_EXPERT, D_MODEL, 2 * D_HIDDEN), dtype=jnp.float32) * s
        bgu = jnp.zeros((N_EXPERT, 2 * D_HIDDEN), dtype=jnp.float32)
        Wd = jax.random.normal(k_d, (N_EXPERT, D_HIDDEN, D_MODEL), dtype=jnp.float32) * s
        bd = jnp.zeros((N_EXPERT, D_MODEL), dtype=jnp.float32)
        return {'x': x, 'Wg': Wg, 'Wgu': Wgu, 'bgu': bgu, 'Wd': Wd, 'bd': bd}
    _L0_ffn_all = _L0_ffn_setup()
    _L0_ffn_in = {k: v for k, v in _L0_ffn_all.items() if k in ('Wg', 'Wgu', 'bgu', 'Wd', 'bd')}
    del _L0_ffn_all
    return {'x': x, 'txt': txt, 'L0_tok_gamma': _L0_tok_in['gamma'], 'L0_tok_beta': _L0_tok_in['beta'], 'L0_tok_W': _L0_tok_in['W'], 'L0_tok_b': _L0_tok_in['b'], 'L0_attn_log_decay': _L0_attn_in['log_decay'], 'L0_attn_mix_w': _L0_attn_in['mix_w'], 'L0_attn_mix_b': _L0_attn_in['mix_b'], 'L0_ffn_Wg': _L0_ffn_in['Wg'], 'L0_ffn_Wgu': _L0_ffn_in['Wgu'], 'L0_ffn_bgu': _L0_ffn_in['bgu'], 'L0_ffn_Wd': _L0_ffn_in['Wd'], 'L0_ffn_bd': _L0_ffn_in['bd']}

def reference(x, txt, L0_tok_gamma, L0_tok_beta, L0_tok_W, L0_tok_b, L0_attn_log_decay, L0_attn_mix_w, L0_attn_mix_b, L0_ffn_Wg, L0_ffn_Wgu, L0_ffn_bgu, L0_ffn_Wd, L0_ffn_bd):
    import jax
    import jax.numpy as jnp

    def _L0_tok_ref(x, gamma, beta, W, b):
        import jax, jax.numpy as jnp
        import numpy as np
        HP = 4
        PATCH = 8
        EPS = 1e-07

        def _shifts(x):
            h, w = (x.shape[2], x.shape[3])
            pad2 = ((0, 0), (0, 0))
            left_up = jnp.pad(x[:, :, HP:, :w - HP], pad2 + ((0, HP), (HP, 0)))
            right_up = jnp.pad(x[:, :, HP:, HP:], pad2 + ((0, HP), (0, HP)))
            left_down = jnp.pad(x[:, :, :h - HP, :w - HP], pad2 + ((HP, 0), (HP, 0)))
            right_down = jnp.pad(x[:, :, :h - HP, HP:], pad2 + ((HP, 0), (0, HP)))
            return (left_up, right_up, left_down, right_down)
        lu, ru, ld, rd = _shifts(x)
        concat = jnp.concatenate((x, lu, ru, ld, rd), axis=1)
        mean = jnp.mean(concat, axis=(1, 2, 3), keepdims=True)
        var = jnp.var(concat, axis=(1, 2, 3), keepdims=True)
        normed = (concat - mean) * jax.lax.rsqrt(var + EPS)
        normed = normed * gamma[None] + beta[None]
        y = jax.lax.conv_general_dilated(normed, W, window_strides=(PATCH, PATCH), padding='VALID', dimension_numbers=('NCHW', 'OIHW', 'NCHW'))
        y = y + b[None, :, None, None]
        B, E = (y.shape[0], y.shape[1])
        y = y.reshape(B, E, -1).transpose(0, 2, 1)
        return y

    def _L0_attn_ref(x, log_decay, mix_w, mix_b):
        import jax, jax.numpy as jnp
        import numpy as np
        B, T, C = (8, 1024, 128)
        Bx, Tx, Cx = x.shape
        decay = jax.nn.sigmoid(log_decay)
        t = jnp.arange(Tx, dtype=x.dtype)
        p_s = decay[None, :] ** t[:, None]
        p_t = decay[None, :] ** (Tx - 1 - t)[:, None]
        y = p_t[None] * jnp.cumsum(p_s[None] * x, axis=1)
        return y @ mix_w.T + mix_b

    def _L0_ffn_ref(x, Wg, Wgu, bgu, Wd, bd):
        import jax, jax.numpy as jnp
        import numpy as np
        N_EXPERT = 8
        D_MODEL = 128
        D_HIDDEN = 256
        TOP_K = 2
        b, t, d = x.shape
        xf = x.reshape(-1, d)
        N = xf.shape[0]
        logits = xf @ Wg
        topw, topi = jax.lax.top_k(logits, TOP_K)
        topw = jax.nn.softmax(topw, axis=-1)
        comb = jnp.zeros((N, N_EXPERT), dtype=xf.dtype)
        comb = comb.at[jnp.arange(N)[:, None], topi].add(topw)
        gu = jnp.einsum('nd,edh->enh', xf, Wgu) + bgu[:, None, :]
        g, u = jnp.split(gu, 2, axis=-1)
        h = jax.nn.silu(g) * u
        eo = jnp.einsum('enh,ehd->end', h, Wd) + bd[:, None, :]
        out = jnp.einsum('end,ne->nd', eo, comb)
        return out.reshape(b, t, d)
    h = _L0_tok_ref(x, L0_tok_gamma, L0_tok_beta, L0_tok_W, L0_tok_b)
    h = jnp.concatenate([h, txt], axis=1)
    h = h + _L0_attn_ref(_layernorm(h, axis=-1), L0_attn_log_decay, L0_attn_mix_w, L0_attn_mix_b)
    h = h + _L0_ffn_ref(_layernorm(h, axis=-1), L0_ffn_Wg, L0_ffn_Wgu, L0_ffn_bgu, L0_ffn_Wd, L0_ffn_bd)
    return h

_drawn_inputs = setup_inputs


def setup_inputs(seed=0):
    import zlib

    import numpy as np

    out = dict(_drawn_inputs(seed))
    spreads = {'L0_tok_b': (0.0, 0.1),
     'L0_attn_mix_b': (0.0, 0.1),
     'L0_ffn_bgu': (0.0, 0.8),
     'L0_ffn_bd': (0.0, 0.1)}
    factors = {'L0_ffn_Wgu': 4.316, 'L0_ffn_Wd': 4.279}
    for name, (base, spread) in spreads.items():
        noise = np.random.default_rng([zlib.crc32(name.encode()), seed]).standard_normal(out[name].shape)
        drawn = base * np.exp(spread * noise) if base else spread * noise
        out[name] = jnp.asarray(drawn.astype(out[name].dtype))
    for name, factor in factors.items():
        out[name] = (out[name] * factor).astype(out[name].dtype)
    return out
```

```python
from contextlib import ExitStack

import concourse.bass as bass
from concourse import mybir

F32 = mybir.dt.float32
F32R = mybir.dt.float32r
U32 = mybir.dt.uint32
ALU = mybir.AluOpType
ACT = mybir.ActivationFunctionType

P = 128
D = 128
B = 16
S = 104
PATCH = 8
HP = 4
NY = S // PATCH
GB = 8
G = B // GB
PI = NY * GB
T_IMG = NY * NY
T_TXT = 512
T = T_IMG + T_TXT
ROWS = PATCH * S
NSRC = 5
E = 8
HID = 256
HT = HID // P
W4 = 4
UN = E * HT
RING = 8
SHORT = 2
IMG_CHUNKS = 1 + (G * NY - SHORT) // W4
CHUNKS = IMG_CHUNKS + B
LAG = 4
SPLIT = 2
NA = 22
NB = 32
REV = NA * NB - T

C_ID, C_AVG, C_IOTA, C_EXP = 0, 128, 128 + PI, 128 + PI + E
C_W = C_EXP + 2 * (NA + NB)

NXG = [(0, 4), (4, 4), (8, 4), (12, 1)]


PE_AT = dict(mix=1, x_T=4, out_T=5, logits=7, comb_T=10, z_T=13)
ACT_AT = dict(down_copy=4, x_high=4, keep_h1=8, comb_out=10, image_y=13)
POOL_AT = dict(norm2=1, gate_exp=7, norm1=10, text_bias=12, text_y=14)
DVE_AT = dict(mixed=0, norm_apply=2, x_low=4, result=5, top_two=7, routing=8, text_stats=9, text_norm=11, text_sums=13)


UP_BANK = [u % 3 for u in range(UN - 1)] + [1]
UP_AGO = [next(d for d in range(1, UN) if UP_BANK[u - d] == UP_BANK[u]) for u in range(UN)]


def tiles_of(chunk):
    return {"short": (PI, SHORT), "img": (PI, W4), "txt": (P, W4)}[chunk]


def cols_of(chunk):
    p, w = tiles_of(chunk)
    return p * w


def wait(eng, sem, value):
    if not isinstance(value, int) or value > 0:
        eng.wait_ge(sem, value)


def program(nc, x, txt, gamma, beta, tokW, tokb, log_decay, mix_w, mix_b, Wg, Wgu, bgu, Wd, bd, consts, comb_dram, out):
    ctx = ExitStack()
    with ctx:
        def sb(name, shape, dt=F32):
            return ctx.enter_context(nc.sbuf_tensor(name, shape, dt))

        def bank(name):
            return ctx.enter_context(nc.psum_tensor(name, [P, 512], F32))

        def sem(name):
            return ctx.enter_context(nc.semaphore(name))

        cst = sb("cst", [P, C_W])
        ident = cst[:, C_ID:C_ID + P]
        avg = cst[0:PI, C_AVG:C_AVG + PI]
        iota = cst[:, C_IOTA:C_IOTA + E]
        wgu_hi = sb("wgu_hi", [P, E * 512], F32R)
        wgu_lo = sb("wgu_lo", [P, E * 512], F32R)
        wd_hi = sb("wd_hi", [P, E * HT * D], F32R)
        wd_lo = sb("wd_lo", [P, E * HT * D], F32R)
        wg = sb("wg", [P, E])
        wg_split = sb("wg_split", [P, 2 * E], F32R)
        bguT = sb("bguT", [P, 4 * E])
        bd_sb = sb("bd_sb", [E, D])
        wtokT = sb("wtokT", [P, NSRC * D])
        mixT = sb("mixT", [P, D])
        mixb = sb("mixb", [P, D])
        tokb_col = sb("tokb_col", [P, 1])
        pow_s = sb("pow_s", [P, NA * NB])
        pow_t = sb("pow_t", [P, NA * NB])
        one = sb("one", [P, 1])
        nhalf = sb("nhalf", [P, W4])
        euler = sb("euler", [P, W4])
        h_img = sb("h_img", [P, G * NY * D])
        wtok = h_img[:, 0:NSRC * D]
        mixw = h_img[:, NSRC * D:(NSRC + 1) * D]
        bgu_rows = h_img[0:4 * E, (NSRC + 1) * D:(NSRC + 2) * D]
        carry = sb("carry", [P, B])
        x_hi = sb("x_hi", [P, 2 * 512], F32R)
        x_lo = sb("x_lo", [P, 2 * 512], F32R)
        h_hi = sb("h_hi", [P, RING * 512], F32R)
        h_lo = sb("h_lo", [P, RING * 512], F32R)
        space = sb("space", [P, 6 * ROWS + 4 * NSRC * ROWS])
        top = [0]

        def part(n):
            top[0] += n
            assert top[0] <= space.shape[1], top[0]
            return space[:, top[0] - n:top[0]]

        xraw = part(6 * ROWS)
        patches = part(2 * NSRC * ROWS)
        gbraw = part(2 * NSRC * ROWS)
        top[0] -= 2 * NSRC * ROWS
        xgT = [part(NSRC * W4 * PI) for _ in range(2)]
        bias_e = xgT[1][:, 0:NY * PI]
        zs_i = part(GB * T_IMG)
        cum_i = part(GB * T_IMG)
        wraw = [part(512) for _ in range(2)]
        gbT = sb("gbT", [P, NSRC * NY * 2 * NY])
        z_i = sb("z_i", [P, W4 * D])
        dec_b = z_i[:, 0:2 * (NA + NB)]
        pows = z_i[:, 2 * (NA + NB):4 * (NA + NB)]
        dec = z_i[:, 4 * (NA + NB):4 * (NA + NB) + 4]
        top[0] = 0
        y_img = part(G * NY * PI)
        comb_b = part(E * 512)
        h_f = [part(512) for _ in range(4)]
        sil = [part(512) for _ in range(4)]
        silc = [part(512) for _ in range(4)]
        xt = part(512)
        h_bias = part(512)
        z = part(512)
        zs = part(512)
        cum = part(512)
        yT = part(512)
        x2 = part(512)
        h1_new = part(512)
        h1 = [part(512) for _ in range(2)]
        down_sb = part(512)
        o_sb = part(512)
        combT = [part(512)[0:E] for _ in range(2)]
        lg = part(W4 * E)
        hit = part(W4 * 2 * E)
        hitw = part(W4 * 2 * E)
        recs = sb("recs", [P, 25 * 6])
        rec1 = sb("rec1", [P, W4 * 6])
        rec2 = sb("rec2", [P, W4 * 6])
        mvi = sb("mvi", [P, 2])
        ims = sb("ims", [P, 6])
        mv1 = sb("mv1", [P, W4 * 2])
        mv2 = sb("mv2", [P, W4 * 2])
        ve1 = sb("ve1", [P, W4])
        ve2 = sb("ve2", [P, W4])
        rs1 = sb("rs1", [P, W4])
        rs2 = sb("rs2", [P, W4])
        zpad = sb("zpad", [P, 128])
        top8 = sb("top8", [P, W4 * E])
        idx8 = sb("idx8", [P, W4 * E], U32)
        gap = sb("gap", [P, W4])
        ex = sb("ex", [P, W4])
        ex1 = sb("ex1", [P, W4])
        w2 = sb("w2", [P, W4 * 2])
        comb = sb("comb", [P, W4 * E])

        gate_ps = [bank("gate0"), bank("gate1")]
        up_ps = [bank("up0"), bank("up1"), bank("up2")]
        down_ps = bank("down")
        tr_ps = bank("tr")
        mx_ps = bank("mx")
        quad = gate_ps + up_ps[0:2]
        avg_ps = up_ps[2]
        conv_ps = [down_ps, mx_ps]

        N = {}
        for name in ("const vecs wtok wmix bgu wraw0 wraw1 wgate bd gb gx0 gx1 gx2 xt comb_w store "
                     "setup small gb_patch wT wT_out gbT gbT_out wsplit_hi wsplit_lo wg_hi_done wg_lo_done dec1 dec2 dec3 powin pow_done powers "
                     "beta_mm beta_out beta_tr bias_done "
                     "im_stat im_aggr im_mean im_dev im_sq im_var im_eps im_rstd im_pad im_tr im_xg im_conv im_h im_hI "
                     "im_rec im_mv im_ve im_rs im_z im_zT im_zs im_cum im_carry im_y "
                     "rec1_ok mv1_ok ve1_ok rs1_ok z_ok zT_ok zs_ok cum_ok y_ok hb_ok mix_ok h1_ok kept_ok rec2_ok mv2_ok ve2_ok rs2_ok x2_ok "
                     "xT_ok xhi_ok xlo_ok lg_ok lsum_ok top_ok idx_ok gap_ok ex_ok ex1_ok w0_ok w1_ok hit_ok hitw_ok comb_ok combT_ok combT_sb "
                     "gate_ok up_ok sil_ok silc_ok h_ok hhi_ok hlo_ok down_ok down_out outT_ok o_ok").split():
            N[name] = sem("s_" + name)
        combb = [sem(f"s_combb{e}") for e in range(E)]
        W = type("Sems", (), N)

        block = ctx.enter_context(nc.Block())

        xraw5 = xraw.rearrange("p (t c r w) -> p t c r w", t=3, c=2, r=PATCH)
        patch5 = patches.rearrange("p (j x q w) -> p j q x w", j=NSRC, x=NY, w=PATCH)
        h_tiles = h_img[0:PI, :].rearrange("p (x g d) -> p x g d", g=G, d=D)
        gb4 = gbraw.rearrange("p (k r w) -> p k r w", k=2 * NSRC, r=PATCH)
        gbT4 = gbT[:, :].rearrange("p (j x q) -> p j x q", j=NSRC, x=NY)
        SRC_TILE = [0, 1, 1, 2, 2]
        RAW_COL = [0, 0, HP, 0, HP]
        RAW_LEN = [S, S - HP, S - HP, S - HP, S - HP]

        wd_v = Wd.rearrange("e (t q) n -> q e t n", t=HT)
        PIECES = E + E // 2
        pieces = [(Wgu[i], None, wgu_hi[:, 512 * i:512 * i + 512], wgu_lo[:, 512 * i:512 * i + 512]) for i in range(E)]
        pieces += [(wd_v[:, 2 * i:2 * i + 2, :, :], True, wd_hi[:, 512 * i:512 * i + 512],
                    wd_lo[:, 512 * i:512 * i + 512]) for i in range(E // 2)]

        def stores_before(n, kind):
            return 0 if kind == "short" else G + (n - 1) * W4 if kind == "img" else (
                G + (IMG_CHUNKS - 1) * W4 + n - IMG_CHUNKS)

        def run(body, eng):
            body(0, 0, "short", None, "img", "img", False)
            body(1, 1, "img", "short", "img", "img", False)
            body(2, 0, "img", "img", "img", "img", False)
            body(3, 1, "img", "img", "img", "img", False)
            body(4, 0, "img", "img", "img", "img", False)
            body(5, 1, "img", "img", "img", "txt", True)
            body(6, 0, "img", "img", "txt", "txt", True)
            body(7, 1, "txt", "img", "txt", "txt", True)
            with eng.Fori(0, 6) as i:
                body(i * 2 + 8, 0, "txt", "txt", "txt", "txt", True)
                body(i * 2 + 9, 1, "txt", "txt", "txt", "txt", True)
            body(20, 0, "txt", "txt", "txt", "txt", False)
            body(21, 1, "txt", "txt", "txt", None, False)
            body(22, 0, "txt", "txt", None, None, False)

        @block.sync
        def _(sp):
            sp.dma_start(cst[:, :], consts).then_inc(W.const, 16)

            def load_images(g):
                for t in range(3):
                    if g > 0:
                        sp.wait_ge(W.im_pad, g)
                    s = [W.gx0, W.gx1, W.gx2][t]
                    for c in range(2):
                        img = x[g * GB:(g + 1) * GB, c, :, :]
                        if t == 0:
                            sp.dma_start(xraw5[0:PI, 0, c, :, :].rearrange("p r w -> p (r w)"),
                                         img.rearrange("b (n r) w -> n b (r w)", r=PATCH)).then_inc(s, 16)
                            continue
                        body = img[:, HP:S - HP, :].rearrange("b (n r) w -> n b (r w)", r=PATCH)
                        if t == 1:
                            sp.dma_start(xraw5[0:PI - GB, 1, c, :, :].rearrange("p r w -> p (r w)"), body).then_inc(s, 16)
                            sp.dma_start(xraw5[PI - GB:PI, 1, c, 0:HP, :], img[:, S - HP:S, :]).then_inc(s, 16)
                        else:
                            sp.dma_start(xraw5[GB:PI, 2, c, :, :].rearrange("p r w -> p (r w)"), body).then_inc(s, 16)
                            sp.dma_start(xraw5[0:GB, 2, c, HP:PATCH, :], img[:, 0:HP, :]).then_inc(s, 16)

            load_images(0)
            sp.dma_start(gb4[0:NY].rearrange("p k r w -> p k (r w)"),
                         gamma.rearrange("k (n r) w -> n k (r w)", r=PATCH)).then_inc(W.gb, 16)
            sp.dma_start(gb4[NY:2 * NY].rearrange("p k r w -> p k (r w)"),
                         beta.rearrange("k (n r) w -> n k (r w)", r=PATCH)).then_inc(W.gb, 16)
            load_images(1)

            sp.wait_ge(W.im_xg, 2 * len(NXG) * NSRC)
            sp.wait_ge(W.im_y, 2)

            def load_text(n):
                sp.dma_start(xt.rearrange("p (j d) -> p j d", j=W4),
                             txt[bass.ds(n - IMG_CHUNKS, 1), :, :].rearrange("o (p j) d -> (o p) j d", j=W4)
                             ).then_inc(W.xt, 16)

            def send_comb(n, buf, kind):
                cols = cols_of(kind)
                sp.wait_ge(W.combT_sb, n + 1)
                sp.nop(nofuse=True)
                wait(sp, W.silc_ok, (n - 1) * UN)
                sp.nop(nofuse=True)
                sp.dma_start(comb_dram[buf, :, 0:cols], combT[buf][:, 0:cols]).then_inc(W.comb_w, 16)
                sp.wait_ge(W.comb_w, (n + 1) * 16)
                sp.nop(nofuse=True)
                for e in range(E):
                    wait(sp, W.silc_ok, (n - 1) * UN + HT * (e + 1))
                    sp.nop(nofuse=True)
                    sp.dma_start(comb_b[:, e * 512:e * 512 + cols],
                                 comb_dram[buf, e:e + 1, 0:cols].to_broadcast([P, cols])).then_inc(combb[e], 16)

            def store(n, kind):
                sp.wait_ge(W.o_ok, n + 1)
                sp.nop(nofuse=True)
                if kind == "txt":
                    sp.dma_start(out[bass.ds(n - IMG_CHUNKS, 1), T_IMG:T, :].rearrange("o (p j) d -> (o p) j d", j=W4),
                                 o_sb.rearrange("p (j d) -> p j d", j=W4)).then_inc(W.store, 16)
                    return
                first = 0 if kind == "short" else n * 2 - 1
                for g in range(G):
                    for i in range(tiles_of(kind)[1] // G):
                        dst = out[g * GB:(g + 1) * GB, 0:T_IMG, :].rearrange("b (y q) d -> q y b d", q=NY)[first + i]
                        sp.dma_start(dst, o_sb[0:PI, (i * G + g) * D:(i * G + g + 1) * D]).then_inc(W.store, 16)

            load_text(IMG_CHUNKS)
            send_comb(0, 0, "short")

            def chunk(c, buf, kind, before, after, after2, load):
                if before:
                    store(c - 1, before)
                if after:
                    send_comb(c + 1, 1 - buf, after)
                if load:
                    sp.wait_ge(W.z_ok, c + 3 - IMG_CHUNKS)
                    sp.nop(nofuse=True)
                    sp.wait_ge(W.hb_ok, c + 3 - IMG_CHUNKS)
                    sp.nop(nofuse=True)
                    load_text(c + 3)

            run(chunk, sp)
            store(CHUNKS - 1, "txt")
            sp.wait_ge(W.store, stores_before(CHUNKS, "txt") * 16)

        @block.tensor
        def _(pe):
            def mm(o, l, r, a, z_):
                return nc.tensor.matmul(o, l, r, start=a, stop=z_)

            pe.wait_ge(W.const, 16)
            pe.wait_ge(W.wtok, 16)
            for j in range(NSRC):
                dst = quad[0][:, j * D:(j + 1) * D] if j < 4 else quad[1][:, 0:D]
                nc.tensor.transpose(dst, wtok[:, j * D:(j + 1) * D], ident)
            pe.wait_ge(W.wmix, 16)
            nc.tensor.transpose(quad[1][:, D:2 * D], mixw[:, :], ident)
            pe.wait_ge(W.bgu, 16)
            nc.tensor.transpose(quad[1][:, 2 * D:2 * D + 4 * E], bgu_rows[:, :], ident[0:4 * E, 0:4 * E]).then_inc(W.wT, 1)
            gbanks = [quad[2], quad[3], tr_ps, mx_ps, down_ps]
            for j in range(NSRC):
                pe.wait_ge(W.gb_patch, j + 1)
                for nx in range(NY):
                    last = nc.tensor.transpose(gbanks[j][:, nx * 2 * NY:(nx + 1) * 2 * NY],
                                               patches[0:2 * NY, (j * NY + nx) * P:(j * NY + nx + 1) * P],
                                               ident[0:2 * NY, 0:2 * NY])
                last.then_inc(W.gbT, 1)
            def image_means(g):
                pe.wait_ge(W.im_aggr, g + 1)
                mm(avg_ps[0:PI, 0:1], avg, mvi[0:PI, 0:1], True, True).then_inc(W.im_mean, 1)
                pe.wait_ge(W.im_sq, g + 1)
                mm(avg_ps[0:PI, 1:2], avg, ims[0:PI, 2:3], True, True).then_inc(W.im_var, 1)

            image_means(0)
            pe.wait_ge(W.im_eps, 1)
            pe.wait_ge(W.wT_out, 3)
            pe.wait_ge(W.gbT_out, NSRC)
            for j in range(NSRC):
                last = mm(avg_ps[:, 0:T_IMG], wtokT[:, j * D:(j + 1) * D], gbT4[:, j, :, NY:2 * NY], j == 0, j == NSRC - 1)
            last.then_inc(W.beta_mm, 1)
            pe.wait_ge(W.beta_out, 1)
            for nx in range(NY):
                last = nc.tensor.transpose(quad[nx // 4][0:PI, (nx % 4) * D:(nx % 4 + 1) * D],
                                           bias_e[:, nx * PI:(nx + 1) * PI], ident)
            last.then_inc(W.beta_tr, 1)

            nth = 0
            conv = 0
            for g in range(G):
                if g == 0:
                    pe.wait_ge(W.bias_done, 4)
                else:
                    image_means(g)
                pe.wait_ge(W.im_pad, g + 1)

                def image_transposes(k, nth):
                    nx0, w = NXG[k]
                    for j in range(NSRC):
                        wait(pe, W.im_xg, nth + j - 3)
                        for i in range(w):
                            c0 = (j * NY + nx0 + i) * P
                            last = nc.tensor.transpose(quad[(nth + j) % 4][:, i * PI:(i + 1) * PI],
                                                       patches[0:PI, c0:c0 + P], ident[0:PI, 0:PI])
                        last.then_inc(W.im_tr, 1)

                def image_conv(k, nth, conv):
                    pe.wait_ge(W.im_xg, nth + NSRC)
                    wait(pe, W.im_h, conv - 1)
                    nx0, w = NXG[k]
                    for i in range(w):
                        for j in range(NSRC):
                            last = mm(conv_ps[conv % 2][0:PI, i * D:(i + 1) * D],
                                      xgT[conv % 2][:, (j * W4 + i) * PI:(j * W4 + i + 1) * PI],
                                      wtokT[:, j * D:(j + 1) * D], j == 0, j == NSRC - 1)
                    last.then_inc(W.im_conv, 1)

                def z_transposes(k, conv):
                    pe.wait_ge(W.im_z, conv + 1)
                    wait(pe, W.im_zs, conv)
                    nx0, w = NXG[k]
                    for i in range(w):
                        last = nc.tensor.transpose(tr_ps[:, i * PI:(i + 1) * PI], z_i[0:PI, i * D:(i + 1) * D], ident[0:PI, 0:PI])
                    last.then_inc(W.im_zT, 1)

                image_transposes(0, nth)
                for k in range(len(NXG)):
                    if k + 1 < len(NXG):
                        image_transposes(k + 1, nth + NSRC)
                    image_conv(k, nth, conv)
                    if k > 1:
                        z_transposes(k - 2, conv - 2)
                    nth += NSRC
                    conv += 1
                z_transposes(len(NXG) - 2, conv - 2)
                z_transposes(len(NXG) - 1, conv - 1)

            def z_T(n):
                pe.wait_ge(W.z_ok, n - IMG_CHUNKS + 1)
                pe.wait_ge(W.lsum_ok, n)
                for j in range(W4):
                    last = nc.tensor.transpose(tr_ps[:, j * P:(j + 1) * P], z[:, j * D:(j + 1) * D], ident)
                last.then_inc(W.zT_ok, 1)

            def mix(n, kind):
                p, w = tiles_of(kind)
                pe.wait_ge(W.y_ok, n + 1)
                wait(pe, W.combT_sb, n)
                for j in range(w):
                    lhs = yT[:, j:j + W4 * (P - 1) + 1:W4] if kind == "txt" else yT[:, j * PI:(j + 1) * PI]
                    last = mm(mx_ps[0:p, j * D:(j + 1) * D], lhs, mixT[:, :], True, True)
                last.then_inc(W.mix_ok, 1)

            def x_T(n, kind):
                p, w = tiles_of(kind)
                pe.wait_ge(W.x2_ok, n + 1)
                if kind == "txt":
                    pe.wait_ge(W.zs_ok, n - IMG_CHUNKS + 1)
                else:
                    wait(pe, W.lsum_ok, n)
                for j in range(w):
                    last = nc.tensor.transpose(tr_ps[:, j * p:(j + 1) * p], x2[0:p, j * D:(j + 1) * D], ident[0:p, 0:p])
                last.then_inc(W.xT_ok, 1)

            def logits(n, buf, kind):
                p, w = tiles_of(kind)
                pe.wait_ge(W.xhi_ok, n + 1)
                pe.wait_ge(W.xlo_ok, n + 1)
                for j in range(w):
                    o = tr_ps[0:p, j * 2 * E:(j + 1) * 2 * E]
                    xs = [v[:, buf * 512 + j * p:buf * 512 + (j + 1) * p] for v in (x_hi, x_lo)]
                    mm(o, xs[0], wg_split[:, :], True, False)
                    last = mm(o, xs[1], wg_split[:, :], False, True)
                last.then_inc(W.lg_ok, 1)

            def comb_T(n, kind):
                p, w = tiles_of(kind)
                pe.wait_ge(W.comb_ok, n + 1)
                wait(pe, W.o_ok, n - 1)
                for j in range(w):
                    last = nc.tensor.transpose(mx_ps[0:E, j * p:(j + 1) * p], comb[0:p, j * E:(j + 1) * E], ident[0:p, 0:p])
                last.then_inc(W.combT_ok, 1)

            def gate(c, buf, u, kind):
                if u == 0:
                    pe.wait_ge(W.xhi_ok, c + 1)
                    pe.wait_ge(W.xlo_ok, c + 1)
                wait(pe, W.sil_ok, c * UN + u - 1)
                into(gate_ps[u % 2], 0, buf, u, kind).then_inc(W.gate_ok, 1)

            def up(c, buf, u, kind):
                wait(pe, W.h_ok, c * UN + u - UP_AGO[u] + 1)
                into(up_ps[UP_BANK[u]], HID, buf, u, kind).then_inc(W.up_ok, 1)

            def into(ps, off, buf, u, kind):
                cols = cols_of(kind)
                e, t = divmod(u, HT)
                xs = [v[:, buf * 512:buf * 512 + cols] for v in (x_hi, x_lo)]
                o = ps[:, 0:cols]
                c0 = e * 512 + off + t * P
                mm(o, wgu_hi[:, c0:c0 + P], xs[0], True, False)
                mm(o, wgu_hi[:, c0:c0 + P], xs[1], False, False)
                return mm(o, wgu_lo[:, c0:c0 + P], xs[0], False, True)

            def down(c, buf, u, kind):
                cols = cols_of(kind)
                q = c * UN + u
                r = u % RING
                o = down_ps[:, 0:cols]
                if u == 0:
                    wait(pe, W.down_out, c)
                    pe.wait_ge(W.combT_sb, c + 1)
                    mm(o, bd_sb[:, :], combT[buf][:, 0:cols], True, False)
                pe.wait_ge(W.hhi_ok, q + 1)
                pe.wait_ge(W.hlo_ok, q + 1)
                hs = [v[:, r * 512:r * 512 + cols] for v in (h_hi, h_lo)]
                mm(o, wd_hi[:, u * D:(u + 1) * D], hs[0], False, False)
                mm(o, wd_hi[:, u * D:(u + 1) * D], hs[1], False, False)
                mm(o, wd_lo[:, u * D:(u + 1) * D], hs[0], False, u == UN - 1).then_inc(W.down_ok, 1)

            def out_T(c, kind, h1_done):
                p, w = tiles_of(kind)
                pe.wait_ge(W.down_out, c + 1)
                pe.wait_ge(W.h1_ok, h1_done)
                for j in range(w):
                    last = nc.tensor.transpose(mx_ps[0:p, j * D:(j + 1) * D], down_sb[:, j * p:(j + 1) * p], ident)
                last.then_inc(W.outT_ok, 1)

            pe.wait_ge(W.wsplit_hi, PIECES)
            pe.wait_ge(W.wsplit_lo, PIECES)
            pe.wait_ge(W.wg_hi_done, 1)
            pe.wait_ge(W.wg_lo_done, 1)
            pe.wait_ge(W.im_h, 2 * len(NXG))
            mix(0, "short")
            x_T(0, "short")
            logits(0, 0, "short")
            pe.wait_ge(W.bd, 16)
            comb_T(0, "short")
            gate(0, 0, 0, "short")

            def chunk(c, buf, kind, before, after, after2, load):
                for u in range(UN):
                    if u + 1 < UN:
                        gate(c, buf, u + 1, kind)
                    elif after:
                        gate(c + 1, 1 - buf, 0, after)
                    up(c, buf, u, kind)
                    if u >= LAG:
                        down(c, buf, u - LAG, kind)
                    elif before:
                        down(c - 1, 1 - buf, UN + u - LAG, before)
                    if u == PE_AT["mix"] and after:
                        mix(c + 1, after)
                    if u == PE_AT["x_T"] and after:
                        x_T(c + 1, after)
                    if u == PE_AT["out_T"] and before:
                        out_T(c - 1, before, c + 2 if after else c + 1)
                    if u == PE_AT["logits"] and after:
                        logits(c + 1, 1 - buf, after)
                    if u == PE_AT["comb_T"] and after:
                        comb_T(c + 1, after)
                    if u == PE_AT["z_T"] and after2 == "txt":
                        z_T(c + 2)

            run(chunk, pe)
            for u in range(UN - LAG, UN):
                down(CHUNKS - 1, (CHUNKS - 1) % 2, u, "txt")
            out_T(CHUNKS - 1, "txt", CHUNKS)

        @block.scalar
        def _(act):
            copy = nc.scalar.copy
            for dst, src, s in ((wtok.rearrange("p (o n) -> p o n", o=1), tokW.rearrange("m (o k) -> m o k", o=1), W.wtok),
                                (mixw, mix_w, W.wmix),
                                (bgu_rows, bgu.rearrange("e (k q) -> (e k) q", q=P), W.bgu),
                                (dec[:, 0:1], log_decay.rearrange("(p o) -> p o", o=1), W.vecs),
                                (tokb_col[:, :], tokb.rearrange("(p o) -> p o", o=1), W.vecs),
                                (mixb[:, :], mix_b.rearrange("(o n) -> o n", o=1).to_broadcast([P, D]), W.vecs),
                                (bd_sb[:, :], bd, W.bd),
                                (wg[:, :], Wg, W.wgate)):
                act.dma_start(dst, src).then_inc(s, 16)
            act.preload_act_table(ACT.Silu)

            act.wait_ge(W.wT, 1)
            copy(wtokT[:, 0:4 * D], quad[0][:, 0:4 * D]).then_inc(W.wT_out, 1)
            copy(wtokT[:, 4 * D:5 * D], quad[1][:, 0:D]).then_inc(W.wT_out, 1)
            copy(mixT[:, :], quad[1][:, D:2 * D]).then_inc(W.wT_out, 1)
            copy(bguT[:, :], quad[1][:, 2 * D:2 * D + 4 * E]).then_inc(W.wT_out, 1)
            gbanks = [quad[2], quad[3], tr_ps, mx_ps, down_ps]
            act.wait_ge(W.gb, 32)
            for j in range(NSRC):
                copy(patch5[0:2 * NY, j, :, :, :],
                     gb4[0:2 * NY, 2 * j:2 * j + 2, :, :].rearrange("p k r (x w) -> p (k r) x w", w=PATCH)).then_inc(W.gb_patch, 1)
            for j in range(NSRC):
                act.wait_ge(W.gbT, j + 1)
                copy(gbT[:, j * NY * 2 * NY:(j + 1) * NY * 2 * NY], gbanks[j][:, 0:NY * 2 * NY]).then_inc(W.gbT_out, 1)
            act.wait_ge(W.wgate, 16)
            copy(wg_split[:, 0:E], wg[:, :]).then_inc(W.wg_hi_done, 1)

            act.wait_ge(W.gbT, NSRC)
            act.wait_ge(W.gbT_out, NSRC)

            def load_piece(i):
                src, down_piece, _, _ = pieces[i]
                dst = wraw[i % 2].rearrange("p (e t n) -> p e t n", e=2, t=HT) if down_piece else wraw[i % 2]
                act.dma_start(dst, src).then_inc(W.wraw1 if i % 2 else W.wraw0, 16)

            load_piece(0)
            load_piece(1)
            act.wait_ge(W.beta_tr, 1)
            act.wait_ge(W.wT_out, 4)
            for k in range(4):
                w = min(4, NY - 4 * k)
                for g in range(G):
                    last = copy(h_tiles[:, 4 * k:4 * k + w, g, :], quad[k][0:PI, 0:w * D].rearrange("p (x d) -> p x d", d=D))
                last.then_inc(W.bias_done, 1)
            for i in range(PIECES):
                act.wait_ge(W.wraw1 if i % 2 else W.wraw0, (i // 2 + 1) * 16)
                copy(pieces[i][2], wraw[i % 2]).then_inc(W.wsplit_hi, 1)
                if i + 2 < PIECES:
                    act.wait_ge(W.wsplit_hi, i + 1)
                    act.wait_ge(W.wsplit_lo, i + 1)
                    load_piece(i + 2)

            def image_y(n, kind):
                if n == 0:
                    act.wait_ge(W.im_y, G)
                wait(act, W.mix_ok, n)
                first = 0 if kind == "short" else n * 4 - 2
                cols = cols_of(kind)
                copy(yT[:, 0:cols], y_img[:, bass.ds(first * PI, cols)]).then_inc(W.y_ok, 1)

            def x_high(n, buf, kind):
                act.wait_ge(W.xT_ok, n + 1)
                wait(act, W.up_ok, (n - 1) * UN)
                cols = cols_of(kind)
                copy(x_hi[:, buf * 512:buf * 512 + cols], tr_ps[:, 0:cols]).then_inc(W.xhi_ok, 1)

            def comb_out(n, buf, kind):
                act.wait_ge(W.combT_ok, n + 1)
                wait(act, W.down_ok, (n - 2) * UN + 1)
                wait(act, W.comb_w, (n - 1) * 16)
                cols = cols_of(kind)
                copy(combT[buf][:, 0:cols], mx_ps[0:E, 0:cols]).then_inc(W.combT_sb, 1)

            def keep_h1(n, buf, kind):
                p, w = tiles_of(kind)
                act.wait_ge(W.h1_ok, n + 1)
                wait(act, W.o_ok, n - 1)
                copy(h1[buf][0:p, 0:w * D], h1_new[0:p, 0:w * D]).then_inc(W.kept_ok, 1)

            def down_copy(n, kind):
                act.wait_ge(W.down_ok, (n + 1) * UN)
                wait(act, W.outT_ok, n)
                cols = cols_of(kind)
                copy(down_sb[:, 0:cols], down_ps[:, 0:cols]).then_inc(W.down_out, 1)

            def silu(c, u, kind):
                q = c * UN + u
                e, t = divmod(u, HT)
                cols = cols_of(kind)
                act.wait_ge(W.gate_ok, q + 1)
                wait(act, W.silc_ok, q - 3)
                nc.scalar.activation(sil[u % 4][:, 0:cols], gate_ps[u % 2][:, 0:cols], ACT.Silu,
                                     bias=bguT[:, 4 * e + t:4 * e + t + 1]).then_inc(W.sil_ok, 1)

            def hidden_high(c, u, kind):
                q = c * UN + u
                cols = cols_of(kind)
                act.wait_ge(W.h_ok, q + 1)
                wait(act, W.down_ok, q - RING + 1)
                r = u % RING
                copy(h_hi[:, r * 512:r * 512 + cols], h_f[u % 4][:, 0:cols]).then_inc(W.hhi_ok, 1)

            act.wait_ge(W.im_xg, 2 * len(NXG) * NSRC)
            image_y(0, "short")
            x_high(0, 0, "short")
            keep_h1(0, 0, "short")
            comb_out(0, 0, "short")
            image_y(1, "img")

            def chunk(c, buf, kind, before, after, after2, load):
                for u in range(UN):
                    silu(c, u, kind)
                    if u == ACT_AT["down_copy"] and before:
                        down_copy(c - 1, before)
                    if u >= SPLIT:
                        hidden_high(c, u - SPLIT, kind)
                    elif before:
                        hidden_high(c - 1, UN + u - SPLIT, before)
                    if u == ACT_AT["x_high"] and after:
                        x_high(c + 1, 1 - buf, after)
                    if u == ACT_AT["keep_h1"] and after:
                        keep_h1(c + 1, 1 - buf, after)
                    if u == ACT_AT["comb_out"] and after:
                        comb_out(c + 1, 1 - buf, after)
                    if u == ACT_AT["image_y"] and after2 == "img":
                        image_y(c + 2, after2)

            run(chunk, act)
            for u in range(UN - SPLIT, UN):
                hidden_high(CHUNKS - 1, u, "txt")
            down_copy(CHUNKS - 1, "txt")

        @block.gpsimd
        def _(pool):
            tt = nc.gpsimd.tensor_tensor
            nc.gpsimd.memset(euler[:, :], 2.718281828459045).then_inc(W.setup, 1)
            nc.gpsimd.memset(nhalf[:, :], -0.5).then_inc(W.setup, 1)
            pool.wait_ge(W.setup, 2)
            pool.wait_ge(W.dec1, 1)
            tt(dec[:, 2:3], euler[:, 0:1], dec[:, 1:2], ALU.pow).then_inc(W.dec2, 1)
            pool.wait_ge(W.powin, 1)
            tt(pows, dec_b, cst[:, C_EXP:C_W], ALU.pow).then_inc(W.pow_done, 1)

            pool.wait_ge(W.wg_hi_done, 1)
            tt(wg_split[:, E:2 * E], wg[:, :], wg_split[:, 0:E].bitcast(F32), ALU.subtract).then_inc(W.wg_lo_done, 1)

            def weight_low(i):
                pool.wait_ge(W.wsplit_hi, i + 1)
                tt(pieces[i][3], wraw[i % 2], pieces[i][2].bitcast(F32), ALU.subtract).then_inc(W.wsplit_lo, 1)

            def rstd(out_, var, w, ready, done, count, p):
                pool.wait_ge(ready, count)
                tt(out_[0:p, 0:w], var[0:p, 0:w], nhalf[0:p, 0:w], ALU.pow).then_inc(done, 1)

            def decayed_image_sums(g):
                pool.wait_ge(W.im_cum, g + 1)
                pool.wait_ge(W.im_pad, G)
                yv = y_img.rearrange("p (x g y b) -> p x g y b", x=NY, g=G, b=GB)[:, :, g]
                tt(yv, cum_i.rearrange("p (b y x) -> p x y b", b=GB, y=NY),
                   pow_t[:, REV:REV + T_IMG].rearrange("p (o y x) -> p x y o", o=1, y=NY).to_broadcast([P, NY, NY, GB]),
                   ALU.mult).then_inc(W.im_y, 1)

            piece = 0
            tile = 0
            for g in range(G):
                rstd(ims[:, 5:6], ims[:, 4:5], 1, W.im_eps, W.im_rstd, g + 1, PI)
                if g == 1:
                    decayed_image_sums(0)
                for k, (nx0, w) in enumerate(NXG):
                    for _ in range(2):
                        if piece < PIECES:
                            weight_low(piece)
                            piece += 1
                    wait(pool, W.im_z, tile)
                    rstd(rs1, ve1, w, W.im_ve, W.im_rs, tile + 1, PI)
                    pool.wait_ge(W.im_z, tile + 1)
                    for i in range(w):
                        o = h_img[0:PI, ((nx0 + i) * G + g) * D:((nx0 + i) * G + g + 1) * D]
                        last = tt(o, o, mixb[0:PI, :], ALU.add)
                    last.then_inc(W.im_hI, 1)
                    tile += 1
            decayed_image_sums(1)

            def norm2(n, kind):
                p, w = tiles_of(kind)
                wait(pool, W.x2_ok, n)
                rstd(rs2, ve2, w, W.ve2_ok, W.rs2_ok, n + 1, p)

            def gate_exp(n, kind):
                p, w = tiles_of(kind)
                pool.wait_ge(W.gap_ok, n + 1)
                wait(pool, W.w1_ok, n)
                tt(ex[0:p, 0:w], euler[0:p, 0:w], gap[0:p, 0:w], ALU.pow).then_inc(W.ex_ok, 1)

            def norm1(n):
                wait(pool, W.z_ok, n - IMG_CHUNKS)
                rstd(rs1, ve1, W4, W.ve1_ok, W.rs1_ok, n - IMG_CHUNKS + 1, P)

            def text_bias(n):
                pool.wait_ge(W.xt, (n - IMG_CHUNKS + 1) * 16)
                pool.wait_ge(W.h1_ok, n)
                tt(h_bias.rearrange("p (j d) -> p j d", j=W4), xt.rearrange("p (j d) -> p j d", j=W4),
                   mixb[:, :].rearrange("p (o d) -> p o d", o=1).to_broadcast([P, W4, D]), ALU.add).then_inc(W.hb_ok, 1)

            def text_y(n):
                pool.wait_ge(W.cum_ok, n - IMG_CHUNKS + 1)
                pool.wait_ge(W.mix_ok, n)
                tt(yT, cum, pow_t[:, REV + T_IMG:REV + T], ALU.mult).then_inc(W.y_ok, 1)

            def weigh(c, u, kind):
                q = c * UN + u
                e, t = divmod(u, HT)
                cols = cols_of(kind)
                if t == 0:
                    pool.wait_ge(combb[e], (c + 1) * 16)
                pool.wait_ge(W.sil_ok, q + 1)
                wait(pool, W.h_ok, q - 3)
                tt(silc[u % 4][:, 0:cols], sil[u % 4][:, 0:cols], comb_b[:, e * 512:e * 512 + cols],
                   ALU.mult).then_inc(W.silc_ok, 1)

            norm2(0, "short")
            gate_exp(0, "short")

            def chunk(c, buf, kind, before, after, after2, load):
                for u in range(UN):
                    weigh(c, u, kind)
                    if u == POOL_AT["norm2"] and after:
                        norm2(c + 1, after)
                    if u == POOL_AT["gate_exp"] and after:
                        gate_exp(c + 1, after)
                    if after2 == "txt":
                        if u == POOL_AT["norm1"]:
                            norm1(c + 2)
                        if u == POOL_AT["text_bias"]:
                            text_bias(c + 2)
                        if u == POOL_AT["text_y"]:
                            text_y(c + 2)

            run(chunk, pool)

        @block.vector
        def _(dve):
            V = nc.vector
            V.memset(one[:, :], 1.0).then_inc(W.small, 1)
            V.memset(zpad[:, :], 0.0).then_inc(W.small, 1)
            V.memset(xraw5[96:PI, 1, :, HP:PATCH, :], 0.0).then_inc(W.small, 1)
            V.memset(xraw5[0:GB, 2, :, 0:HP, :], 0.0).then_inc(W.small, 1)
            zeros = 4 * 2 * PATCH * HP
            V.memset(recs[:, 144:150], 0.0).then_inc(W.small, 1)
            dve.wait_ge(W.small, 5)
            V.memset(recs[:, 144:145], zeros / 2).then_inc(W.small, 1)
            V.memset(recs[:, 147:148], zeros / 2).then_inc(W.small, 1)
            dve.wait_ge(W.small, 7)
            dve.wait_ge(W.vecs, 48)
            V.tensor_scalar(dec[:, 1:2], dec[:, 0:1], -1.0, None, ALU.mult).then_inc(W.dec1, 1)
            dve.wait_ge(W.dec2, 1)
            V.tensor_scalar(dec[:, 3:4], dec[:, 2:3], 1.0, None, ALU.add).then_inc(W.dec3, 1)
            dve.wait_ge(W.dec3, 1)
            V.reciprocal(dec[:, 0:1], dec[:, 3:4]).then_inc(W.dec3, 1)
            dve.wait_ge(W.dec3, 2)
            dve.wait_ge(W.const, 16)
            V.tensor_copy(dec_b, dec[:, 0:1].to_broadcast([P, 2 * (NA + NB)])).then_inc(W.powin, 1)

            def image_stats(g):
                k = 0
                for t in range(3):
                    dve.wait_ge([W.gx0, W.gx1, W.gx2][t], 16 * [2, 4, 4][t] * (g + 1))
                    for c in range(2):
                        for r in range(0, PATCH, HP):
                            V.bn_stats(recs[0:PI, 6 * k:6 * k + 6],
                                       xraw5[0:PI, t, c, r:r + HP, 0:S] if t == 0 else xraw5[0:PI, t, c, r:r + HP, HP:S - HP])
                            k += 1
                for t in (1, 2):
                    for c0 in (0, S - HP):
                        last = V.bn_stats(recs[0:PI, 6 * k:6 * k + 6],
                                          xraw5[0:PI, t, :, :, c0:c0 + HP].rearrange("p c r w -> p (c r) w"))
                        k += 1
                last.then_inc(W.im_stat, 1)
                dve.wait_ge(W.im_stat, 2 * g + 1)
                V.tensor_copy(recs[0:PI, 6 * k:6 * k + 48], recs[0:PI, 24:72]).then_inc(W.im_stat, 1)
                dve.wait_ge(W.im_stat, 2 * g + 2)
                V.bn_aggr(mvi[0:PI, :], recs[0:PI, :]).then_inc(W.im_aggr, 1)
                dve.wait_ge(W.im_aggr, g + 1)
                dve.wait_ge(W.im_mean, g + 1)
                V.tensor_copy(ims[0:PI, 0:1], avg_ps[0:PI, 0:1]).then_inc(W.im_dev, 1)
                dve.wait_ge(W.im_dev, 2 * g + 1)
                V.tensor_tensor(ims[0:PI, 1:2], mvi[0:PI, 0:1], ims[0:PI, 0:1], ALU.subtract).then_inc(W.im_dev, 1)
                dve.wait_ge(W.im_dev, 2 * g + 2)
                V.scalar_tensor_tensor(ims[0:PI, 2:3], ims[0:PI, 1:2], ims[0:PI, 1:2], mvi[0:PI, 1:2],
                                       ALU.mult, ALU.add).then_inc(W.im_sq, 1)
                dve.wait_ge(W.im_var, g + 1)
                V.tensor_scalar(ims[0:PI, 4:5], avg_ps[0:PI, 1:2], 1e-7, None, ALU.add).then_inc(W.im_eps, 1)

            def image_norm(g):
                dve.wait_ge(W.im_rstd, g + 1)
                if g == 0:
                    dve.wait_ge(W.gbT, NSRC)
                else:
                    dve.wait_ge(W.im_tr, len(NXG) * NSRC)
                sc = (ims[0:PI, 0:1], ims[0:PI, 5:6], ALU.subtract, ALU.mult)
                raw = [xraw5[0:PI, t, :, :, :].rearrange("p c r w -> p (c r) w") for t in range(3)]

                grid = [v.rearrange("p q (x w) -> p q x w", w=PATCH) for v in raw]
                V.tensor_scalar(patch5[0:PI, 0], grid[0], *sc)
                zero = zpad[0:PI, 0:64].rearrange("p (r o w) -> p r o w", o=1, w=HP)
                for j in range(1, NSRC):
                    v, dst = grid[SRC_TILE[j]], patch5[0:PI, j]
                    if RAW_COL[j] == 0:
                        V.tensor_scalar(dst[:, :, :, HP:PATCH], v[:, :, :, 0:HP], *sc)
                        V.tensor_scalar(dst[:, :, 1:NY, 0:HP], v[:, :, 0:NY - 1, HP:PATCH], *sc)
                        last = V.tensor_scalar(dst[:, :, 0:1, 0:HP], zero, *sc)
                    else:
                        V.tensor_scalar(dst[:, :, :, 0:HP], v[:, :, :, HP:PATCH], *sc)
                        V.tensor_scalar(dst[:, :, 0:NY - 1, HP:PATCH], v[:, :, 1:NY, 0:HP], *sc)
                        last = V.tensor_scalar(dst[:, :, NY - 1:NY, HP:PATCH], zero, *sc)
                last.then_inc(W.im_pad, 1)

            def image_gamma(g, k, nth, conv):
                nx0, w = NXG[k]
                wait(dve, W.im_conv, conv - 1)
                for j in range(NSRC):
                    dve.wait_ge(W.im_tr, nth + j + 1)
                    V.tensor_tensor(xgT[conv % 2][:, j * W4 * PI:(j * W4 + w) * PI].rearrange("p (x y b) -> p x y b", x=w, b=GB),
                                    quad[(nth + j) % 4][:, 0:w * PI].rearrange("p (x y b) -> p x y b", x=w, b=GB),
                                    gbT4[:, j, nx0:nx0 + w, 0:NY].unsqueeze(3).to_broadcast([P, w, NY, GB]),
                                    ALU.mult).then_inc(W.im_xg, 1)

            def image_tokens(g, k, conv):
                nx0, w = NXG[k]
                dve.wait_ge(W.im_conv, conv + 1)
                hv = h_tiles[:, nx0:nx0 + w, g, :]
                V.tensor_tensor(hv, conv_ps[conv % 2][0:PI, 0:w * D].rearrange("p (x d) -> p x d", d=D),
                                hv, ALU.add).then_inc(W.im_h, 1)
                dve.wait_ge(W.im_h, conv + 1)
                for i in range(w):
                    last = V.bn_stats(rec1[0:PI, 6 * i:6 * i + 6], hv[:, i, :])
                last.then_inc(W.im_rec, 1)
                dve.wait_ge(W.im_rec, conv + 1)
                for i in range(w):
                    last = V.bn_aggr(mv1[0:PI, 2 * i:2 * i + 2], rec1[0:PI, 6 * i:6 * i + 6])
                last.then_inc(W.im_mv, 1)
                dve.wait_ge(W.im_mv, conv + 1)
                wait(dve, W.im_rs, conv)
                V.tensor_scalar(ve1[0:PI, 0:w], mv1[0:PI, 1:2 * w:2], 1e-5, None, ALU.add).then_inc(W.im_ve, 1)
                dve.wait_ge(W.im_rs, conv + 1)
                wait(dve, W.im_zT, conv)
                for i in range(w):
                    last = V.tensor_scalar(z_i[0:PI, i * D:(i + 1) * D], hv[:, i, :], mv1[0:PI, 2 * i:2 * i + 1],
                                           rs1[0:PI, i:i + 1], ALU.subtract, ALU.mult)
                last.then_inc(W.im_z, 1)

            def image_decay(g, k, conv):
                nx0, w = NXG[k]
                dve.wait_ge(W.im_zT, conv + 1)
                if k == 0:
                    wait(dve, W.im_cum, g)
                V.tensor_tensor(zs_i.rearrange("p (b y x) -> p x y b", b=GB, y=NY)[:, nx0:nx0 + w],
                                tr_ps[:, 0:w * PI].rearrange("p (x y b) -> p x y b", x=w, b=GB),
                                pow_s[:, 0:T_IMG].rearrange("p (y x o) -> p x y o", o=1, y=NY)[:, nx0:nx0 + w]
                                .to_broadcast([P, w, NY, GB]), ALU.mult).then_inc(W.im_zs, 1)

            def image_sums(g):
                dve.wait_ge(W.im_zs, (g + 1) * len(NXG))
                wait(dve, W.im_y, g)
                for b in range(GB):
                    last = V.tensor_tensor_scan(cum_i[:, b * T_IMG:(b + 1) * T_IMG], one[:, :].to_broadcast([P, T_IMG]),
                                                zs_i[:, b * T_IMG:(b + 1) * T_IMG], 0.0, ALU.mult, ALU.add)
                last.then_inc(W.im_cum, 1)
                dve.wait_ge(W.im_cum, g + 1)
                V.tensor_copy(carry[:, g * GB:(g + 1) * GB], cum_i[:, T_IMG - 1:GB * T_IMG:T_IMG]).then_inc(W.im_carry, 1)

            image_stats(0)
            dve.wait_ge(W.beta_mm, 1)
            V.tensor_scalar(bias_e.rearrange("p (q b) -> p q b", b=GB), avg_ps[:, 0:T_IMG].unsqueeze(2).to_broadcast([P, T_IMG, GB]),
                            tokb_col[:, 0:1], None, ALU.add).then_inc(W.beta_out, 1)
            dve.wait_ge(W.pow_done, 1)
            for dst, o in ((pow_s, 0), (pow_t, NA + NB)):
                V.tensor_tensor(dst[:, :].rearrange("p (a b) -> p a b", a=NA),
                                pows[:, o:o + NA].unsqueeze(2).to_broadcast([P, NA, NB]),
                                pows[:, o + NA:o + NA + NB].unsqueeze(1).to_broadcast([P, NA, NB]),
                                ALU.mult).then_inc(W.powers, 1)
            dve.wait_ge(W.bias_done, 4)
            dve.wait_ge(W.powers, 2)
            nth = conv = 0
            for g in range(G):
                if g > 0:
                    image_stats(g)
                image_norm(g)
                dve.wait_ge(W.beta_tr, 1)
                image_gamma(g, 0, nth, conv)
                for k in range(len(NXG)):
                    if k + 1 < len(NXG):
                        image_gamma(g, k + 1, nth + NSRC, conv + 1)
                    if k > 0:
                        image_tokens(g, k - 1, conv - 1)
                    if k > 1:
                        image_decay(g, k - 2, conv - 2)
                    nth += NSRC
                    conv += 1
                image_tokens(g, len(NXG) - 1, conv - 1)
                image_decay(g, len(NXG) - 2, conv - 2)
                image_decay(g, len(NXG) - 1, conv - 1)
                image_sums(g)

            def mixed(n, kind):
                p, w = tiles_of(kind)
                dve.wait_ge(W.mix_ok, n + 1)
                if kind == "txt":
                    dve.wait_ge(W.hb_ok, n - IMG_CHUNKS + 1)
                    skip = h_bias
                else:
                    first = 0 if kind == "short" else n * 4 - 2
                    skip = h_img[0:p, bass.ds(first * D, w * D)]
                wait(dve, W.kept_ok, n)
                wait(dve, W.x2_ok, n)
                V.tensor_tensor(h1_new[0:p, 0:w * D], mx_ps[0:p, 0:w * D], skip, ALU.add).then_inc(W.h1_ok, 1)
                dve.wait_ge(W.h1_ok, n + 1)
                wait(dve, W.mv2_ok, n)
                for i in range(w):
                    last = V.bn_stats(rec2[0:p, 6 * i:6 * i + 6], h1_new[0:p, i * D:(i + 1) * D])
                last.then_inc(W.rec2_ok, 1)
                dve.wait_ge(W.rec2_ok, n + 1)
                wait(dve, W.x2_ok, n)
                wait(dve, W.ve2_ok, n)
                dve.nop(nofuse=True)
                for i in range(w):
                    last = V.bn_aggr(mv2[0:p, 2 * i:2 * i + 2], rec2[0:p, 6 * i:6 * i + 6])
                last.then_inc(W.mv2_ok, 1)
                dve.wait_ge(W.mv2_ok, n + 1)
                wait(dve, W.rs2_ok, n)
                V.tensor_scalar(ve2[0:p, 0:w], mv2[0:p, 1:2 * w:2], 1e-5, None, ALU.add).then_inc(W.ve2_ok, 1)

            def norm_apply(n, kind):
                p, w = tiles_of(kind)
                dve.wait_ge(W.rs2_ok, n + 1)
                wait(dve, W.xT_ok, n)
                for i in range(w):
                    last = V.tensor_scalar(x2[0:p, i * D:(i + 1) * D], h1_new[0:p, i * D:(i + 1) * D],
                                           mv2[0:p, 2 * i:2 * i + 1], rs2[0:p, i:i + 1], ALU.subtract, ALU.mult)
                last.then_inc(W.x2_ok, 1)

            def x_low(n, buf, kind):
                cols = cols_of(kind)
                dve.wait_ge(W.xhi_ok, n + 1)
                V.tensor_tensor(x_lo[:, buf * 512:buf * 512 + cols], tr_ps[:, 0:cols],
                                x_hi[:, buf * 512:buf * 512 + cols].bitcast(F32), ALU.subtract).then_inc(W.xlo_ok, 1)

            def top_two(n, kind):
                p, w = tiles_of(kind)
                dve.wait_ge(W.lg_ok, n + 1)
                wait(dve, W.idx_ok, n)
                wait(dve, W.gap_ok, n)
                V.tensor_reduce(lg[0:p, 0:w * E], tr_ps[0:p, 0:w * 2 * E].rearrange("p (i k e) -> p i e k", k=2, e=E),
                                mybir.AxisListType.X, ALU.add).then_inc(W.lsum_ok, 1)
                dve.wait_ge(W.lsum_ok, n + 1)
                dve.nop(nofuse=True)
                for i in range(w):
                    last = V.max(top8[0:p, i * E:(i + 1) * E], lg[0:p, i * E:(i + 1) * E])
                last.then_inc(W.top_ok, 1)
                dve.wait_ge(W.top_ok, n + 1)
                wait(dve, W.hit_ok, n)
                dve.nop(nofuse=True)
                for i in range(w):
                    last = V.max_index(idx8[0:p, i * E:(i + 1) * E], top8[0:p, i * E:(i + 1) * E],
                                       lg[0:p, i * E:(i + 1) * E])
                last.then_inc(W.idx_ok, 1)
                wait(dve, W.ex_ok, n)
                V.tensor_tensor(gap[0:p, 0:w], top8[0:p, 1:w * E:E], top8[0:p, 0:w * E:E], ALU.subtract).then_inc(W.gap_ok, 1)

            def routing(n, kind):
                p, w = tiles_of(kind)
                dve.wait_ge(W.idx_ok, n + 1)
                wait(dve, W.hitw_ok, n)
                top2 = idx8[0:p, 0:w * E].rearrange("p (i e) -> p i e", e=E)[:, :, 0:2]
                V.tensor_tensor(hit[0:p, 0:w * 2 * E].rearrange("p (i k e) -> p i k e", k=2, e=E),
                                iota[0:p].unsqueeze(1).unsqueeze(1).to_broadcast([p, w, 2, E]),
                                top2.unsqueeze(3).to_broadcast([p, w, 2, E]), ALU.is_equal).then_inc(W.hit_ok, 1)
                dve.wait_ge(W.ex_ok, n + 1)
                wait(dve, W.w0_ok, n)
                V.tensor_scalar(ex1[0:p, 0:w], ex[0:p, 0:w], 1.0, None, ALU.add).then_inc(W.ex1_ok, 1)
                dve.wait_ge(W.ex1_ok, n + 1)
                V.reciprocal(w2[0:p, 0:2 * w:2], ex1[0:p, 0:w]).then_inc(W.w0_ok, 1)
                dve.wait_ge(W.w0_ok, n + 1)
                V.tensor_tensor(w2[0:p, 1:2 * w:2], ex[0:p, 0:w], w2[0:p, 0:2 * w:2], ALU.mult).then_inc(W.w1_ok, 1)
                dve.wait_ge(W.w1_ok, n + 1)
                dve.wait_ge(W.hit_ok, n + 1)
                wait(dve, W.comb_ok, n)
                V.tensor_tensor(hitw[0:p, 0:w * 2 * E].rearrange("p (i e) -> p i e", e=E),
                                hit[0:p, 0:w * 2 * E].rearrange("p (i e) -> p i e", e=E),
                                w2[0:p, 0:2 * w].unsqueeze(2).to_broadcast([p, 2 * w, E]), ALU.mult).then_inc(W.hitw_ok, 1)
                dve.wait_ge(W.hitw_ok, n + 1)
                wait(dve, W.combT_ok, n)
                hw = hitw[0:p, 0:w * 2 * E].rearrange("p (i k e) -> p i k e", k=2, e=E)
                V.tensor_tensor(comb[0:p, 0:w * E].rearrange("p (i e) -> p i e", e=E), hw[:, :, 0, :], hw[:, :, 1, :],
                                ALU.add).then_inc(W.comb_ok, 1)

            def text_stats(n):
                b = n - IMG_CHUNKS
                dve.wait_ge(W.xt, (b + 1) * 16)
                wait(dve, W.mv1_ok, b)
                for i in range(W4):
                    last = V.bn_stats(rec1[:, 6 * i:6 * i + 6], xt[:, i * D:(i + 1) * D])
                last.then_inc(W.rec1_ok, 1)
                dve.wait_ge(W.rec1_ok, b + 1)
                wait(dve, W.z_ok, b)
                wait(dve, W.ve1_ok, b)
                dve.nop(nofuse=True)
                for i in range(W4):
                    last = V.bn_aggr(mv1[:, 2 * i:2 * i + 2], rec1[:, 6 * i:6 * i + 6])
                last.then_inc(W.mv1_ok, 1)
                dve.wait_ge(W.mv1_ok, b + 1)
                wait(dve, W.rs1_ok, b)
                V.tensor_scalar(ve1[:, :], mv1[:, 1:2 * W4:2], 1e-5, None, ALU.add).then_inc(W.ve1_ok, 1)

            def text_norm(n):
                b = n - IMG_CHUNKS
                dve.wait_ge(W.rs1_ok, b + 1)
                wait(dve, W.zT_ok, b)
                for i in range(W4):
                    last = V.tensor_scalar(z[:, i * D:(i + 1) * D], xt[:, i * D:(i + 1) * D], mv1[:, 2 * i:2 * i + 1],
                                           rs1[:, i:i + 1], ALU.subtract, ALU.mult)
                last.then_inc(W.z_ok, 1)

            def text_sums(n):
                b = n - IMG_CHUNKS
                dve.wait_ge(W.zT_ok, b + 1)
                wait(dve, W.cum_ok, b)
                V.tensor_tensor(zs.rearrange("p (q j) -> p q j", j=W4), tr_ps[:, :].rearrange("p (j q) -> p q j", j=W4),
                                pow_s[:, T_IMG:T].rearrange("p (q j) -> p q j", j=W4), ALU.mult).then_inc(W.zs_ok, 1)
                dve.wait_ge(W.zs_ok, b + 1)
                dve.wait_ge(W.y_ok, n)
                V.tensor_tensor_scan(cum, one[:, :].to_broadcast([P, T_TXT]), zs, carry[:, bass.ds(b, 1)],
                                     ALU.mult, ALU.add).then_inc(W.cum_ok, 1)

            def hidden(c, u, kind):
                q = c * UN + u
                e, t = divmod(u, HT)
                cols = cols_of(kind)
                dve.wait_ge(W.up_ok, q + 1)
                dve.wait_ge(W.silc_ok, q + 1)
                wait(dve, W.hhi_ok, q - 3)
                wait(dve, W.hlo_ok, q - 3)
                k = 4 * e + HT + t
                V.scalar_tensor_tensor(h_f[u % 4][:, 0:cols], up_ps[UP_BANK[u]][:, 0:cols], bguT[:, k:k + 1],
                                       silc[u % 4][:, 0:cols], ALU.add, ALU.mult).then_inc(W.h_ok, 1)

            def hidden_low(c, u, kind):
                q = c * UN + u
                cols = cols_of(kind)
                dve.wait_ge(W.hhi_ok, q + 1)
                wait(dve, W.down_ok, q - RING + 1)
                r = u % RING
                V.tensor_tensor(h_lo[:, r * 512:r * 512 + cols], h_f[u % 4][:, 0:cols],
                                h_hi[:, r * 512:r * 512 + cols].bitcast(F32), ALU.subtract).then_inc(W.hlo_ok, 1)

            def result(n, buf, kind):
                p, w = tiles_of(kind)
                dve.wait_ge(W.outT_ok, n + 1)
                dve.wait_ge(W.kept_ok, n + 1)
                if kind != "short":
                    dve.wait_ge(W.store, stores_before(n, kind) * 16)
                V.tensor_tensor(o_sb[0:p, 0:w * D], mx_ps[0:p, 0:w * D], h1[buf][0:p, 0:w * D], ALU.add).then_inc(W.o_ok, 1)

            dve.wait_ge(W.im_carry, G)
            dve.wait_ge(W.im_hI, 2 * len(NXG))
            mixed(0, "short")
            norm_apply(0, "short")
            x_low(0, 0, "short")
            top_two(0, "short")
            routing(0, "short")

            def chunk(c, buf, kind, before, after, after2, load):
                for u in range(UN):
                    hidden(c, u, kind)
                    if u >= SPLIT:
                        hidden_low(c, u - SPLIT, kind)
                    elif before:
                        hidden_low(c - 1, UN + u - SPLIT, before)
                    if after:
                        if u == DVE_AT["mixed"]:
                            mixed(c + 1, after)
                        if u == DVE_AT["norm_apply"]:
                            norm_apply(c + 1, after)
                        if u == DVE_AT["x_low"]:
                            x_low(c + 1, 1 - buf, after)
                        if u == DVE_AT["top_two"]:
                            top_two(c + 1, after)
                        if u == DVE_AT["routing"]:
                            routing(c + 1, after)
                    if u == DVE_AT["result"] and before:
                        result(c - 1, 1 - buf, before)
                    if after2 == "txt":
                        if u == DVE_AT["text_stats"]:
                            text_stats(c + 2)
                        if u == DVE_AT["text_norm"]:
                            text_norm(c + 2)
                        if u == DVE_AT["text_sums"]:
                            text_sums(c + 2)

            run(chunk, dve)
            for u in range(UN - SPLIT, UN):
                hidden_low(CHUNKS - 1, u, "txt")
            result(CHUNKS - 1, (CHUNKS - 1) % 2, "txt")


_INS = ["x", "txt", "L0_tok_gamma", "L0_tok_beta", "L0_tok_W", "L0_tok_b", "L0_attn_log_decay", "L0_attn_mix_w",
        "L0_attn_mix_b", "L0_ffn_Wg", "L0_ffn_Wgu", "L0_ffn_bgu", "L0_ffn_Wd", "L0_ffn_bd"]


def shape_constants():
    import numpy as np
    c = np.zeros((P, C_W), np.float32)
    c[:, C_ID:C_ID + P] = np.eye(P)
    q = np.arange(PI)
    c[0:PI, C_AVG:C_AVG + PI] = (q[:, None] % GB == q[None, :] % GB) / NY
    c[:, C_IOTA:C_IOTA + E] = np.arange(E)
    c[:, C_EXP:C_W] = np.concatenate([NB * np.arange(NA), np.arange(NB), NB * np.arange(NA)[::-1], np.arange(NB)[::-1]])
    return c


def kernel(**inputs):
    import numpy as _np
    import concourse.bacc as _bacc
    from concourse import mybir as _mybir
    from concourse.bass_utils import run_bass_kernel_spmd as _run

    nc = _bacc.Bacc("TRN2", target_bir_lowering=False, num_devices=1)
    arrays, args = {}, []
    for name in _INS:
        a = _np.ascontiguousarray(inputs[name])
        if name == "L0_tok_W":
            a = a.reshape(D, -1)
        arrays[f"in_{name}_dram"] = a
        args.append(nc.dram_tensor(f"in_{name}_dram", a.shape, _mybir.dt.from_np(a.dtype), kind="ExternalInput").ap())
    c = shape_constants()
    arrays["in_const_dram"] = c
    args.append(nc.dram_tensor("in_const_dram", c.shape, _mybir.dt.from_np(c.dtype), kind="ExternalInput").ap())
    args.append(nc.dram_tensor("comb_dram", (2, E, 512), F32, kind="Internal").ap())
    args.append(nc.dram_tensor("out_0_dram", (B, T, D), F32, kind="ExternalOutput").ap())
    program(nc, *args)
    r = _run(nc, [arrays], core_ids=[0])
    return r.results[0]["out_0_dram"]
```

```python
from contextlib import ExitStack

import concourse.bass as bass
from concourse import mybir

F32 = mybir.dt.float32
F32R = mybir.dt.float32r
U32 = mybir.dt.uint32
ALU = mybir.AluOpType
ACT = mybir.ActivationFunctionType

P = 128
D = 128
B = 16
S = 104
PATCH = 8
HP = 4
NY = S // PATCH
GB = 8
G = B // GB
PI = NY * GB
T_IMG = NY * NY
T_TXT = 512
T = T_IMG + T_TXT
ROWS = PATCH * S
NSRC = 5
E = 8
HID = 256
HT = HID // P
W4 = 4
UN = E * HT
RING = 8
SHORT = 2
IMG_CHUNKS = 1 + (G * NY - SHORT) // W4
CHUNKS = IMG_CHUNKS + B
LAG = 4
SPLIT = 2
NA = 22
NB = 32
REV = NA * NB - T

C_ID, C_AVG, C_IOTA, C_EXP = 0, 128, 128 + PI, 128 + PI + E
C_W = C_EXP + 2 * (NA + NB)

NXG = [(0, 4), (4, 4), (8, 4), (12, 1)]


STEPS = [(g, nx0, w) for g in range(G) for nx0, w in NXG]
KG = len(NXG)
LAST = len(STEPS) - 1
SUM_PARTS = [(0, 0, SHORT), (0, SHORT, 5), (0, SHORT + 5, NY - SHORT - 5), (1, 0, 1), (1, 1, NY - 1)]

PE_AT = dict(mix=1, x_T=4, out_T=5, logits=7, comb_T=10, z_T=13)
ACT_AT = dict(down_copy=4, x_high=4, keep_h1=8, comb_out=10, image_y=13)
POOL_AT = dict(norm2=1, gate_exp=7, norm1=10, text_bias=12, text_y=14)
DVE_AT = dict(mixed=0, norm_apply=2, x_low=4, result=5, top_two=7, routing=8, text_stats=9, text_norm=11, text_sums=13)


UP_BANK = [u % 3 for u in range(UN - 1)] + [1]
UP_AGO = [next(d for d in range(1, UN) if UP_BANK[u - d] == UP_BANK[u]) for u in range(UN)]


def tiles_of(chunk):
    return {"short": (PI, SHORT), "img": (PI, W4), "txt": (P, W4)}[chunk]


def tiles_before(n):
    return 0 if n == 0 else SHORT + (n - 1) * W4


def needed(parts, n):
    last = min(tiles_before(n + 1), G * NY) - 1
    return 1 + next(i for i, (g, nx0, w) in enumerate(parts) if g * NY + nx0 <= last < g * NY + nx0 + w)


def cols_of(chunk):
    p, w = tiles_of(chunk)
    return p * w


def wait(eng, sem, value):
    if not isinstance(value, int) or value > 0:
        eng.wait_ge(sem, value)


def program(nc, x, txt, gamma, beta, tokW, tokb, log_decay, mix_w, mix_b, Wg, Wgu, bgu, Wd, bd, consts, comb_dram, out):
    ctx = ExitStack()
    with ctx:
        def sb(name, shape, dt=F32):
            return ctx.enter_context(nc.sbuf_tensor(name, shape, dt))

        def bank(name):
            return ctx.enter_context(nc.psum_tensor(name, [P, 512], F32))

        def sem(name):
            return ctx.enter_context(nc.semaphore(name))

        cst = sb("cst", [P, C_W])
        ident = cst[:, C_ID:C_ID + P]
        avg = cst[0:PI, C_AVG:C_AVG + PI]
        iota = cst[:, C_IOTA:C_IOTA + E]
        wgu_hi = sb("wgu_hi", [P, E * 512], F32R)
        wgu_lo = sb("wgu_lo", [P, E * 512], F32R)
        wd_hi = sb("wd_hi", [P, E * HT * D], F32R)
        wd_lo = sb("wd_lo", [P, E * HT * D], F32R)
        wg = sb("wg", [P, E])
        wg_split = sb("wg_split", [P, 2 * E], F32R)
        bguT = sb("bguT", [P, 4 * E])
        bd_sb = sb("bd_sb", [E, D])
        wtokT = sb("wtokT", [P, NSRC * D])
        mixT = sb("mixT", [P, D])
        mixb = sb("mixb", [P, D])
        tokb_col = sb("tokb_col", [P, 1])
        pow_s = sb("pow_s", [P, NA * NB])
        pow_t = sb("pow_t", [P, NA * NB])
        one = sb("one", [P, 1])
        nhalf = sb("nhalf", [P, W4])
        euler = sb("euler", [P, W4])
        h_img = sb("h_img", [P, G * NY * D])
        wtok = h_img[:, 0:NSRC * D]
        mixw = h_img[:, NSRC * D:(NSRC + 1) * D]
        bgu_rows = h_img[0:4 * E, (NSRC + 1) * D:(NSRC + 2) * D]
        carry = sb("carry", [P, B])
        x_hi = sb("x_hi", [P, 2 * 512], F32R)
        x_lo = sb("x_lo", [P, 2 * 512], F32R)
        h_hi = sb("h_hi", [P, RING * 512], F32R)
        h_lo = sb("h_lo", [P, RING * 512], F32R)
        space = sb("space", [P, 6 * ROWS + 4 * NSRC * ROWS])
        top = [0]

        def part(n):
            top[0] += n
            assert top[0] <= space.shape[1], top[0]
            return space[:, top[0] - n:top[0]]

        xraw = part(6 * ROWS)
        patches = part(2 * NSRC * ROWS)
        gbraw = part(2 * NSRC * ROWS)
        top[0] -= 2 * NSRC * ROWS
        xgT = [part(NSRC * W4 * PI) for _ in range(2)]
        bias_e = xgT[1][:, 0:NY * PI]
        zs_i = part(GB * T_IMG)
        cum_i = part(GB * T_IMG)
        wraw = [part(512) for _ in range(2)]
        gbT = sb("gbT", [P, NSRC * NY * 2 * NY])
        z_i = sb("z_i", [P, W4 * D])
        dec_b = z_i[:, 0:2 * (NA + NB)]
        pows = z_i[:, 2 * (NA + NB):4 * (NA + NB)]
        dec = z_i[:, 4 * (NA + NB):4 * (NA + NB) + 4]
        top[0] = 0
        y_img = part(G * NY * PI)
        yT = part(512)
        x2 = part(512)
        h1_new = part(512)
        h1 = [part(512)]
        lg = part(W4 * E)
        hit = part(W4 * 2 * E)
        hitw = part(W4 * 2 * E)
        assert top[0] <= 6 * ROWS
        top[0] = 6 * ROWS
        comb_b = part(E * 512)
        combT = [part(512)[0:E] for _ in range(2)]
        h_f = [part(512) for _ in range(4)]
        down_sb = part(512)
        h1.append(part(512))
        assert top[0] <= 16 * ROWS
        top[0] = 16 * ROWS
        sil = [part(512) for _ in range(4)]
        silc = [part(512) for _ in range(4)]
        top[0] = 16 * ROWS + 2 * NSRC * W4 * PI
        xt = part(512)
        h_bias = part(512)
        z = part(512)
        zs = part(512)
        cum = part(512)
        top[0] = 16 * ROWS + 2 * NSRC * W4 * PI + 2 * GB * T_IMG
        o_sb = part(512)
        recs = sb("recs", [P, 25 * 6])
        rec1 = sb("rec1", [P, W4 * 6])
        rec2 = sb("rec2", [P, W4 * 6])
        mvi = sb("mvi", [P, 2])
        ims = sb("ims", [P, 6])
        mv1 = sb("mv1", [P, W4 * 2])
        mv2 = sb("mv2", [P, W4 * 2])
        ve1 = sb("ve1", [P, W4])
        ve2 = sb("ve2", [P, W4])
        rs1 = sb("rs1", [P, W4])
        rs2 = sb("rs2", [P, W4])
        zpad = sb("zpad", [P, 128])
        top8 = sb("top8", [P, W4 * E])
        idx8 = sb("idx8", [P, W4 * E], U32)
        gap = sb("gap", [P, W4])
        ex = sb("ex", [P, W4])
        ex1 = sb("ex1", [P, W4])
        w2 = sb("w2", [P, W4 * 2])
        comb = sb("comb", [P, W4 * E])

        gate_ps = [bank("gate0"), bank("gate1")]
        up_ps = [bank("up0"), bank("up1"), bank("up2")]
        down_ps = bank("down")
        tr_ps = bank("tr")
        mx_ps = bank("mx")
        quad = gate_ps + up_ps[0:2]
        avg_ps = up_ps[2]
        beta_ps = down_ps
        conv_ps = [down_ps, mx_ps]

        N = {}
        for name in ("const ldec vecs wtok wmix bgu wraw0 wraw1 wgate bd gb gx0 gx1 gx2 xt comb_w store "
                     "setup small gb_even gb_odd wT wT_out gbT gbT_out wsplit_hi wsplit_lo wg_hi_done wg_lo_done dec1 dec2 dec3 powin pow_done powers "
                     "beta_mm beta_out beta_tr bias_done "
                     "im_stat im_aggr im_mean im_dev im_sq im_var im_eps im_rstd im_pad im_tr im_xg im_conv im_h im_hI "
                     "im_rec im_mv im_ve im_rs im_z im_zT im_zs im_cum im_carry im_y "
                     "rec1_ok mv1_ok ve1_ok rs1_ok z_ok zT_ok zs_ok cum_ok y_ok hb_ok mix_ok h1_ok kept_ok rec2_ok mv2_ok ve2_ok rs2_ok x2_ok "
                     "xT_ok xhi_ok xlo_ok lg_ok lsum_ok top_ok idx_ok gap_ok ex_ok ex1_ok w0_ok w1_ok hit_ok hitw_ok comb_ok combT_ok combT_sb "
                     "gate_ok up_ok sil_ok silc_ok h_ok hhi_ok hlo_ok down_ok down_out outT_ok o_ok").split():
            N[name] = sem("s_" + name)
        combb = [sem(f"s_combb{e}") for e in range(E)]
        W = type("Sems", (), N)

        block = ctx.enter_context(nc.Block())

        xraw5 = xraw.rearrange("p (t c r w) -> p t c r w", t=3, c=2, r=PATCH)
        patch5 = patches.rearrange("p (j x q w) -> p j q x w", j=NSRC, x=NY, w=PATCH)
        h_tiles = h_img[0:PI, :].rearrange("p (g x d) -> p x g d", g=G, d=D)
        gb4 = gbraw.rearrange("p (k r w) -> p k r w", k=2 * NSRC, r=PATCH)
        gbT4 = gbT[:, :].rearrange("p (j x q) -> p j x q", j=NSRC, x=NY)
        SRC_TILE = [0, 1, 1, 2, 2]
        RAW_COL = [0, 0, HP, 0, HP]
        RAW_LEN = [S, S - HP, S - HP, S - HP, S - HP]

        wd_v = Wd.rearrange("e (t q) n -> q e t n", t=HT)
        PIECES = E + E // 2
        pieces = [(Wgu[i], None, wgu_hi[:, 512 * i:512 * i + 512], wgu_lo[:, 512 * i:512 * i + 512]) for i in range(E)]
        pieces += [(wd_v[:, 2 * i:2 * i + 2, :, :], True, wd_hi[:, 512 * i:512 * i + 512],
                    wd_lo[:, 512 * i:512 * i + 512]) for i in range(E // 2)]

        def stores_before(n, kind):
            return 0 if kind == "short" else G + (n - 1) * W4 if kind == "img" else (
                G + (IMG_CHUNKS - 1) * W4 + n - IMG_CHUNKS)

        def run(body, eng):
            body(0, 0, "short", None, "img", "img", False)
            body(1, 1, "img", "short", "img", "img", False)
            body(2, 0, "img", "img", "img", "img", False)
            body(3, 1, "img", "img", "img", "img", False)
            body(4, 0, "img", "img", "img", "img", False)
            body(5, 1, "img", "img", "img", "txt", True)
            body(6, 0, "img", "img", "txt", "txt", True)
            body(7, 1, "txt", "img", "txt", "txt", True)
            with eng.Fori(0, 6) as i:
                body(i * 2 + 8, 0, "txt", "txt", "txt", "txt", True)
                body(i * 2 + 9, 1, "txt", "txt", "txt", "txt", True)
            body(20, 0, "txt", "txt", "txt", "txt", False)
            body(21, 1, "txt", "txt", "txt", None, False)
            body(22, 0, "txt", "txt", None, None, False)

        @block.sync
        def _(sp):
            sp.dma_start(cst[:, :], consts).then_inc(W.const, 16)

            def load_images(g):
                for t in range(3):
                    if g > 0:
                        sp.wait_ge(W.im_pad, g)
                    s = [W.gx0, W.gx1, W.gx2][t]
                    for c in range(2):
                        img = x[g * GB:(g + 1) * GB, c, :, :]
                        if t == 0:
                            sp.dma_start(xraw5[0:PI, 0, c, :, :].rearrange("p r w -> p (r w)"),
                                         img.rearrange("b (n r) w -> n b (r w)", r=PATCH)).then_inc(s, 16)
                            continue
                        body = img[:, HP:S - HP, :].rearrange("b (n r) w -> n b (r w)", r=PATCH)
                        if t == 1:
                            sp.dma_start(xraw5[0:PI - GB, 1, c, :, :].rearrange("p r w -> p (r w)"), body).then_inc(s, 16)
                            sp.dma_start(xraw5[PI - GB:PI, 1, c, 0:HP, :], img[:, S - HP:S, :]).then_inc(s, 16)
                        else:
                            sp.dma_start(xraw5[GB:PI, 2, c, :, :].rearrange("p r w -> p (r w)"), body).then_inc(s, 16)
                            sp.dma_start(xraw5[0:GB, 2, c, HP:PATCH, :], img[:, 0:HP, :]).then_inc(s, 16)

            sp.dma_start(gb4[0:NY].rearrange("p k r w -> p k (r w)"),
                         gamma.rearrange("k (n r) w -> n k (r w)", r=PATCH)).then_inc(W.gb, 16)
            sp.dma_start(gb4[NY:2 * NY].rearrange("p k r w -> p k (r w)"),
                         beta.rearrange("k (n r) w -> n k (r w)", r=PATCH)).then_inc(W.gb, 16)
            load_images(0)
            load_images(1)

            def load_text(n):
                sp.dma_start(xt.rearrange("p (j d) -> p j d", j=W4),
                             txt[bass.ds(n - IMG_CHUNKS, 1), :, :].rearrange("o (p j) d -> (o p) j d", j=W4)
                             ).then_inc(W.xt, 16)

            def send_comb(n, buf, kind):
                cols = cols_of(kind)
                sp.wait_ge(W.combT_sb, n + 1)
                sp.nop(nofuse=True)
                wait(sp, W.silc_ok, (n - 1) * UN)
                sp.nop(nofuse=True)
                sp.dma_start(comb_dram[buf, :, 0:cols], combT[buf][:, 0:cols]).then_inc(W.comb_w, 16)
                sp.wait_ge(W.comb_w, (n + 1) * 16)
                sp.nop(nofuse=True)
                for e in range(E):
                    wait(sp, W.silc_ok, (n - 1) * UN + HT * (e + 1))
                    sp.nop(nofuse=True)
                    sp.dma_start(comb_b[:, e * 512:e * 512 + cols],
                                 comb_dram[buf, e:e + 1, 0:cols].to_broadcast([P, cols])).then_inc(combb[e], 16)

            def store(n, kind):
                sp.wait_ge(W.o_ok, n + 1)
                sp.nop(nofuse=True)
                if kind == "txt":
                    sp.dma_start(out[bass.ds(n - IMG_CHUNKS, 1), T_IMG:T, :].rearrange("o (p j) d -> (o p) j d", j=W4),
                                 o_sb.rearrange("p (j d) -> p j d", j=W4)).then_inc(W.store, 16)
                    return
                for i in range(tiles_of(kind)[1]):
                    g, nx = divmod(tiles_before(n) + i, NY)
                    dst = out[g * GB:(g + 1) * GB, 0:T_IMG, :].rearrange("b (y q) d -> q y b d", q=NY)[nx]
                    sp.dma_start(dst, o_sb[0:PI, i * D:(i + 1) * D]).then_inc(W.store, 16)

            sp.wait_ge(W.im_tr, len(STEPS) * NSRC)
            send_comb(0, 0, "short")
            sp.wait_ge(W.im_cum, G)
            load_text(IMG_CHUNKS)

            def chunk(c, buf, kind, before, after, after2, load):
                if before:
                    store(c - 1, before)
                if after:
                    send_comb(c + 1, 1 - buf, after)
                if load:
                    sp.wait_ge(W.z_ok, c + 3 - IMG_CHUNKS)
                    sp.nop(nofuse=True)
                    sp.wait_ge(W.hb_ok, c + 3 - IMG_CHUNKS)
                    sp.nop(nofuse=True)
                    load_text(c + 3)

            run(chunk, sp)
            store(CHUNKS - 1, "txt")
            sp.wait_ge(W.store, stores_before(CHUNKS, "txt") * 16)

        @block.tensor
        def _(pe):
            def mm(o, l, r, a, z_):
                return nc.tensor.matmul(o, l, r, start=a, stop=z_)

            pe.wait_ge(W.const, 16)
            pe.wait_ge(W.wtok, 16)
            for j in range(NSRC):
                dst = quad[0][:, j * D:(j + 1) * D] if j < 4 else quad[1][:, 0:D]
                nc.tensor.transpose(dst, wtok[:, j * D:(j + 1) * D], ident)
            pe.wait_ge(W.wmix, 16)
            nc.tensor.transpose(quad[1][:, D:2 * D], mixw[:, :], ident)
            pe.wait_ge(W.bgu, 16)
            nc.tensor.transpose(quad[1][:, 2 * D:2 * D + 4 * E], bgu_rows[:, :], ident[0:4 * E, 0:4 * E]).then_inc(W.wT, 1)
            gbanks = [quad[2], quad[3], tr_ps, mx_ps, down_ps]
            for j in range(NSRC):
                pe.wait_ge(W.gb_odd if j % 2 else W.gb_even, j // 2 + 1)
                for nx in range(NY):
                    last = nc.tensor.transpose(gbanks[j][:, nx * 2 * NY:(nx + 1) * 2 * NY],
                                               patches[0:2 * NY, (j * NY + nx) * P:(j * NY + nx + 1) * P],
                                               ident[0:2 * NY, 0:2 * NY])
                last.then_inc(W.gbT, 1)
            pe.wait_ge(W.wT_out, 2)
            pe.wait_ge(W.gbT_out, NSRC)
            for j in range(NSRC):
                last = mm(beta_ps[:, 0:T_IMG], wtokT[:, j * D:(j + 1) * D], gbT4[:, j, :, NY:2 * NY], j == 0, j == NSRC - 1)
            last.then_inc(W.beta_mm, 1)

            def image_means(g):
                pe.wait_ge(W.im_aggr, g + 1)
                mm(avg_ps[0:PI, 0:1], avg, mvi[0:PI, 0:1], True, True).then_inc(W.im_mean, 1)
                pe.wait_ge(W.im_sq, g + 1)
                mm(avg_ps[0:PI, 1:2], avg, ims[0:PI, 2:3], True, True).then_inc(W.im_var, 1)

            image_means(0)
            pe.wait_ge(W.beta_out, 1)
            pe.wait_ge(W.wT_out, 4)
            for nx in range(NY):
                last = nc.tensor.transpose(quad[nx // 4][0:PI, (nx % 4) * D:(nx % 4 + 1) * D],
                                           bias_e[:, nx * PI:(nx + 1) * PI], ident)
            last.then_inc(W.beta_tr, 1)

            def z_T(n):
                pe.wait_ge(W.z_ok, n - IMG_CHUNKS + 1)
                pe.wait_ge(W.lsum_ok, n)
                for j in range(W4):
                    last = nc.tensor.transpose(tr_ps[:, j * P:(j + 1) * P], z[:, j * D:(j + 1) * D], ident)
                last.then_inc(W.zT_ok, 1)

            def mix(n, kind):
                p, w = tiles_of(kind)
                pe.wait_ge(W.y_ok, n + 1)
                wait(pe, W.combT_sb, n)
                for j in range(w):
                    lhs = yT[:, j:j + W4 * (P - 1) + 1:W4] if kind == "txt" else yT[:, j * PI:(j + 1) * PI]
                    last = mm(mx_ps[0:p, j * D:(j + 1) * D], lhs, mixT[:, :], True, True)
                last.then_inc(W.mix_ok, 1)

            def x_T(n, kind):
                p, w = tiles_of(kind)
                pe.wait_ge(W.x2_ok, n + 1)
                if kind == "txt":
                    pe.wait_ge(W.zs_ok, n - IMG_CHUNKS + 1)
                else:
                    wait(pe, W.lsum_ok, n)
                    if n < 2:
                        pe.wait_ge(W.im_zs, LAST - 1 if n == 0 else LAST + 1)
                for j in range(w):
                    last = nc.tensor.transpose(tr_ps[:, j * p:(j + 1) * p], x2[0:p, j * D:(j + 1) * D], ident[0:p, 0:p])
                last.then_inc(W.xT_ok, 1)

            def logits(n, buf, kind):
                p, w = tiles_of(kind)
                pe.wait_ge(W.xhi_ok, n + 1)
                pe.wait_ge(W.xlo_ok, n + 1)
                for j in range(w):
                    o = tr_ps[0:p, j * 2 * E:(j + 1) * 2 * E]
                    xs = [v[:, buf * 512 + j * p:buf * 512 + (j + 1) * p] for v in (x_hi, x_lo)]
                    mm(o, xs[0], wg_split[:, :], True, False)
                    last = mm(o, xs[1], wg_split[:, :], False, True)
                last.then_inc(W.lg_ok, 1)

            def comb_T(n, kind):
                p, w = tiles_of(kind)
                pe.wait_ge(W.comb_ok, n + 1)
                wait(pe, W.o_ok, n - 1)
                for j in range(w):
                    last = nc.tensor.transpose(mx_ps[0:E, j * p:(j + 1) * p], comb[0:p, j * E:(j + 1) * E], ident[0:p, 0:p])
                last.then_inc(W.combT_ok, 1)

            def gate(c, buf, u, kind):
                if u == 0:
                    pe.wait_ge(W.xhi_ok, c + 1)
                    pe.wait_ge(W.xlo_ok, c + 1)
                wait(pe, W.sil_ok, c * UN + u - 1)
                into(gate_ps[u % 2], 0, buf, u, kind).then_inc(W.gate_ok, 1)

            def up(c, buf, u, kind):
                wait(pe, W.h_ok, c * UN + u - UP_AGO[u] + 1)
                into(up_ps[UP_BANK[u]], HID, buf, u, kind).then_inc(W.up_ok, 1)

            def into(ps, off, buf, u, kind):
                cols = cols_of(kind)
                e, t = divmod(u, HT)
                xs = [v[:, buf * 512:buf * 512 + cols] for v in (x_hi, x_lo)]
                o = ps[:, 0:cols]
                c0 = e * 512 + off + t * P
                mm(o, wgu_hi[:, c0:c0 + P], xs[0], True, False)
                mm(o, wgu_hi[:, c0:c0 + P], xs[1], False, False)
                return mm(o, wgu_lo[:, c0:c0 + P], xs[0], False, True)

            def down(c, buf, u, kind):
                cols = cols_of(kind)
                q = c * UN + u
                r = u % RING
                o = down_ps[:, 0:cols]
                if u == 0:
                    wait(pe, W.down_out, c)
                    pe.wait_ge(W.combT_sb, c + 1)
                    mm(o, bd_sb[:, :], combT[buf][:, 0:cols], True, False)
                pe.wait_ge(W.hhi_ok, q + 1)
                pe.wait_ge(W.hlo_ok, q + 1)
                hs = [v[:, r * 512:r * 512 + cols] for v in (h_hi, h_lo)]
                mm(o, wd_hi[:, u * D:(u + 1) * D], hs[0], False, False)
                mm(o, wd_hi[:, u * D:(u + 1) * D], hs[1], False, False)
                mm(o, wd_lo[:, u * D:(u + 1) * D], hs[0], False, u == UN - 1).then_inc(W.down_ok, 1)

            def out_T(c, kind, h1_done):
                p, w = tiles_of(kind)
                pe.wait_ge(W.down_out, c + 1)
                pe.wait_ge(W.h1_ok, h1_done)
                for j in range(w):
                    last = nc.tensor.transpose(mx_ps[0:p, j * D:(j + 1) * D], down_sb[:, j * p:(j + 1) * p], ident)
                last.then_inc(W.outT_ok, 1)

            def chunk(c, buf, kind, before, after, after2, load):
                for u in range(UN):
                    if u + 1 < UN:
                        gate(c, buf, u + 1, kind)
                    elif after:
                        gate(c + 1, 1 - buf, 0, after)
                    up(c, buf, u, kind)
                    if u >= LAG:
                        down(c, buf, u - LAG, kind)
                    elif before:
                        down(c - 1, 1 - buf, UN + u - LAG, before)
                    if u == PE_AT["mix"] and after:
                        mix(c + 1, after)
                    if u == PE_AT["x_T"] and after:
                        x_T(c + 1, after)
                    if u == PE_AT["out_T"] and before:
                        out_T(c - 1, before, c + 2 if after else c + 1)
                    if u == PE_AT["logits"] and after:
                        logits(c + 1, 1 - buf, after)
                    if u == PE_AT["comb_T"] and after:
                        comb_T(c + 1, after)
                    if u == PE_AT["z_T"] and after2 == "txt":
                        z_T(c + 2)

            def image_transposes(s):
                g, nx0, w = STEPS[s]
                if s % KG == 0:
                    if g > 0:
                        image_means(g)
                    pe.wait_ge(W.im_pad, g + 1)
                for j in range(NSRC):
                    n = s * NSRC + j
                    if n < 4:
                        pe.wait_ge(W.bias_done, n + 1)
                    wait(pe, W.im_xg, n - 3)
                    for i in range(w):
                        c0 = (j * NY + nx0 + i) * P
                        last = nc.tensor.transpose(quad[n % 4][:, i * PI:(i + 1) * PI],
                                                   patches[0:PI, c0:c0 + P], ident[0:PI, 0:PI])
                    last.then_inc(W.im_tr, 1)

            def image_conv(s):
                g, nx0, w = STEPS[s]
                pe.wait_ge(W.im_xg, (s + 1) * NSRC)
                wait(pe, W.im_h, s - 1)
                if s == LAST:
                    pe.wait_ge(W.h1_ok, 1)
                for i in range(w):
                    for j in range(NSRC):
                        last = mm(conv_ps[s % 2][0:PI, i * D:(i + 1) * D],
                                  xgT[s % 2][:, (j * W4 + i) * PI:(j * W4 + i + 1) * PI],
                                  wtokT[:, j * D:(j + 1) * D], j == 0, j == NSRC - 1)
                last.then_inc(W.im_conv, 1)

            def z_transposes(s):
                g, nx0, w = STEPS[s]
                pe.wait_ge(W.im_z, s + 1)
                wait(pe, W.im_zs, s)
                for i in range(w):
                    last = nc.tensor.transpose(tr_ps[:, i * PI:(i + 1) * PI], z_i[0:PI, i * D:(i + 1) * D], ident[0:PI, 0:PI])
                last.then_inc(W.im_zT, 1)

            image_transposes(0)
            for s in range(len(STEPS)):
                if s + 1 < len(STEPS):
                    image_transposes(s + 1)
                if s > 1:
                    z_transposes(s - 2)
                image_conv(s)
                if s == LAST - 1:
                    pe.wait_ge(W.im_h, LAST - 1)
                    mix(0, "short")
            x_T(0, "short")
            pe.wait_ge(W.wg_hi_done, 1)
            pe.wait_ge(W.wg_lo_done, 1)
            logits(0, 0, "short")
            pe.wait_ge(W.lsum_ok, 1)
            z_transposes(LAST - 1)
            pe.wait_ge(W.wsplit_hi, PIECES)
            pe.wait_ge(W.wsplit_lo, PIECES)
            gate(0, 0, 0, "short")
            z_transposes(LAST)
            pe.wait_ge(W.im_h, LAST + 1)
            pe.wait_ge(W.bd, 16)
            comb_T(0, "short")

            run(chunk, pe)
            for u in range(UN - LAG, UN):
                down(CHUNKS - 1, (CHUNKS - 1) % 2, u, "txt")
            out_T(CHUNKS - 1, "txt", CHUNKS)

        @block.scalar
        def _(act):
            copy = nc.scalar.copy
            for dst, src, s in ((dec[:, 0:1], log_decay.rearrange("(p o) -> p o", o=1), W.ldec),
                                (wtok.rearrange("p (o n) -> p o n", o=1), tokW.rearrange("m (o k) -> m o k", o=1), W.wtok),
                                (mixw, mix_w, W.wmix),
                                (bgu_rows, bgu.rearrange("e (k q) -> (e k) q", q=P), W.bgu),
                                (tokb_col[:, :], tokb.rearrange("(p o) -> p o", o=1), W.vecs),
                                (mixb[:, :], mix_b.rearrange("(o n) -> o n", o=1).to_broadcast([P, D]), W.vecs),
                                (bd_sb[:, :], bd, W.bd),
                                (wg[:, :], Wg, W.wgate)):
                act.dma_start(dst, src).then_inc(s, 16)
            act.preload_act_table(ACT.Silu)

            act.wait_ge(W.wT, 1)
            copy(wtokT[:, 0:4 * D], quad[0][:, 0:4 * D]).then_inc(W.wT_out, 1)
            copy(wtokT[:, 4 * D:5 * D], quad[1][:, 0:D]).then_inc(W.wT_out, 1)
            copy(mixT[:, :], quad[1][:, D:2 * D]).then_inc(W.wT_out, 1)
            copy(bguT[:, :], quad[1][:, 2 * D:2 * D + 4 * E]).then_inc(W.wT_out, 1)
            gbanks = [quad[2], quad[3], tr_ps, mx_ps, down_ps]
            act.wait_ge(W.gb, 32)
            for j in range(1, NSRC, 2):
                copy(patch5[0:2 * NY, j, :, :, :],
                     gb4[0:2 * NY, 2 * j:2 * j + 2, :, :].rearrange("p k r (x w) -> p (k r) x w", w=PATCH)).then_inc(W.gb_odd, 1)
            for j in range(NSRC):
                act.wait_ge(W.gbT, j + 1)
                copy(gbT[:, j * NY * 2 * NY:(j + 1) * NY * 2 * NY], gbanks[j][:, 0:NY * 2 * NY]).then_inc(W.gbT_out, 1)
            act.wait_ge(W.wgate, 16)
            copy(wg_split[:, 0:E], wg[:, :]).then_inc(W.wg_hi_done, 1)

            act.wait_ge(W.gbT, NSRC)
            act.wait_ge(W.gbT_out, NSRC)

            def load_piece(i):
                src, down_piece, _, _ = pieces[i]
                dst = wraw[i % 2].rearrange("p (e t n) -> p e t n", e=2, t=HT) if down_piece else wraw[i % 2]
                act.dma_start(dst, src).then_inc(W.wraw1 if i % 2 else W.wraw0, 16)

            load_piece(0)
            load_piece(1)

            def split_high(i):
                act.wait_ge(W.wraw1 if i % 2 else W.wraw0, (i // 2 + 1) * 16)
                copy(pieces[i][2], wraw[i % 2]).then_inc(W.wsplit_hi, 1)

            def next_load(i):
                act.wait_ge(W.wsplit_hi, i + 1)
                act.wait_ge(W.wsplit_lo, i + 1)
                load_piece(i + 2)

            split_high(0)
            split_high(1)
            act.wait_ge(W.beta_tr, 1)
            for k in range(4):
                w = min(4, NY - 4 * k)
                for g in range(G):
                    last = copy(h_tiles[:, 4 * k:4 * k + w, g, :], quad[k][0:PI, 0:w * D].rearrange("p (x d) -> p x d", d=D))
                last.then_inc(W.bias_done, 1)
            next_load(0)
            for i in range(1, PIECES):
                if i > 1:
                    split_high(i)
                if i + 2 < PIECES:
                    next_load(i)

            def image_y(n, kind):
                act.wait_ge(W.im_y, needed(SUM_PARTS, n))
                wait(act, W.mix_ok, n)
                first = tiles_before(n)
                cols = cols_of(kind)
                copy(yT[:, 0:cols], y_img[:, first * PI:first * PI + cols]).then_inc(W.y_ok, 1)

            def x_high(n, buf, kind):
                act.wait_ge(W.xT_ok, n + 1)
                wait(act, W.up_ok, (n - 1) * UN)
                cols = cols_of(kind)
                copy(x_hi[:, buf * 512:buf * 512 + cols], tr_ps[:, 0:cols]).then_inc(W.xhi_ok, 1)

            def comb_out(n, buf, kind):
                act.wait_ge(W.combT_ok, n + 1)
                wait(act, W.down_ok, (n - 2) * UN + 1)
                wait(act, W.comb_w, (n - 1) * 16)
                cols = cols_of(kind)
                copy(combT[buf][:, 0:cols], mx_ps[0:E, 0:cols]).then_inc(W.combT_sb, 1)

            def keep_h1(n, buf, kind):
                p, w = tiles_of(kind)
                act.wait_ge(W.h1_ok, n + 1)
                wait(act, W.o_ok, n - 1)
                copy(h1[buf][0:p, 0:w * D], h1_new[0:p, 0:w * D]).then_inc(W.kept_ok, 1)

            def down_copy(n, kind):
                act.wait_ge(W.down_ok, (n + 1) * UN)
                wait(act, W.outT_ok, n)
                cols = cols_of(kind)
                copy(down_sb[:, 0:cols], down_ps[:, 0:cols]).then_inc(W.down_out, 1)

            def silu(c, u, kind):
                q = c * UN + u
                e, t = divmod(u, HT)
                cols = cols_of(kind)
                act.wait_ge(W.gate_ok, q + 1)
                wait(act, W.silc_ok, q - 3)
                nc.scalar.activation(sil[u % 4][:, 0:cols], gate_ps[u % 2][:, 0:cols], ACT.Silu,
                                     bias=bguT[:, 4 * e + t:4 * e + t + 1]).then_inc(W.sil_ok, 1)

            def hidden_high(c, u, kind):
                q = c * UN + u
                cols = cols_of(kind)
                act.wait_ge(W.h_ok, q + 1)
                wait(act, W.down_ok, q - RING + 1)
                r = u % RING
                copy(h_hi[:, r * 512:r * 512 + cols], h_f[u % 4][:, 0:cols]).then_inc(W.hhi_ok, 1)

            image_y(0, "short")
            x_high(0, 0, "short")
            keep_h1(0, 0, "short")
            image_y(1, "img")
            act.wait_ge(W.im_tr, len(STEPS) * NSRC)
            comb_out(0, 0, "short")
            act.wait_ge(W.im_conv, len(STEPS))

            def chunk(c, buf, kind, before, after, after2, load):
                for u in range(UN):
                    silu(c, u, kind)
                    if u == ACT_AT["down_copy"] and before:
                        down_copy(c - 1, before)
                    if u >= SPLIT:
                        hidden_high(c, u - SPLIT, kind)
                    elif before:
                        hidden_high(c - 1, UN + u - SPLIT, before)
                    if u == ACT_AT["x_high"] and after:
                        x_high(c + 1, 1 - buf, after)
                    if u == ACT_AT["keep_h1"] and after:
                        keep_h1(c + 1, 1 - buf, after)
                    if u == ACT_AT["comb_out"] and after:
                        comb_out(c + 1, 1 - buf, after)
                    if u == ACT_AT["image_y"] and after2 == "img":
                        image_y(c + 2, after2)

            run(chunk, act)
            for u in range(UN - SPLIT, UN):
                hidden_high(CHUNKS - 1, u, "txt")
            down_copy(CHUNKS - 1, "txt")

        @block.gpsimd
        def _(pool):
            tt = nc.gpsimd.tensor_tensor
            nc.gpsimd.memset(euler[:, :], 2.718281828459045).then_inc(W.setup, 1)
            nc.gpsimd.memset(nhalf[:, :], -0.5).then_inc(W.setup, 1)
            pool.wait_ge(W.setup, 2)
            pool.wait_ge(W.dec1, 1)
            tt(dec[:, 2:3], euler[:, 0:1], dec[:, 1:2], ALU.pow).then_inc(W.dec2, 1)
            pool.wait_ge(W.powin, 1)
            pool.wait_ge(W.const, 16)
            tt(pows, dec_b, cst[:, C_EXP:C_W], ALU.pow).then_inc(W.pow_done, 1)

            pool.wait_ge(W.wg_hi_done, 1)
            tt(wg_split[:, E:2 * E], wg[:, :], wg_split[:, 0:E].bitcast(F32), ALU.subtract).then_inc(W.wg_lo_done, 1)

            def weight_low(i):
                pool.wait_ge(W.wsplit_hi, i + 1)
                tt(pieces[i][3], wraw[i % 2], pieces[i][2].bitcast(F32), ALU.subtract).then_inc(W.wsplit_lo, 1)

            def rstd(out_, var, w, ready, done, count, p):
                pool.wait_ge(ready, count)
                tt(out_[0:p, 0:w], var[0:p, 0:w], nhalf[0:p, 0:w], ALU.pow).then_inc(done, 1)

            def decayed_image_sums(i):
                g, nx0, w = SUM_PARTS[i]
                nx1 = nx0 + w
                yv = y_img.rearrange("p (g x y b) -> p g x y b", x=NY, g=G, b=GB)[:, g, nx0:nx1]
                tt(yv, cum_i.rearrange("p (b y x) -> p x y b", b=GB, y=NY)[:, nx0:nx1],
                   pow_t[:, REV:REV + T_IMG].rearrange("p (o y x) -> p x y o", o=1, y=NY)[:, nx0:nx1]
                   .to_broadcast([P, w, NY, GB]), ALU.mult).then_inc(W.im_y, 1)

            def norm2(n, kind):
                p, w = tiles_of(kind)
                wait(pool, W.x2_ok, n)
                rstd(rs2, ve2, w, W.ve2_ok, W.rs2_ok, n + 1, p)

            def gate_exp(n, kind):
                p, w = tiles_of(kind)
                pool.wait_ge(W.gap_ok, n + 1)
                wait(pool, W.w1_ok, n)
                tt(ex[0:p, 0:w], euler[0:p, 0:w], gap[0:p, 0:w], ALU.pow).then_inc(W.ex_ok, 1)

            rstd(ims[:, 5:6], ims[:, 4:5], 1, W.im_eps, W.im_rstd, 1, PI)
            early = 8
            for i in range(early):
                weight_low(i)
            for s in range(len(STEPS)):
                g, nx0, w = STEPS[s]
                if s == KG - 2:
                    rstd(ims[:, 5:6], ims[:, 4:5], 1, W.im_eps, W.im_rstd, 2, PI)
                wait(pool, W.im_z, s)
                rstd(rs1, ve1, w, W.im_ve, W.im_rs, s + 1, PI)
                if s < PIECES - early:
                    weight_low(early + s)
                if s == KG + 2:
                    decayed_image_sums(2)
                pool.wait_ge(W.im_z, s + 1)
                for i in range(w):
                    o = h_tiles[:, nx0 + i, g, :]
                    last = tt(o, o, mixb[0:PI, :], ALU.add)
                last.then_inc(W.im_hI, 1)
                if s == KG:
                    pool.wait_ge(W.im_cum, 1)
                    pool.wait_ge(W.im_pad, G)
                    decayed_image_sums(0)
                if s == KG + 1:
                    decayed_image_sums(1)
                    norm2(0, "short")
            gate_exp(0, "short")
            pool.wait_ge(W.im_cum, 2)
            decayed_image_sums(3)
            decayed_image_sums(4)

            def norm1(n):
                wait(pool, W.z_ok, n - IMG_CHUNKS)
                rstd(rs1, ve1, W4, W.ve1_ok, W.rs1_ok, n - IMG_CHUNKS + 1, P)

            def text_bias(n):
                pool.wait_ge(W.xt, (n - IMG_CHUNKS + 1) * 16)
                pool.wait_ge(W.h1_ok, n)
                tt(h_bias.rearrange("p (j d) -> p j d", j=W4), xt.rearrange("p (j d) -> p j d", j=W4),
                   mixb[:, :].rearrange("p (o d) -> p o d", o=1).to_broadcast([P, W4, D]), ALU.add).then_inc(W.hb_ok, 1)

            def text_y(n):
                pool.wait_ge(W.cum_ok, n - IMG_CHUNKS + 1)
                pool.wait_ge(W.mix_ok, n)
                tt(yT, cum, pow_t[:, REV + T_IMG:REV + T], ALU.mult).then_inc(W.y_ok, 1)

            def weigh(c, u, kind):
                q = c * UN + u
                e, t = divmod(u, HT)
                cols = cols_of(kind)
                if t == 0:
                    pool.wait_ge(combb[e], (c + 1) * 16)
                pool.wait_ge(W.sil_ok, q + 1)
                wait(pool, W.h_ok, q - 3)
                tt(silc[u % 4][:, 0:cols], sil[u % 4][:, 0:cols], comb_b[:, e * 512:e * 512 + cols],
                   ALU.mult).then_inc(W.silc_ok, 1)

            def chunk(c, buf, kind, before, after, after2, load):
                for u in range(UN):
                    weigh(c, u, kind)
                    if u == POOL_AT["norm2"] and after:
                        norm2(c + 1, after)
                    if u == POOL_AT["gate_exp"] and after:
                        gate_exp(c + 1, after)
                    if after2 == "txt":
                        if u == POOL_AT["norm1"]:
                            norm1(c + 2)
                        if u == POOL_AT["text_bias"]:
                            text_bias(c + 2)
                        if u == POOL_AT["text_y"]:
                            text_y(c + 2)

            run(chunk, pool)

        @block.vector
        def _(dve):
            V = nc.vector
            dve.wait_ge(W.ldec, 16)
            V.tensor_scalar(dec[:, 1:2], dec[:, 0:1], -1.0, None, ALU.mult).then_inc(W.dec1, 1)
            V.memset(one[:, :], 1.0).then_inc(W.small, 1)
            V.memset(zpad[:, :], 0.0).then_inc(W.small, 1)
            zeros = 4 * 2 * PATCH * HP
            V.memset(recs[:, 144:150], 0.0).then_inc(W.small, 1)
            dve.wait_ge(W.small, 3)
            V.memset(recs[:, 144:145], zeros / 2).then_inc(W.small, 1)
            V.memset(recs[:, 147:148], zeros / 2).then_inc(W.small, 1)
            dve.wait_ge(W.dec2, 1)
            V.tensor_scalar(dec[:, 3:4], dec[:, 2:3], 1.0, None, ALU.add).then_inc(W.dec3, 1)
            dve.wait_ge(W.dec3, 1)
            V.reciprocal(dec[:, 0:1], dec[:, 3:4]).then_inc(W.dec3, 1)
            dve.wait_ge(W.dec3, 2)
            V.tensor_copy(dec_b, dec[:, 0:1].to_broadcast([P, 2 * (NA + NB)])).then_inc(W.powin, 1)
            dve.wait_ge(W.const, 16)
            V.memset(xraw5[96:PI, 1, :, HP:PATCH, :], 0.0).then_inc(W.small, 1)
            V.memset(xraw5[0:GB, 2, :, 0:HP, :], 0.0).then_inc(W.small, 1)
            dve.wait_ge(W.gb, 32)
            for j in range(0, NSRC, 2):
                V.tensor_copy(patch5[0:2 * NY, j, :, :, :],
                              gb4[0:2 * NY, 2 * j:2 * j + 2, :, :].rearrange("p k r (x w) -> p (k r) x w", w=PATCH)
                              ).then_inc(W.gb_even, 1)
            dve.wait_ge(W.small, 7)

            def image_stats(g, t):
                if t < 3:
                    dve.wait_ge([W.gx0, W.gx1, W.gx2][t], 16 * [2, 4, 4][t] * (g + 1))
                    k = 4 * t
                    for c in range(2):
                        for r in range(0, PATCH, HP):
                            last = V.bn_stats(recs[0:PI, 6 * k:6 * k + 6],
                                              xraw5[0:PI, t, c, r:r + HP, 0:S] if t == 0 else xraw5[0:PI, t, c, r:r + HP, HP:S - HP])
                            k += 1
                else:
                    k = 12
                    for q in (1, 2):
                        for c0 in (0, S - HP):
                            last = V.bn_stats(recs[0:PI, 6 * k:6 * k + 6],
                                              xraw5[0:PI, q, :, :, c0:c0 + HP].rearrange("p c r w -> p (c r) w"))
                            k += 1
                last.then_inc(W.im_stat, 1)

            def image_moments(g):
                dve.wait_ge(W.im_stat, 5 * g + 4)
                V.tensor_copy(recs[0:PI, 96:144], recs[0:PI, 24:72]).then_inc(W.im_stat, 1)
                dve.wait_ge(W.im_stat, 5 * g + 5)
                V.bn_aggr(mvi[0:PI, :], recs[0:PI, :]).then_inc(W.im_aggr, 1)
                dve.wait_ge(W.im_aggr, g + 1)
                dve.wait_ge(W.im_mean, g + 1)
                V.tensor_copy(ims[0:PI, 0:1], avg_ps[0:PI, 0:1]).then_inc(W.im_dev, 1)
                dve.wait_ge(W.im_dev, 2 * g + 1)
                V.tensor_tensor(ims[0:PI, 1:2], mvi[0:PI, 0:1], ims[0:PI, 0:1], ALU.subtract).then_inc(W.im_dev, 1)
                dve.wait_ge(W.im_dev, 2 * g + 2)
                V.scalar_tensor_tensor(ims[0:PI, 2:3], ims[0:PI, 1:2], ims[0:PI, 1:2], mvi[0:PI, 1:2],
                                       ALU.mult, ALU.add).then_inc(W.im_sq, 1)
                dve.wait_ge(W.im_var, g + 1)
                V.tensor_scalar(ims[0:PI, 4:5], avg_ps[0:PI, 1:2], 1e-7, None, ALU.add).then_inc(W.im_eps, 1)

            def image_norm(g):
                dve.wait_ge(W.im_rstd, g + 1)
                if g == 0:
                    dve.wait_ge(W.gbT, NSRC)
                else:
                    dve.wait_ge(W.im_tr, KG * NSRC)
                sc = (ims[0:PI, 0:1], ims[0:PI, 5:6], ALU.subtract, ALU.mult)
                raw = [xraw5[0:PI, t, :, :, :].rearrange("p c r w -> p (c r) w") for t in range(3)]

                grid = [v.rearrange("p q (x w) -> p q x w", w=PATCH) for v in raw]
                V.tensor_scalar(patch5[0:PI, 0], grid[0], *sc)
                zero = zpad[0:PI, 0:64].rearrange("p (r o w) -> p r o w", o=1, w=HP)
                for j in range(1, NSRC):
                    v, dst = grid[SRC_TILE[j]], patch5[0:PI, j]
                    if RAW_COL[j] == 0:
                        V.tensor_scalar(dst[:, :, :, HP:PATCH], v[:, :, :, 0:HP], *sc)
                        V.tensor_scalar(dst[:, :, 1:NY, 0:HP], v[:, :, 0:NY - 1, HP:PATCH], *sc)
                        last = V.tensor_scalar(dst[:, :, 0:1, 0:HP], zero, *sc)
                    else:
                        V.tensor_scalar(dst[:, :, :, 0:HP], v[:, :, :, HP:PATCH], *sc)
                        V.tensor_scalar(dst[:, :, 0:NY - 1, HP:PATCH], v[:, :, 1:NY, 0:HP], *sc)
                        last = V.tensor_scalar(dst[:, :, NY - 1:NY, HP:PATCH], zero, *sc)
                last.then_inc(W.im_pad, 1)

            def image_gamma(s):
                g, nx0, w = STEPS[s]
                wait(dve, W.im_conv, s - 1)
                for j in range(NSRC):
                    dve.wait_ge(W.im_tr, s * NSRC + j + 1)
                    V.tensor_tensor(xgT[s % 2][:, j * W4 * PI:(j * W4 + w) * PI].rearrange("p (x y b) -> p x y b", x=w, b=GB),
                                    quad[(s * NSRC + j) % 4][:, 0:w * PI].rearrange("p (x y b) -> p x y b", x=w, b=GB),
                                    gbT4[:, j, nx0:nx0 + w, 0:NY].unsqueeze(3).to_broadcast([P, w, NY, GB]),
                                    ALU.mult).then_inc(W.im_xg, 1)

            def image_tokens(s):
                g, nx0, w = STEPS[s]
                dve.wait_ge(W.im_conv, s + 1)
                hv = h_tiles[:, nx0:nx0 + w, g, :]
                V.tensor_tensor(hv, conv_ps[s % 2][0:PI, 0:w * D].rearrange("p (x d) -> p x d", d=D),
                                hv, ALU.add).then_inc(W.im_h, 1)
                dve.wait_ge(W.im_h, s + 1)
                for i in range(w):
                    last = V.bn_stats(rec1[0:PI, 6 * i:6 * i + 6], hv[:, i, :])
                last.then_inc(W.im_rec, 1)
                dve.wait_ge(W.im_rec, s + 1)
                for i in range(w):
                    last = V.bn_aggr(mv1[0:PI, 2 * i:2 * i + 2], rec1[0:PI, 6 * i:6 * i + 6])
                last.then_inc(W.im_mv, 1)
                dve.wait_ge(W.im_mv, s + 1)
                wait(dve, W.im_rs, s)
                V.tensor_scalar(ve1[0:PI, 0:w], mv1[0:PI, 1:2 * w:2], 1e-5, None, ALU.add).then_inc(W.im_ve, 1)

            def image_tokens_norm(s):
                g, nx0, w = STEPS[s]
                hv = h_tiles[:, nx0:nx0 + w, g, :]
                dve.wait_ge(W.im_rs, s + 1)
                wait(dve, W.im_zT, s)
                for i in range(w):
                    last = V.tensor_scalar(z_i[0:PI, i * D:(i + 1) * D], hv[:, i, :], mv1[0:PI, 2 * i:2 * i + 1],
                                           rs1[0:PI, i:i + 1], ALU.subtract, ALU.mult)
                last.then_inc(W.im_z, 1)

            def image_decay(s):
                g, nx0, w = STEPS[s]
                dve.wait_ge(W.im_zT, s + 1)
                if s % KG == 0:
                    wait(dve, W.im_cum, g)
                V.tensor_tensor(zs_i.rearrange("p (b y x) -> p x y b", b=GB, y=NY)[:, nx0:nx0 + w],
                                tr_ps[:, 0:w * PI].rearrange("p (x y b) -> p x y b", x=w, b=GB),
                                pow_s[:, 0:T_IMG].rearrange("p (y x o) -> p x y o", o=1, y=NY)[:, nx0:nx0 + w]
                                .to_broadcast([P, w, NY, GB]), ALU.mult).then_inc(W.im_zs, 1)

            def image_sums(g):
                dve.wait_ge(W.im_zs, (g + 1) * KG)
                wait(dve, W.im_y, 3 * g)
                for b in range(GB):
                    last = V.tensor_tensor_scan(cum_i[:, b * T_IMG:(b + 1) * T_IMG], one[:, :].to_broadcast([P, T_IMG]),
                                                zs_i[:, b * T_IMG:(b + 1) * T_IMG], 0.0, ALU.mult, ALU.add)
                last.then_inc(W.im_cum, 1)
                dve.wait_ge(W.im_cum, g + 1)
                V.tensor_copy(carry[:, g * GB:(g + 1) * GB], cum_i[:, T_IMG - 1:GB * T_IMG:T_IMG]).then_inc(W.im_carry, 1)

            def mixed(n, kind):
                p, w = tiles_of(kind)
                dve.wait_ge(W.mix_ok, n + 1)
                if kind == "txt":
                    dve.wait_ge(W.hb_ok, n - IMG_CHUNKS + 1)
                    skip = h_bias
                else:
                    dve.wait_ge(W.im_hI, needed(STEPS, n))
                    first = tiles_before(n)
                    skip = h_img[0:p, first * D:(first + w) * D]
                wait(dve, W.kept_ok, n)
                wait(dve, W.x2_ok, n)
                V.tensor_tensor(h1_new[0:p, 0:w * D], mx_ps[0:p, 0:w * D], skip, ALU.add).then_inc(W.h1_ok, 1)
                dve.wait_ge(W.h1_ok, n + 1)
                wait(dve, W.mv2_ok, n)
                for i in range(w):
                    last = V.bn_stats(rec2[0:p, 6 * i:6 * i + 6], h1_new[0:p, i * D:(i + 1) * D])
                last.then_inc(W.rec2_ok, 1)
                dve.wait_ge(W.rec2_ok, n + 1)
                wait(dve, W.x2_ok, n)
                wait(dve, W.ve2_ok, n)
                dve.nop(nofuse=True)
                for i in range(w):
                    last = V.bn_aggr(mv2[0:p, 2 * i:2 * i + 2], rec2[0:p, 6 * i:6 * i + 6])
                last.then_inc(W.mv2_ok, 1)
                dve.wait_ge(W.mv2_ok, n + 1)
                wait(dve, W.rs2_ok, n)
                V.tensor_scalar(ve2[0:p, 0:w], mv2[0:p, 1:2 * w:2], 1e-5, None, ALU.add).then_inc(W.ve2_ok, 1)

            def norm_apply(n, kind):
                p, w = tiles_of(kind)
                dve.wait_ge(W.rs2_ok, n + 1)
                wait(dve, W.xT_ok, n)
                for i in range(w):
                    last = V.tensor_scalar(x2[0:p, i * D:(i + 1) * D], h1_new[0:p, i * D:(i + 1) * D],
                                           mv2[0:p, 2 * i:2 * i + 1], rs2[0:p, i:i + 1], ALU.subtract, ALU.mult)
                last.then_inc(W.x2_ok, 1)

            def x_low(n, buf, kind):
                cols = cols_of(kind)
                dve.wait_ge(W.xhi_ok, n + 1)
                V.tensor_tensor(x_lo[:, buf * 512:buf * 512 + cols], tr_ps[:, 0:cols],
                                x_hi[:, buf * 512:buf * 512 + cols].bitcast(F32), ALU.subtract).then_inc(W.xlo_ok, 1)

            def top_two(n, kind):
                p, w = tiles_of(kind)
                dve.wait_ge(W.lg_ok, n + 1)
                wait(dve, W.idx_ok, n)
                wait(dve, W.gap_ok, n)
                V.tensor_reduce(lg[0:p, 0:w * E], tr_ps[0:p, 0:w * 2 * E].rearrange("p (i k e) -> p i e k", k=2, e=E),
                                mybir.AxisListType.X, ALU.add).then_inc(W.lsum_ok, 1)
                dve.wait_ge(W.lsum_ok, n + 1)
                dve.nop(nofuse=True)
                for i in range(w):
                    last = V.max(top8[0:p, i * E:(i + 1) * E], lg[0:p, i * E:(i + 1) * E])
                last.then_inc(W.top_ok, 1)
                dve.wait_ge(W.top_ok, n + 1)
                wait(dve, W.hit_ok, n)
                dve.nop(nofuse=True)
                for i in range(w):
                    last = V.max_index(idx8[0:p, i * E:(i + 1) * E], top8[0:p, i * E:(i + 1) * E],
                                       lg[0:p, i * E:(i + 1) * E])
                last.then_inc(W.idx_ok, 1)
                wait(dve, W.ex_ok, n)
                V.tensor_tensor(gap[0:p, 0:w], top8[0:p, 1:w * E:E], top8[0:p, 0:w * E:E], ALU.subtract).then_inc(W.gap_ok, 1)

            def routing(n, kind):
                p, w = tiles_of(kind)
                dve.wait_ge(W.idx_ok, n + 1)
                wait(dve, W.hitw_ok, n)
                top2 = idx8[0:p, 0:w * E].rearrange("p (i e) -> p i e", e=E)[:, :, 0:2]
                V.tensor_tensor(hit[0:p, 0:w * 2 * E].rearrange("p (i k e) -> p i k e", k=2, e=E),
                                iota[0:p].unsqueeze(1).unsqueeze(1).to_broadcast([p, w, 2, E]),
                                top2.unsqueeze(3).to_broadcast([p, w, 2, E]), ALU.is_equal).then_inc(W.hit_ok, 1)
                dve.wait_ge(W.ex_ok, n + 1)
                wait(dve, W.w0_ok, n)
                V.tensor_scalar(ex1[0:p, 0:w], ex[0:p, 0:w], 1.0, None, ALU.add).then_inc(W.ex1_ok, 1)
                dve.wait_ge(W.ex1_ok, n + 1)
                V.reciprocal(w2[0:p, 0:2 * w:2], ex1[0:p, 0:w]).then_inc(W.w0_ok, 1)
                dve.wait_ge(W.w0_ok, n + 1)
                V.tensor_tensor(w2[0:p, 1:2 * w:2], ex[0:p, 0:w], w2[0:p, 0:2 * w:2], ALU.mult).then_inc(W.w1_ok, 1)
                dve.wait_ge(W.w1_ok, n + 1)
                dve.wait_ge(W.hit_ok, n + 1)
                wait(dve, W.comb_ok, n)
                V.tensor_tensor(hitw[0:p, 0:w * 2 * E].rearrange("p (i e) -> p i e", e=E),
                                hit[0:p, 0:w * 2 * E].rearrange("p (i e) -> p i e", e=E),
                                w2[0:p, 0:2 * w].unsqueeze(2).to_broadcast([p, 2 * w, E]), ALU.mult).then_inc(W.hitw_ok, 1)
                dve.wait_ge(W.hitw_ok, n + 1)
                wait(dve, W.combT_ok, n)
                hw = hitw[0:p, 0:w * 2 * E].rearrange("p (i k e) -> p i k e", k=2, e=E)
                V.tensor_tensor(comb[0:p, 0:w * E].rearrange("p (i e) -> p i e", e=E), hw[:, :, 0, :], hw[:, :, 1, :],
                                ALU.add).then_inc(W.comb_ok, 1)

            for t in range(4):
                image_stats(0, t)
            image_moments(0)
            dve.wait_ge(W.beta_mm, 1)
            dve.wait_ge(W.vecs, 32)
            V.tensor_scalar(bias_e.rearrange("p (q b) -> p q b", b=GB), beta_ps[:, 0:T_IMG].unsqueeze(2).to_broadcast([P, T_IMG, GB]),
                            tokb_col[:, 0:1], None, ALU.add).then_inc(W.beta_out, 1)
            image_norm(0)
            dve.wait_ge(W.beta_tr, 1)
            image_gamma(0)
            for s in range(len(STEPS)):
                if s == KG - 1:
                    image_norm(1)
                if s + 1 < len(STEPS):
                    image_gamma(s + 1)
                if s == 0:
                    dve.wait_ge(W.pow_done, 1)
                    for dst, o in ((pow_s, 0), (pow_t, NA + NB)):
                        V.tensor_tensor(dst[:, :].rearrange("p (a b) -> p a b", a=NA),
                                        pows[:, o:o + NA].unsqueeze(2).to_broadcast([P, NA, NB]),
                                        pows[:, o + NA:o + NA + NB].unsqueeze(1).to_broadcast([P, NA, NB]),
                                        ALU.mult).then_inc(W.powers, 1)
                    dve.wait_ge(W.bias_done, 4)
                    dve.wait_ge(W.powers, 2)
                if s == 1:
                    image_stats(1, 0)
                if s == KG - 2:
                    for t in range(1, 4):
                        image_stats(1, t)
                    image_moments(1)
                if s > 0:
                    image_tokens(s - 1)
                if s == LAST:
                    norm_apply(0, "short")
                if s > 1:
                    image_decay(s - 2)
                if s > 0:
                    image_tokens_norm(s - 1)
                if s == LAST - 1:
                    dve.wait_ge(W.im_pad, G)
                    mixed(0, "short")
                if s == KG + 1:
                    image_sums(0)
            image_tokens(LAST)
            x_low(0, 0, "short")
            top_two(0, "short")
            image_decay(LAST - 1)
            image_tokens_norm(LAST)
            routing(0, "short")
            image_decay(LAST)
            image_sums(1)
            dve.wait_ge(W.im_carry, G)
            dve.wait_ge(W.wsplit_lo, PIECES)

            def text_stats(n):
                b = n - IMG_CHUNKS
                dve.wait_ge(W.xt, (b + 1) * 16)
                wait(dve, W.mv1_ok, b)
                for i in range(W4):
                    last = V.bn_stats(rec1[:, 6 * i:6 * i + 6], xt[:, i * D:(i + 1) * D])
                last.then_inc(W.rec1_ok, 1)
                dve.wait_ge(W.rec1_ok, b + 1)
                wait(dve, W.z_ok, b)
                wait(dve, W.ve1_ok, b)
                dve.nop(nofuse=True)
                for i in range(W4):
                    last = V.bn_aggr(mv1[:, 2 * i:2 * i + 2], rec1[:, 6 * i:6 * i + 6])
                last.then_inc(W.mv1_ok, 1)
                dve.wait_ge(W.mv1_ok, b + 1)
                wait(dve, W.rs1_ok, b)
                V.tensor_scalar(ve1[:, :], mv1[:, 1:2 * W4:2], 1e-5, None, ALU.add).then_inc(W.ve1_ok, 1)

            def text_norm(n):
                b = n - IMG_CHUNKS
                dve.wait_ge(W.rs1_ok, b + 1)
                wait(dve, W.zT_ok, b)
                for i in range(W4):
                    last = V.tensor_scalar(z[:, i * D:(i + 1) * D], xt[:, i * D:(i + 1) * D], mv1[:, 2 * i:2 * i + 1],
                                           rs1[:, i:i + 1], ALU.subtract, ALU.mult)
                last.then_inc(W.z_ok, 1)

            def text_sums(n):
                b = n - IMG_CHUNKS
                dve.wait_ge(W.zT_ok, b + 1)
                wait(dve, W.cum_ok, b)
                V.tensor_tensor(zs.rearrange("p (q j) -> p q j", j=W4), tr_ps[:, :].rearrange("p (j q) -> p q j", j=W4),
                                pow_s[:, T_IMG:T].rearrange("p (q j) -> p q j", j=W4), ALU.mult).then_inc(W.zs_ok, 1)
                dve.wait_ge(W.zs_ok, b + 1)
                dve.wait_ge(W.y_ok, n)
                V.tensor_tensor_scan(cum, one[:, :].to_broadcast([P, T_TXT]), zs, carry[:, bass.ds(b, 1)],
                                     ALU.mult, ALU.add).then_inc(W.cum_ok, 1)

            def hidden(c, u, kind):
                q = c * UN + u
                e, t = divmod(u, HT)
                cols = cols_of(kind)
                dve.wait_ge(W.up_ok, q + 1)
                dve.wait_ge(W.silc_ok, q + 1)
                wait(dve, W.hhi_ok, q - 3)
                wait(dve, W.hlo_ok, q - 3)
                k = 4 * e + HT + t
                V.scalar_tensor_tensor(h_f[u % 4][:, 0:cols], up_ps[UP_BANK[u]][:, 0:cols], bguT[:, k:k + 1],
                                       silc[u % 4][:, 0:cols], ALU.add, ALU.mult).then_inc(W.h_ok, 1)

            def hidden_low(c, u, kind):
                q = c * UN + u
                cols = cols_of(kind)
                dve.wait_ge(W.hhi_ok, q + 1)
                wait(dve, W.down_ok, q - RING + 1)
                r = u % RING
                V.tensor_tensor(h_lo[:, r * 512:r * 512 + cols], h_f[u % 4][:, 0:cols],
                                h_hi[:, r * 512:r * 512 + cols].bitcast(F32), ALU.subtract).then_inc(W.hlo_ok, 1)

            def result(n, buf, kind):
                p, w = tiles_of(kind)
                dve.wait_ge(W.outT_ok, n + 1)
                dve.wait_ge(W.kept_ok, n + 1)
                if kind != "short":
                    dve.wait_ge(W.store, stores_before(n, kind) * 16)
                V.tensor_tensor(o_sb[0:p, 0:w * D], mx_ps[0:p, 0:w * D], h1[buf][0:p, 0:w * D], ALU.add).then_inc(W.o_ok, 1)

            def chunk(c, buf, kind, before, after, after2, load):
                for u in range(UN):
                    hidden(c, u, kind)
                    if u >= SPLIT:
                        hidden_low(c, u - SPLIT, kind)
                    elif before:
                        hidden_low(c - 1, UN + u - SPLIT, before)
                    if after:
                        if u == DVE_AT["mixed"]:
                            mixed(c + 1, after)
                        if u == DVE_AT["norm_apply"]:
                            norm_apply(c + 1, after)
                        if u == DVE_AT["x_low"]:
                            x_low(c + 1, 1 - buf, after)
                        if u == DVE_AT["top_two"]:
                            top_two(c + 1, after)
                        if u == DVE_AT["routing"]:
                            routing(c + 1, after)
                    if u == DVE_AT["result"] and before:
                        result(c - 1, 1 - buf, before)
                    if after2 == "txt":
                        if u == DVE_AT["text_stats"]:
                            text_stats(c + 2)
                        if u == DVE_AT["text_norm"]:
                            text_norm(c + 2)
                        if u == DVE_AT["text_sums"]:
                            text_sums(c + 2)

            run(chunk, dve)
            for u in range(UN - SPLIT, UN):
                hidden_low(CHUNKS - 1, u, "txt")
            result(CHUNKS - 1, (CHUNKS - 1) % 2, "txt")


_INS = ["x", "txt", "L0_tok_gamma", "L0_tok_beta", "L0_tok_W", "L0_tok_b", "L0_attn_log_decay", "L0_attn_mix_w",
        "L0_attn_mix_b", "L0_ffn_Wg", "L0_ffn_Wgu", "L0_ffn_bgu", "L0_ffn_Wd", "L0_ffn_bd"]


def shape_constants():
    import numpy as np
    c = np.zeros((P, C_W), np.float32)
    c[:, C_ID:C_ID + P] = np.eye(P)
    q = np.arange(PI)
    c[0:PI, C_AVG:C_AVG + PI] = (q[:, None] % GB == q[None, :] % GB) / NY
    c[:, C_IOTA:C_IOTA + E] = np.arange(E)
    c[:, C_EXP:C_W] = np.concatenate([NB * np.arange(NA), np.arange(NB), NB * np.arange(NA)[::-1], np.arange(NB)[::-1]])
    return c


def kernel(**inputs):
    import numpy as _np
    import concourse.bacc as _bacc
    from concourse import mybir as _mybir
    from concourse.bass_utils import run_bass_kernel_spmd as _run

    nc = _bacc.Bacc("TRN2", target_bir_lowering=False, num_devices=1)
    arrays, args = {}, []
    for name in _INS:
        a = _np.ascontiguousarray(inputs[name])
        if name == "L0_tok_W":
            a = a.reshape(D, -1)
        arrays[f"in_{name}_dram"] = a
        args.append(nc.dram_tensor(f"in_{name}_dram", a.shape, _mybir.dt.from_np(a.dtype), kind="ExternalInput").ap())
    c = shape_constants()
    arrays["in_const_dram"] = c
    args.append(nc.dram_tensor("in_const_dram", c.shape, _mybir.dt.from_np(c.dtype), kind="ExternalInput").ap())
    args.append(nc.dram_tensor("comb_dram", (2, E, 512), F32, kind="Internal").ap())
    args.append(nc.dram_tensor("out_0_dram", (B, T, D), F32, kind="ExternalOutput").ap())
    program(nc, *args)
    r = _run(nc, [arrays], core_ids=[0])
    return r.results[0]["out_0_dram"]
```

```python
from contextlib import ExitStack

import concourse.bass as bass
from concourse import mybir

F32 = mybir.dt.float32
F32R = mybir.dt.float32r
U32 = mybir.dt.uint32
ALU = mybir.AluOpType
ACT = mybir.ActivationFunctionType

P = 128
D = 128
B = 16
S = 104
PATCH = 8
HP = 4
NY = S // PATCH
GB = 8
G = B // GB
PI = NY * GB
T_IMG = NY * NY
T_TXT = 512
T = T_IMG + T_TXT
ROWS = PATCH * S
NSRC = 5
E = 8
HID = 256
HT = HID // P
W4 = 4
UN = E * HT
RING = 8
IMG_CHUNKS = G * NY // W4
SHORT = G * NY - IMG_CHUNKS * W4
CHUNKS = IMG_CHUNKS + B + 1
LAST_CHUNK = CHUNKS - 1
LAG = 5
SPLIT = 2
NA = 22
NB = 32
REV = NA * NB - T

C_ID, C_AVG, C_IOTA, C_EXP = 0, 128, 128 + PI, 128 + PI + E
C_LOW = C_EXP + 2 * (NA + NB)
C_W = C_LOW + 2

NXG = [(0, 4), (4, 4), (8, 4), (12, 1)]

STEPS = [(g, nx0, w) for g in range(G) for nx0, w in NXG]
KG = len(NXG)
LAST = len(STEPS) - 1
ACT_SOURCES = (3, 4)
EARLY = 8
SUM_PARTS = [(0, 0, W4), (0, W4, W4), (0, 2 * W4, NY - 2 * W4), (1, 0, 3), (1, 3, NY - 3)]

PE_AT = dict(mix=0, x_T=5, out_T=6, logits=8, comb_T=12, z_T=12)
ACT_AT = dict(down_copy=4, x_high=6, keep_h1=8, comb_out=13, image_y=15)
POOL_AT = dict(comb_low=15, norm2=2, gate_exp=10, norm1=6, text_bias=12, text_y=14)
DVE_AT = dict(mixed=0, mixed_stats=1, mixed_var=1, norm_apply=2, x_low=5, result=7, top_value=8, top_index=8,
              routing=9, routing_sum=9, text_stats=1, text_var=4, text_norm=7, text_decay=11, text_sums=12)


UP_BANK = [u % 3 for u in range(UN - 1)] + [1]
UP_AGO = [next(d for d in range(1, UN) if UP_BANK[u - d] == UP_BANK[u]) for u in range(UN)]


def tiles_of(chunk):
    return {"short": (PI, SHORT), "img": (PI, W4), "txt": (P, W4)}[chunk]


def tiles_before(n):
    return min(n, IMG_CHUNKS) * W4


def needed(parts, n):
    last = min(tiles_before(n) + W4, G * NY) - 1
    return 1 + next(i for i, (g, nx0, w) in enumerate(parts) if g * NY + nx0 <= last < g * NY + nx0 + w)


def cols_of(chunk):
    p, w = tiles_of(chunk)
    return p * w


def wait(eng, sem, value):
    if not isinstance(value, int) or value > 0:
        eng.wait_ge(sem, value)


def program(nc, x, txt, gamma, beta, tokW, tokb, log_decay, mix_w, mix_b, Wg, Wgu, bgu, Wd, bd, consts, comb_dram, out):
    ctx = ExitStack()
    with ctx:
        def sb(name, shape, dt=F32):
            return ctx.enter_context(nc.sbuf_tensor(name, shape, dt))

        def bank(name):
            return ctx.enter_context(nc.psum_tensor(name, [P, 512], F32))

        def sem(name):
            return ctx.enter_context(nc.semaphore(name))

        cst = sb("cst", [P, C_W])
        ident = cst[:, C_ID:C_ID + P]
        avg = cst[0:PI, C_AVG:C_AVG + PI]
        iota = cst[:, C_IOTA:C_IOTA + E]
        low_rows = cst[0:3 * E, C_LOW:C_LOW + 1]
        bd_low_rows = cst[0:3 * E, C_LOW + 1:C_LOW + 2]
        wgu_hi = sb("wgu_hi", [P, E * 512], F32R)
        wgu_lo = sb("wgu_lo", [P, E * 512], F32R)
        wd_hi = sb("wd_hi", [P, E * HT * D], F32R)
        wd_lo = sb("wd_lo", [P, E * HT * D], F32R)
        wg = sb("wg", [P, E])
        wg_split = sb("wg_split", [P, 2 * E], F32R)
        bguT = sb("bguT", [P, 4 * E])
        bd3 = sb("bd3", [3 * E, D], F32R)
        comb3 = sb("comb3", [3 * E, 512], F32R)
        wtokT = sb("wtokT", [P, NSRC * D])
        mixT = sb("mixT", [P, D])
        mixb = sb("mixb", [P, D])
        tokb_col = sb("tokb_col", [P, 1])
        pow_s = sb("pow_s", [P, NA * NB])
        pow_t = sb("pow_t", [P, NA * NB])
        one = sb("one", [P, 1])
        nhalf = sb("nhalf", [P, W4])
        euler = sb("euler", [P, W4])
        h_img = sb("h_img", [P, G * NY * D])
        wtok = h_img[:, 0:NSRC * D]
        mixw = h_img[:, NSRC * D:(NSRC + 1) * D]
        bgu_rows = h_img[0:4 * E, (NSRC + 1) * D:(NSRC + 2) * D]
        carry = sb("carry", [P, B])
        x_hi = sb("x_hi", [P, 2 * 512], F32R)
        x_lo = sb("x_lo", [P, 2 * 512], F32R)
        h_hi = sb("h_hi", [P, RING * 512], F32R)
        h_lo = sb("h_lo", [P, RING * 512], F32R)
        space = sb("space", [P, 16 * ROWS + 2 * NSRC * W4 * PI + 2 * GB * T_IMG + 512])
        top = [0]

        def part(n):
            top[0] += n
            assert top[0] <= space.shape[1], top[0]
            return space[:, top[0] - n:top[0]]

        xraw = part(6 * ROWS)
        patches = part(2 * NSRC * ROWS)
        gbraw = [part(8 * ROWS), h_img[:, 2 * ROWS:4 * ROWS]]
        top[0] -= 8 * ROWS
        xgT = [part(NSRC * W4 * PI) for _ in range(2)]
        bias_e = xgT[1][:, 0:NY * PI]
        zs_i = part(GB * T_IMG)
        cum_i = part(GB * T_IMG)
        wraw = [cum_i[:, i * 512:(i + 1) * 512] for i in range(2)]
        bd_raw = cum_i[0:3 * E, 9 * D:10 * D]
        gbT = sb("gbT", [P, NSRC * NY * 2 * NY])
        z_i = sb("z_i", [P, W4 * D])
        dec_b = z_i[:, 0:2 * (NA + NB)]
        pows = z_i[:, 2 * (NA + NB):4 * (NA + NB)]
        dec = z_i[:, 4 * (NA + NB):4 * (NA + NB) + 4]
        top[0] = 0
        y_img = part(G * NY * PI)
        yT = part(512)
        x2 = part(512)
        h1_new = part(512)
        h1 = [part(512)]
        lg = part(W4 * E)
        hit = part(W4 * 2 * E)
        hitw = part(W4 * 2 * E)
        assert top[0] <= 6 * ROWS
        top[0] = 6 * ROWS
        comb_b = part(E * 512)
        combT = [part(512)[0:3 * E] for _ in range(2)]
        h_f = [part(512) for _ in range(4)]
        down_sb = part(512)
        h1.append(part(512))
        comb = part(W4 * 3 * E)
        assert top[0] <= 16 * ROWS
        top[0] = 16 * ROWS
        sil = [part(512) for _ in range(4)]
        silc = [part(512) for _ in range(4)]
        top[0] = 16 * ROWS + 2 * NSRC * W4 * PI
        xt = part(512)
        h_bias = part(512)
        z = part(512)
        zs = part(512)
        cum = part(512)
        top[0] = 16 * ROWS + 2 * NSRC * W4 * PI + 2 * GB * T_IMG
        o_sb = part(512)
        recs = sb("recs", [P, 25 * 6])
        rec1 = sb("rec1", [P, W4 * 6])
        rec2 = sb("rec2", [P, W4 * 6])
        mvi = sb("mvi", [P, 2])
        ims = sb("ims", [P, 6])
        mv1 = sb("mv1", [P, W4 * 2])
        mv2 = sb("mv2", [P, W4 * 2])
        ve1 = sb("ve1", [P, W4])
        ve2 = sb("ve2", [P, W4])
        rs1 = sb("rs1", [P, W4])
        nm1 = sb("nm1", [P, W4])
        sh1 = sb("sh1", [P, W4])
        rs2 = sb("rs2", [P, W4])
        zpad = sb("zpad", [P, 128])
        top8 = sb("top8", [P, W4 * E])
        idx8 = sb("idx8", [P, W4 * E], U32)
        gap = sb("gap", [P, W4])
        ex = sb("ex", [P, W4])
        ex1 = sb("ex1", [P, W4])
        w2 = sb("w2", [P, W4 * 2])

        gate_ps = [bank("gate0"), bank("gate1")]
        up_ps = [bank("up0"), bank("up1"), bank("up2")]
        down_ps = bank("down")
        tr_ps = bank("tr")
        mx_ps = bank("mx")
        quad = gate_ps + up_ps
        avg_ps = tr_ps
        beta_ps = down_ps
        beta_banks = [quad[2], quad[3], tr_ps, mx_ps]
        conv_ps = [down_ps, mx_ps]

        N = {}
        for name in ("const ldec vecs wtok wmix bgu wraw0 wraw1 wgate bd gb gx0 gx1 gx2 xt comb_w store "
                     "setup small gb_even gb_odd wT wT_out gbT gbT_out wsplit_hi wsplit_lo wg_hi_done wg_lo_done "
                     "bd3_hi bd3_ok dec1 dec2 dec3 powin pow_done powers "
                     "beta_mm beta_out beta_tr bias_done "
                     "im_stat im_aggr im_mean im_dev im_sq im_var im_eps im_rstd im_shift im_pad im_pad_act im_tr im_xg "
                     "im_conv im_h im_hI "
                     "im_rec im_mv im_ve im_neg im_rs im_sh im_z im_zT im_zs im_cum im_carry im_y "
                     "rec1_ok mv1_ok ve1_ok rs1_ok z_ok zT_ok zs_ok cum_ok y_ok hb_ok mix_ok h1_ok kept_ok "
                     "rec2_ok mv2_ok ve2_ok rs2_ok x2_ok "
                     "xT_ok xhi_ok xlo_ok lg_ok lsum_ok top_ok idx_ok gap_ok ex_ok ex1_ok w0_ok w1_ok hit_ok hitw_ok "
                     "comb_ok combT_ok combT_sb comb3_hi comb3_ok "
                     "gate_ok up_ok sil_ok silc_ok h_ok hhi_ok hlo_ok down_ok down_out outT_ok o_ok").split():
            N[name] = sem("s_" + name)
        combb = [sem(f"s_combb{e}") for e in range(E)]
        W = type("Sems", (), N)

        block = ctx.enter_context(nc.Block())

        xraw5 = xraw.rearrange("p (t c r w) -> p t c r w", t=3, c=2, r=PATCH)
        patch5 = patches.rearrange("p (j x q w) -> p j q x w", j=NSRC, x=NY, w=PATCH)
        h_tiles = h_img[0:PI, :].rearrange("p (g x d) -> p x g d", g=G, d=D)
        gb4 = [v.rearrange("p (k r w) -> p k r w", r=PATCH, w=S) for v in gbraw]
        gb_of = [gb4[j // 4][0:2 * NY, 2 * (j % 4):2 * (j % 4) + 2, :, :].rearrange("p k r (x w) -> p (k r) x w", w=PATCH)
                 for j in range(NSRC)]
        gbT4 = gbT[:, :].rearrange("p (j x q) -> p j x q", j=NSRC, x=NY)
        SRC_TILE = [0, 1, 1, 2, 2]
        RAW_COL = [0, 0, HP, 0, HP]

        def shifted(j):
            v = xraw5[0:PI, SRC_TILE[j], :, :, :].rearrange("p c r (x w) -> p (c r) x w", w=PATCH)
            dst = patch5[0:PI, j]
            zero = zpad[0:PI, 0:64].rearrange("p (r o w) -> p r o w", o=1, w=HP)
            if RAW_COL[j] == 0:
                return ((dst[:, :, :, HP:PATCH], v[:, :, :, 0:HP]), (dst[:, :, 1:NY, 0:HP], v[:, :, 0:NY - 1, HP:PATCH]),
                        (dst[:, :, 0:1, 0:HP], zero))
            return ((dst[:, :, :, 0:HP], v[:, :, :, HP:PATCH]), (dst[:, :, 0:NY - 1, HP:PATCH], v[:, :, 1:NY, 0:HP]),
                    (dst[:, :, NY - 1:NY, HP:PATCH], zero))

        wd_v = Wd.rearrange("e (t q) n -> q e t n", t=HT)
        PIECES = E + E // 2
        pieces = [(Wgu[i], None, wgu_hi[:, 512 * i:512 * i + 512], wgu_lo[:, 512 * i:512 * i + 512]) for i in range(E)]
        pieces += [(wd_v[:, 2 * i:2 * i + 2, :, :], True, wd_hi[:, 512 * i:512 * i + 512],
                    wd_lo[:, 512 * i:512 * i + 512]) for i in range(E // 2)]

        def stores_before(n, kind):
            return n * W4 if kind == "img" else IMG_CHUNKS * W4 + n - IMG_CHUNKS

        def run(body, eng):
            body(0, 0, "img", None, "img", "img", False)
            for c in range(1, 4):
                body(c, c % 2, "img", "img", "img", "img", False)
            body(4, 0, "img", "img", "img", "txt", True)
            body(5, 1, "img", "img", "txt", "txt", True)
            body(6, 0, "txt", "img", "txt", "txt", True)
            with eng.Fori(0, 6) as i:
                body(i * 2 + 7, 1, "txt", "txt", "txt", "txt", True)
                body(i * 2 + 8, 0, "txt", "txt", "txt", "txt", True)
            body(19, 1, "txt", "txt", "txt", "txt", False)
            body(20, 0, "txt", "txt", "txt", "short", False)
            body(21, 1, "txt", "txt", "short", None, False)
            body(22, 0, "short", "txt", None, None, False)

        @block.sync
        def _(sp):
            sp.dma_start(cst[:, :], consts).then_inc(W.const, 16)

            def load_images(g):
                for t in range(3):
                    if g > 0:
                        sp.wait_ge(W.im_pad, g)
                        sp.wait_ge(W.im_pad_act, g)
                    s = [W.gx0, W.gx1, W.gx2][t]
                    for c in range(2):
                        img = x[g * GB:(g + 1) * GB, c, :, :]
                        if t == 0:
                            sp.dma_start(xraw5[0:PI, 0, c, :, :].rearrange("p r w -> p (r w)"),
                                         img.rearrange("b (n r) w -> n b (r w)", r=PATCH)).then_inc(s, 16)
                            continue
                        body = img[:, HP:S - HP, :].rearrange("b (n r) w -> n b (r w)", r=PATCH)
                        if t == 1:
                            sp.dma_start(xraw5[0:PI - GB, 1, c, :, :].rearrange("p r w -> p (r w)"), body).then_inc(s, 16)
                            sp.dma_start(xraw5[PI - GB:PI, 1, c, 0:HP, :], img[:, S - HP:S, :]).then_inc(s, 16)
                        else:
                            sp.dma_start(xraw5[GB:PI, 2, c, :, :].rearrange("p r w -> p (r w)"), body).then_inc(s, 16)
                            sp.dma_start(xraw5[0:GB, 2, c, HP:PATCH, :], img[:, 0:HP, :]).then_inc(s, 16)

            for i, (k0, k1) in enumerate(((0, 8), (8, 10))):
                for v, p0 in ((gamma, 0), (beta, NY)):
                    sp.dma_start(gb4[i][p0:p0 + NY].rearrange("p k r w -> p k (r w)"),
                                 v[k0:k1].rearrange("k (n r) w -> n k (r w)", r=PATCH)).then_inc(W.gb, 16)
            load_images(0)
            for dst, src, s in ((tokb_col[:, :], tokb.rearrange("(p o) -> p o", o=1), W.vecs),
                                (mixb[:, :], mix_b.rearrange("(o n) -> o n", o=1).to_broadcast([P, D]), W.vecs),
                                (wg[:, :], Wg, W.wgate),
                                *((bd_raw[i * E:(i + 1) * E], bd, W.bd) for i in range(3))):
                sp.dma_start(dst, src).then_inc(s, 16)
            load_images(1)

            def load_text(n):
                sp.dma_start(xt.rearrange("p (j d) -> p j d", j=W4),
                             txt[bass.ds(n - IMG_CHUNKS, 1), :, :].rearrange("o (p j) d -> (o p) j d", j=W4)
                             ).then_inc(W.xt, 16)

            def send_comb(n, buf, kind):
                cols = cols_of(kind)
                sp.wait_ge(W.combT_sb, n + 1)
                sp.nop(nofuse=True)
                wait(sp, W.silc_ok, (n - 1) * UN)
                sp.nop(nofuse=True)
                sp.dma_start(comb_dram[buf, :, 0:cols], combT[buf][0:E, 0:cols]).then_inc(W.comb_w, 16)
                sp.wait_ge(W.comb_w, (n + 1) * 16)
                sp.nop(nofuse=True)
                for e in range(E):
                    wait(sp, W.silc_ok, (n - 1) * UN + HT * (e + 1))
                    sp.nop(nofuse=True)
                    sp.dma_start(comb_b[:, e * 512:e * 512 + cols],
                                 comb_dram[buf, e:e + 1, 0:cols].to_broadcast([P, cols])).then_inc(combb[e], 16)

            def store(n, kind):
                sp.wait_ge(W.o_ok, n + 1)
                sp.nop(nofuse=True)
                if kind == "txt":
                    sp.dma_start(out[bass.ds(n - IMG_CHUNKS, 1), T_IMG:T, :].rearrange("o (p j) d -> (o p) j d", j=W4),
                                 o_sb.rearrange("p (j d) -> p j d", j=W4)).then_inc(W.store, 16)
                    return
                for i in range(tiles_of(kind)[1]):
                    g, nx = divmod(tiles_before(n) + i, NY)
                    dst = out[g * GB:(g + 1) * GB, 0:T_IMG, :].rearrange("b (y q) d -> q y b d", q=NY)[nx]
                    sp.dma_start(dst, o_sb[0:PI, i * D:(i + 1) * D]).then_inc(W.store, 16)

            sp.wait_ge(W.im_tr, len(STEPS) * NSRC)
            send_comb(0, 0, "img")
            sp.wait_ge(W.im_cum, G)
            load_text(IMG_CHUNKS)

            def chunk(c, buf, kind, before, after, after2, load):
                if before:
                    store(c - 1, before)
                if after:
                    send_comb(c + 1, 1 - buf, after)
                if load:
                    sp.wait_ge(W.z_ok, c + 3 - IMG_CHUNKS)
                    sp.nop(nofuse=True)
                    sp.wait_ge(W.hb_ok, c + 3 - IMG_CHUNKS)
                    sp.nop(nofuse=True)
                    load_text(c + 3)

            run(chunk, sp)
            store(LAST_CHUNK, "short")
            sp.wait_ge(W.store, (G * NY + B) * 16)

        @block.tensor
        def _(pe):
            def mm(o, l, r, a, z_):
                return nc.tensor.matmul(o, l, r, start=a, stop=z_)

            pe.wait_ge(W.const, 16)
            pe.wait_ge(W.wtok, 16)
            for j in range(NSRC):
                dst = quad[0][:, j * D:(j + 1) * D] if j < 4 else quad[1][:, 0:D]
                nc.tensor.transpose(dst, wtok[:, j * D:(j + 1) * D], ident)
            pe.wait_ge(W.wmix, 16)
            nc.tensor.transpose(quad[1][:, D:2 * D], mixw[:, :], ident)
            pe.wait_ge(W.bgu, 16)
            nc.tensor.transpose(quad[1][:, 2 * D:2 * D + 4 * E], bgu_rows[:, :], ident[0:4 * E, 0:4 * E]).then_inc(W.wT, 1)
            gbanks = [quad[2], quad[3], tr_ps, mx_ps, down_ps]
            for j in range(NSRC):
                pe.wait_ge(W.gb_odd if j % 2 else W.gb_even, j // 2 + 1)
                for nx in range(NY):
                    last = nc.tensor.transpose(gbanks[j][:, nx * 2 * NY:(nx + 1) * 2 * NY],
                                               patches[0:2 * NY, (j * NY + nx) * P:(j * NY + nx + 1) * P],
                                               ident[0:2 * NY, 0:2 * NY])
                last.then_inc(W.gbT, 1)
            pe.wait_ge(W.wT_out, 2)
            pe.wait_ge(W.gbT_out, NSRC)
            for j in range(NSRC):
                last = mm(beta_ps[:, 0:T_IMG], wtokT[:, j * D:(j + 1) * D], gbT4[:, j, :, NY:2 * NY], j == 0, j == NSRC - 1)
            last.then_inc(W.beta_mm, 1)

            def image_mean(g):
                pe.wait_ge(W.im_aggr, g + 1)
                mm(avg_ps[0:PI, 0:1], avg, mvi[0:PI, 0:1], True, True).then_inc(W.im_mean, 1)

            def image_var(g):
                pe.wait_ge(W.im_sq, g + 1)
                mm(avg_ps[0:PI, 1:2], avg, ims[0:PI, 2:3], True, True).then_inc(W.im_var, 1)

            image_mean(0)
            image_var(0)
            pe.wait_ge(W.beta_out, 1)
            pe.wait_ge(W.im_eps, 1)
            for nx in range(NY):
                last = nc.tensor.transpose(beta_banks[nx // 4][0:PI, (nx % 4) * D:(nx % 4 + 1) * D],
                                           bias_e[:, nx * PI:(nx + 1) * PI], ident)
            last.then_inc(W.beta_tr, 1)

            def z_T(n):
                pe.wait_ge(W.z_ok, n - IMG_CHUNKS + 1)
                pe.wait_ge(W.lsum_ok, n)
                for j in range(W4):
                    last = nc.tensor.transpose(tr_ps[:, j * P:(j + 1) * P], z[:, j * D:(j + 1) * D], ident)
                last.then_inc(W.zT_ok, 1)

            def mix(n, kind):
                p, w = tiles_of(kind)
                pe.wait_ge(W.y_ok, n + 1)
                wait(pe, W.comb3_hi, n)
                for j in range(w):
                    lhs = yT[:, j:j + W4 * (P - 1) + 1:W4] if kind == "txt" else yT[:, j * PI:(j + 1) * PI]
                    last = mm(mx_ps[0:p, j * D:(j + 1) * D], lhs, mixT[:, :], True, True)
                last.then_inc(W.mix_ok, 1)

            def x_T(n, kind):
                p, w = tiles_of(kind)
                pe.wait_ge(W.x2_ok, n + 1)
                if kind == "txt":
                    pe.wait_ge(W.zs_ok, n - IMG_CHUNKS + 1)
                else:
                    wait(pe, W.lsum_ok, n)
                    if n < 2:
                        pe.wait_ge(W.im_zs, LAST - 1 if n == 0 else LAST + 1)
                for j in range(w):
                    last = nc.tensor.transpose(tr_ps[:, j * p:(j + 1) * p], x2[0:p, j * D:(j + 1) * D], ident[0:p, 0:p])
                last.then_inc(W.xT_ok, 1)

            def logits(n, buf, kind):
                p, w = tiles_of(kind)
                pe.wait_ge(W.xhi_ok, n + 1)
                pe.wait_ge(W.xlo_ok, n + 1)
                for j in range(w):
                    o = tr_ps[0:p, j * 2 * E:(j + 1) * 2 * E]
                    xs = [v[:, buf * 512 + j * p:buf * 512 + (j + 1) * p] for v in (x_hi, x_lo)]
                    mm(o, xs[0], wg_split[:, :], True, False)
                    last = mm(o, xs[1], wg_split[:, :], False, True)
                last.then_inc(W.lg_ok, 1)

            def comb_T(n, kind):
                p, w = tiles_of(kind)
                pe.wait_ge(W.comb_ok, n + 1)
                wait(pe, W.o_ok, n - 1)
                for j in range(w):
                    last = nc.tensor.transpose(mx_ps[0:3 * E, j * p:(j + 1) * p], comb[0:p, j * 3 * E:(j + 1) * 3 * E], ident[0:p, 0:p])
                last.then_inc(W.combT_ok, 1)

            def gate(c, buf, u, kind):
                if u == 0:
                    pe.wait_ge(W.xhi_ok, c + 1)
                    pe.wait_ge(W.xlo_ok, c + 1)
                wait(pe, W.sil_ok, c * UN + u - 1)
                into(gate_ps[u % 2], 0, buf, u, kind).then_inc(W.gate_ok, 1)

            def up(c, buf, u, kind):
                wait(pe, W.h_ok, c * UN + u - UP_AGO[u] + 1)
                into(up_ps[UP_BANK[u]], HID, buf, u, kind).then_inc(W.up_ok, 1)

            def into(ps, off, buf, u, kind):
                cols = cols_of(kind)
                e, t = divmod(u, HT)
                xs = [v[:, buf * 512:buf * 512 + cols] for v in (x_hi, x_lo)]
                o = ps[:, 0:cols]
                c0 = e * 512 + off + t * P
                mm(o, wgu_hi[:, c0:c0 + P], xs[0], True, False)
                mm(o, wgu_hi[:, c0:c0 + P], xs[1], False, False)
                return mm(o, wgu_lo[:, c0:c0 + P], xs[0], False, True)

            def down(c, buf, u, kind):
                cols = cols_of(kind)
                q = c * UN + u
                r = u % RING
                o = down_ps[:, 0:cols]
                if u == 0:
                    wait(pe, W.down_out, c)
                    pe.wait_ge(W.comb3_ok, c + 1)
                    mm(o, bd3[:, :], comb3[:, 0:cols], True, False)
                pe.wait_ge(W.hhi_ok, q + 1)
                pe.wait_ge(W.hlo_ok, q + 1)
                hs = [v[:, r * 512:r * 512 + cols] for v in (h_hi, h_lo)]
                mm(o, wd_hi[:, u * D:(u + 1) * D], hs[0], False, False)
                mm(o, wd_hi[:, u * D:(u + 1) * D], hs[1], False, False)
                mm(o, wd_lo[:, u * D:(u + 1) * D], hs[0], False, u == UN - 1).then_inc(W.down_ok, 1)

            def out_T(c, kind, h1_done):
                p, w = tiles_of(kind)
                pe.wait_ge(W.down_out, c + 1)
                pe.wait_ge(W.h1_ok, h1_done)
                for j in range(w):
                    last = nc.tensor.transpose(mx_ps[0:p, j * D:(j + 1) * D], down_sb[:, j * p:(j + 1) * p], ident)
                last.then_inc(W.outT_ok, 1)

            def chunk(c, buf, kind, before, after, after2, load):
                for u in range(UN):
                    if u + 1 < UN:
                        gate(c, buf, u + 1, kind)
                    elif after:
                        gate(c + 1, 1 - buf, 0, after)
                    up(c, buf, u, kind)
                    if u >= LAG:
                        down(c, buf, u - LAG, kind)
                    elif before:
                        down(c - 1, 1 - buf, UN + u - LAG, before)
                    if u == PE_AT["mix"] and after:
                        mix(c + 1, after)
                    if u == PE_AT["x_T"] and after:
                        x_T(c + 1, after)
                    if u == PE_AT["out_T"] and before:
                        out_T(c - 1, before, c + 2 if after else c + 1)
                    if u == PE_AT["logits"] and after:
                        logits(c + 1, 1 - buf, after)
                    if u == PE_AT["comb_T"] and after:
                        comb_T(c + 1, after)
                    if u == PE_AT["z_T"] and after2 == "txt":
                        z_T(c + 2)

            def image_transposes(s):
                g, nx0, w = STEPS[s]
                if s % KG == 0:
                    pe.wait_ge(W.im_pad, g + 1)
                    pe.wait_ge(W.im_pad_act, g + 1)
                for j in range(NSRC):
                    n = s * NSRC + j
                    if n == 0:
                        pe.wait_ge(W.wT_out, 4)
                    if n in (2, 3):
                        pe.wait_ge(W.bias_done, n - 1)
                    wait(pe, W.im_xg, n - 4)
                    for i in range(w):
                        c0 = (j * NY + nx0 + i) * P
                        last = nc.tensor.transpose(quad[j][:, i * PI:(i + 1) * PI],
                                                   patches[0:PI, c0:c0 + P], ident[0:PI, 0:PI])
                    last.then_inc(W.im_tr, 1)

            def image_conv(s):
                g, nx0, w = STEPS[s]
                pe.wait_ge(W.im_xg, (s + 1) * NSRC)
                if s == 1:
                    pe.wait_ge(W.bias_done, 4)
                wait(pe, W.im_h, s - 1)
                if s == LAST:
                    pe.wait_ge(W.h1_ok, 1)
                for i in range(w):
                    for j in range(NSRC):
                        last = mm(conv_ps[s % 2][0:PI, i * D:(i + 1) * D],
                                  xgT[s % 2][:, (j * W4 + i) * PI:(j * W4 + i + 1) * PI],
                                  wtokT[:, j * D:(j + 1) * D], j == 0, j == NSRC - 1)
                last.then_inc(W.im_conv, 1)

            def z_transposes(s):
                g, nx0, w = STEPS[s]
                pe.wait_ge(W.im_z, s + 1)
                wait(pe, W.im_zs, s)
                for i in range(w):
                    last = nc.tensor.transpose(tr_ps[:, i * PI:(i + 1) * PI], z_i[0:PI, i * D:(i + 1) * D], ident[0:PI, 0:PI])
                last.then_inc(W.im_zT, 1)

            image_transposes(0)
            for s in range(len(STEPS)):
                if s != KG - 1 and s < LAST:
                    image_transposes(s + 1)
                if s == KG - 2:
                    image_conv(s)
                    image_mean(1)
                    image_var(1)
                    pe.wait_ge(W.im_eps, 2)
                if s == LAST - 1:
                    pe.wait_ge(W.im_h, LAST - 1)
                    mix(0, "img")
                if s > 1:
                    z_transposes(s - 2)
                if s != KG - 2:
                    image_conv(s)
                if s == KG - 1:
                    image_transposes(s + 1)
            x_T(0, "img")
            pe.wait_ge(W.wg_hi_done, 1)
            pe.wait_ge(W.wg_lo_done, 1)
            logits(0, 0, "img")
            pe.wait_ge(W.lsum_ok, 1)
            z_transposes(LAST - 1)
            pe.wait_ge(W.wsplit_hi, PIECES)
            pe.wait_ge(W.wsplit_lo, PIECES)
            gate(0, 0, 0, "img")
            pe.wait_ge(W.im_h, LAST + 1)
            pe.wait_ge(W.bd3_ok, 1)
            comb_T(0, "img")
            z_transposes(LAST)

            run(chunk, pe)
            for u in range(UN - LAG, UN):
                down(LAST_CHUNK, LAST_CHUNK % 2, u, "short")
            out_T(LAST_CHUNK, "short", CHUNKS)

        @block.scalar
        def _(act):
            copy = nc.scalar.copy
            for dst, src, s in ((dec[:, 0:1], log_decay.rearrange("(p o) -> p o", o=1), W.ldec),
                                (wtok.rearrange("p (o n) -> p o n", o=1), tokW.rearrange("m (o k) -> m o k", o=1), W.wtok),
                                (mixw, mix_w, W.wmix),
                                (bgu_rows, bgu.rearrange("e (k q) -> (e k) q", q=P), W.bgu)):
                act.dma_start(dst, src).then_inc(s, 16)
            act.preload_act_table(ACT.Silu)

            act.wait_ge(W.wT, 1)
            copy(wtokT[:, 0:4 * D], quad[0][:, 0:4 * D]).then_inc(W.wT_out, 1)
            copy(wtokT[:, 4 * D:5 * D], quad[1][:, 0:D]).then_inc(W.wT_out, 1)
            copy(mixT[:, :], quad[1][:, D:2 * D]).then_inc(W.wT_out, 1)
            copy(bguT[:, :], quad[1][:, 2 * D:2 * D + 4 * E]).then_inc(W.wT_out, 1)
            gbanks = [quad[2], quad[3], tr_ps, mx_ps, down_ps]
            act.wait_ge(W.gb, 64)
            for j in range(1, NSRC, 2):
                copy(patch5[0:2 * NY, j, :, :, :], gb_of[j]).then_inc(W.gb_odd, 1)
            for j in range(NSRC):
                act.wait_ge(W.gbT, j + 1)
                copy(gbT[:, j * NY * 2 * NY:(j + 1) * NY * 2 * NY], gbanks[j][:, 0:NY * 2 * NY]).then_inc(W.gbT_out, 1)
            act.wait_ge(W.wgate, 16)
            copy(wg_split[:, 0:E], wg[:, :]).then_inc(W.wg_hi_done, 1)
            act.wait_ge(W.bd, 48)
            nc.scalar.mul(bd3[:, :], bd_raw, bd_low_rows).then_inc(W.bd3_hi, 1)

            act.wait_ge(W.gbT, NSRC)
            act.wait_ge(W.gbT_out, NSRC)

            def load_piece(i):
                src, down_piece, _, _ = pieces[i]
                dst = wraw[i % 2].rearrange("p (e t n) -> p e t n", e=2, t=HT) if down_piece else wraw[i % 2]
                act.dma_start(dst, src).then_inc(W.wraw1 if i % 2 else W.wraw0, 16)

            load_piece(0)
            load_piece(1)

            def split_high(i):
                act.wait_ge(W.wraw1 if i % 2 else W.wraw0, (i // 2 + 1) * 16)
                copy(pieces[i][2], wraw[i % 2]).then_inc(W.wsplit_hi, 1)

            def next_load(i):
                act.wait_ge(W.wsplit_hi, i + 1)
                act.wait_ge(W.wsplit_lo, i + 1)
                load_piece(i + 2)

            def image_norm(g):
                act.wait_ge(W.im_shift, g + 1)
                if g == 0:
                    act.wait_ge(W.gbT, NSRC)
                else:
                    act.wait_ge(W.im_tr, KG * NSRC)
                for j in range(ACT_SOURCES[g], NSRC):
                    for dst, v in shifted(j):
                        last = nc.scalar.activation(dst, v, ACT.Identity, bias=ims[0:PI, 3:4], scale=ims[0:PI, 5:6])
                last.then_inc(W.im_pad_act, 1)

            split_high(0)
            split_high(1)
            act.wait_ge(W.beta_mm, 1)
            act.wait_ge(W.vecs, 32)
            nc.scalar.activation(bias_e.rearrange("p (q b) -> p q b", b=GB),
                                 beta_ps[:, 0:T_IMG].unsqueeze(2).to_broadcast([P, T_IMG, GB]),
                                 ACT.Identity, bias=tokb_col[:, 0:1]).then_inc(W.beta_out, 1)
            next_load(0)
            next_load(1)
            image_norm(0)
            act.wait_ge(W.beta_tr, 1)
            for k in range(4):
                w = min(4, NY - 4 * k)
                for g in range(G):
                    last = copy(h_tiles[:, 4 * k:4 * k + w, g, :], beta_banks[k][0:PI, 0:w * D].rearrange("p (x d) -> p x d", d=D))
                last.then_inc(W.bias_done, 1)

            def image_z(s):
                g, nx0, w = STEPS[s]
                act.wait_ge(W.im_sh, s + 1)
                wait(act, W.im_zT, s)
                for i in range(w):
                    last = nc.scalar.activation(z_i[0:PI, i * D:(i + 1) * D], h_tiles[:, nx0 + i, g, :], ACT.Identity,
                                                bias=sh1[0:PI, i:i + 1], scale=rs1[0:PI, i:i + 1])
                last.then_inc(W.im_z, 1)

            for i in range(2, PIECES):
                if i >= EARLY and (i - EARLY) % 2 == 0:
                    image_z((i - EARLY) // 2)
                split_high(i)
                if i + 2 < PIECES:
                    next_load(i)
            image_norm(1)
            for s in range(2, LAST - 3):
                image_z(s)

            def image_y(n, kind):
                act.wait_ge(W.im_y, needed(SUM_PARTS, n))
                wait(act, W.mix_ok, n)
                first = tiles_before(n)
                cols = cols_of(kind)
                copy(yT[:, 0:cols], y_img[:, first * PI:first * PI + cols]).then_inc(W.y_ok, 1)

            def x_high(n, buf, kind):
                act.wait_ge(W.xT_ok, n + 1)
                wait(act, W.up_ok, (n - 1) * UN)
                cols = cols_of(kind)
                copy(x_hi[:, buf * 512:buf * 512 + cols], tr_ps[:, 0:cols]).then_inc(W.xhi_ok, 1)

            def comb_out(n, buf, kind):
                act.wait_ge(W.combT_ok, n + 1)
                wait(act, W.comb3_ok, n - 1)
                wait(act, W.comb_w, (n - 1) * 16)
                cols = cols_of(kind)
                copy(combT[buf][:, 0:cols], mx_ps[0:3 * E, 0:cols]).then_inc(W.combT_sb, 1)
                wait(act, W.down_ok, (n - 1) * UN + 1)
                nc.scalar.mul(comb3[:, 0:cols], mx_ps[0:3 * E, 0:cols], low_rows).then_inc(W.comb3_hi, 1)

            def keep_h1(n, buf, kind):
                p, w = tiles_of(kind)
                act.wait_ge(W.h1_ok, n + 1)
                wait(act, W.o_ok, n - 1)
                copy(h1[buf][0:p, 0:w * D], h1_new[0:p, 0:w * D]).then_inc(W.kept_ok, 1)

            def down_copy(n, kind):
                act.wait_ge(W.down_ok, (n + 1) * UN)
                wait(act, W.outT_ok, n)
                cols = cols_of(kind)
                copy(down_sb[:, 0:cols], down_ps[:, 0:cols]).then_inc(W.down_out, 1)

            def silu(c, u, kind):
                q = c * UN + u
                e, t = divmod(u, HT)
                cols = cols_of(kind)
                act.wait_ge(W.gate_ok, q + 1)
                wait(act, W.silc_ok, q - 3)
                nc.scalar.activation(sil[u % 4][:, 0:cols], gate_ps[u % 2][:, 0:cols], ACT.Silu,
                                     bias=bguT[:, 4 * e + t:4 * e + t + 1]).then_inc(W.sil_ok, 1)

            def hidden_high(c, u, kind):
                q = c * UN + u
                cols = cols_of(kind)
                act.wait_ge(W.h_ok, q + 1)
                wait(act, W.down_ok, q - RING + 1)
                r = u % RING
                copy(h_hi[:, r * 512:r * 512 + cols], h_f[u % 4][:, 0:cols]).then_inc(W.hhi_ok, 1)

            image_y(0, "img")
            image_z(LAST - 3)
            image_z(LAST - 2)
            x_high(0, 0, "img")
            image_z(LAST - 1)
            act.wait_ge(W.im_tr, len(STEPS) * NSRC)
            comb_out(0, 0, "img")
            image_z(LAST)
            keep_h1(0, 0, "img")
            image_y(1, "img")
            act.wait_ge(W.im_conv, len(STEPS))

            def chunk(c, buf, kind, before, after, after2, load):
                for u in range(UN):
                    silu(c, u, kind)
                    if u == ACT_AT["down_copy"] and before:
                        down_copy(c - 1, before)
                    if u >= SPLIT:
                        hidden_high(c, u - SPLIT, kind)
                    elif before:
                        hidden_high(c - 1, UN + u - SPLIT, before)
                    if u == ACT_AT["x_high"] and after:
                        x_high(c + 1, 1 - buf, after)
                    if u == ACT_AT["keep_h1"] and after:
                        keep_h1(c + 1, 1 - buf, after)
                    if u == ACT_AT["comb_out"] and after:
                        comb_out(c + 1, 1 - buf, after)
                    if u == ACT_AT["image_y"] and after2 in ("img", "short"):
                        image_y(c + 2, after2)

            run(chunk, act)
            for u in range(UN - SPLIT, UN):
                hidden_high(LAST_CHUNK, u, "short")
            down_copy(LAST_CHUNK, "short")

        @block.gpsimd
        def _(pool):
            tt = nc.gpsimd.tensor_tensor
            nc.gpsimd.memset(euler[:, :], 2.718281828459045).then_inc(W.setup, 1)
            nc.gpsimd.memset(nhalf[:, :], -0.5).then_inc(W.setup, 1)
            pool.wait_ge(W.setup, 2)
            pool.wait_ge(W.dec1, 1)
            tt(dec[:, 2:3], euler[:, 0:1], dec[:, 1:2], ALU.pow).then_inc(W.dec2, 1)
            pool.wait_ge(W.powin, 1)
            pool.wait_ge(W.const, 16)
            tt(pows[:, 0:NA + NB], dec_b[:, 0:NA + NB], cst[:, C_EXP:C_EXP + NA + NB], ALU.pow).then_inc(W.pow_done, 1)

            pool.wait_ge(W.wg_hi_done, 1)
            tt(wg_split[:, E:2 * E], wg[:, :], wg_split[:, 0:E].bitcast(F32), ALU.subtract).then_inc(W.wg_lo_done, 1)

            pool.wait_ge(W.bd3_hi, 1)
            tt(bd3[:, :], bd_raw, bd3[:, :].bitcast(F32), ALU.subtract).then_inc(W.bd3_ok, 1)

            def weight_low(i):
                pool.wait_ge(W.wsplit_hi, i + 1)
                tt(pieces[i][3], wraw[i % 2], pieces[i][2].bitcast(F32), ALU.subtract).then_inc(W.wsplit_lo, 1)

            def rstd(out_, var, w, ready, done, count, p):
                pool.wait_ge(ready, count)
                tt(out_[0:p, 0:w], var[0:p, 0:w], nhalf[0:p, 0:w], ALU.pow).then_inc(done, 1)

            def decayed_image_sums(i):
                g, nx0, w = SUM_PARTS[i]
                nx1 = nx0 + w
                yv = y_img.rearrange("p (g x y b) -> p g x y b", x=NY, g=G, b=GB)[:, g, nx0:nx1]
                tt(yv, cum_i.rearrange("p (b y x) -> p x y b", b=GB, y=NY)[:, nx0:nx1],
                   pow_t[:, REV:REV + T_IMG].rearrange("p (o y x) -> p x y o", o=1, y=NY)[:, nx0:nx1]
                   .to_broadcast([P, w, NY, GB]), ALU.mult).then_inc(W.im_y, 1)

            def norm2(n, kind):
                p, w = tiles_of(kind)
                wait(pool, W.x2_ok, n)
                rstd(rs2, ve2, w, W.ve2_ok, W.rs2_ok, n + 1, p)

            def comb_low(n, buf, kind):
                cols = cols_of(kind)
                pool.wait_ge(W.comb3_hi, n + 1)
                tt(comb3[:, 0:cols], combT[buf][:, 0:cols], comb3[:, 0:cols].bitcast(F32), ALU.subtract).then_inc(W.comb3_ok, 1)

            def gate_exp(n, kind):
                p, w = tiles_of(kind)
                pool.wait_ge(W.gap_ok, n + 1)
                wait(pool, W.w1_ok, n)
                tt(ex[0:p, 0:w], euler[0:p, 0:w], gap[0:p, 0:w], ALU.pow).then_inc(W.ex_ok, 1)

            weight_low(0)
            weight_low(1)
            rstd(ims[:, 5:6], ims[:, 4:5], 1, W.im_eps, W.im_rstd, 1, PI)
            tt(pows[:, NA + NB:], dec_b[:, NA + NB:], cst[:, C_EXP + NA + NB:C_LOW], ALU.pow).then_inc(W.pow_done, 1)
            for i in range(2, EARLY):
                weight_low(i)
            for s in range(len(STEPS)):
                g, nx0, w = STEPS[s]
                if s == KG - 3:
                    rstd(ims[:, 5:6], ims[:, 4:5], 1, W.im_eps, W.im_rstd, 2, PI)
                if s == KG:
                    pool.wait_ge(W.im_cum, 1)
                    pool.wait_ge(W.im_pad, G)
                    pool.wait_ge(W.im_pad_act, G)
                    decayed_image_sums(0)
                wait(pool, W.im_z, s)
                rstd(rs1, ve1, w, W.im_ve, W.im_rs, s + 1, PI)
                pool.wait_ge(W.im_neg, s + 1)
                pool.wait_ge(W.im_rs, s + 1)
                tt(sh1[0:PI, 0:w], nm1[0:PI, 0:w], rs1[0:PI, 0:w], ALU.mult).then_inc(W.im_sh, 1)
                for i in range(EARLY + 2 * s, min(EARLY + 2 * s + 2, PIECES)):
                    weight_low(i)
                if s == KG + 1:
                    norm2(0, "img")
                if s == LAST - 1:
                    gate_exp(0, "img")
                pool.wait_ge(W.im_z, s + 1)
                for i in range(w):
                    o = h_tiles[:, nx0 + i, g, :]
                    last = tt(o, o, mixb[0:PI, :], ALU.add)
                last.then_inc(W.im_hI, 1)
                if s == KG + 1:
                    decayed_image_sums(1)
                    decayed_image_sums(2)

            def norm1(n):
                wait(pool, W.z_ok, n - IMG_CHUNKS)
                rstd(rs1, ve1, W4, W.ve1_ok, W.rs1_ok, n - IMG_CHUNKS + 1, P)

            def text_bias(n):
                pool.wait_ge(W.xt, (n - IMG_CHUNKS + 1) * 16)
                pool.wait_ge(W.h1_ok, n)
                tt(h_bias.rearrange("p (j d) -> p j d", j=W4), xt.rearrange("p (j d) -> p j d", j=W4),
                   mixb[:, :].rearrange("p (o d) -> p o d", o=1).to_broadcast([P, W4, D]), ALU.add).then_inc(W.hb_ok, 1)

            def text_y(n):
                pool.wait_ge(W.cum_ok, n - IMG_CHUNKS + 1)
                pool.wait_ge(W.mix_ok, n)
                tt(yT, cum, pow_t[:, REV + T_IMG:REV + T], ALU.mult).then_inc(W.y_ok, 1)

            def weigh(c, u, kind):
                q = c * UN + u
                e, t = divmod(u, HT)
                cols = cols_of(kind)
                if t == 0:
                    pool.wait_ge(combb[e], (c + 1) * 16)
                pool.wait_ge(W.sil_ok, q + 1)
                wait(pool, W.h_ok, q - 3)
                tt(silc[u % 4][:, 0:cols], sil[u % 4][:, 0:cols], comb_b[:, e * 512:e * 512 + cols],
                   ALU.mult).then_inc(W.silc_ok, 1)

            def chunk(c, buf, kind, before, after, after2, load):
                for u in range(UN):
                    weigh(c, u, kind)
                    if not before:
                        if u == 1:
                            comb_low(0, 0, "img")
                        if u == 3:
                            pool.wait_ge(W.im_cum, G)
                            decayed_image_sums(3)
                        if u == 5:
                            decayed_image_sums(4)
                    if u == POOL_AT["norm2"] and after:
                        norm2(c + 1, after)
                    if u == POOL_AT["gate_exp"] and after:
                        gate_exp(c + 1, after)
                    if u == POOL_AT["comb_low"] and after:
                        comb_low(c + 1, 1 - buf, after)
                    if after2 == "txt":
                        if u == POOL_AT["norm1"]:
                            norm1(c + 2)
                        if u == POOL_AT["text_bias"]:
                            text_bias(c + 2)
                        if u == POOL_AT["text_y"]:
                            text_y(c + 2)

            run(chunk, pool)

        @block.vector
        def _(dve):
            V = nc.vector
            dve.wait_ge(W.ldec, 16)
            V.tensor_scalar(dec[:, 1:2], dec[:, 0:1], -1.0, None, ALU.mult).then_inc(W.dec1, 1)
            V.memset(one[:, :], 1.0).then_inc(W.small, 1)
            V.memset(zpad[:, :], 0.0).then_inc(W.small, 1)
            zeros = 4 * 2 * PATCH * HP
            V.memset(recs[:, 144:150], 0.0).then_inc(W.small, 1)
            dve.wait_ge(W.small, 3)
            V.memset(recs[:, 144:145], zeros / 2).then_inc(W.small, 1)
            V.memset(recs[:, 147:148], zeros / 2).then_inc(W.small, 1)
            dve.wait_ge(W.dec2, 1)
            V.tensor_scalar(dec[:, 3:4], dec[:, 2:3], 1.0, None, ALU.add).then_inc(W.dec3, 1)
            dve.wait_ge(W.dec3, 1)
            V.reciprocal(dec[:, 0:1], dec[:, 3:4]).then_inc(W.dec3, 1)
            dve.wait_ge(W.dec3, 2)
            V.tensor_copy(dec_b, dec[:, 0:1].to_broadcast([P, 2 * (NA + NB)])).then_inc(W.powin, 1)
            dve.wait_ge(W.const, 16)
            V.memset(xraw5[96:PI, 1, :, HP:PATCH, :], 0.0).then_inc(W.small, 1)
            V.memset(xraw5[0:GB, 2, :, 0:HP, :], 0.0).then_inc(W.small, 1)
            dve.wait_ge(W.gb, 64)
            for j in range(0, NSRC, 2):
                V.tensor_copy(patch5[0:2 * NY, j, :, :, :],
                              gb_of[j]
                              ).then_inc(W.gb_even, 1)
            dve.wait_ge(W.small, 7)

            def image_stats(g, t):
                if t < 3:
                    dve.wait_ge([W.gx0, W.gx1, W.gx2][t], 16 * [2, 4, 4][t] * (g + 1))
                    k = 4 * t
                    for c in range(2):
                        for r in range(0, PATCH, HP):
                            last = V.bn_stats(recs[0:PI, 6 * k:6 * k + 6],
                                              xraw5[0:PI, t, c, r:r + HP, 0:S] if t == 0 else xraw5[0:PI, t, c, r:r + HP, HP:S - HP])
                            k += 1
                else:
                    k = 12
                    for q in (1, 2):
                        for c0 in (0, S - HP):
                            last = V.bn_stats(recs[0:PI, 6 * k:6 * k + 6],
                                              xraw5[0:PI, q, :, :, c0:c0 + HP].rearrange("p c r w -> p (c r) w"))
                            k += 1
                last.then_inc(W.im_stat, 1)

            def image_moments(g):
                dve.wait_ge(W.im_stat, 5 * g + 4)
                V.tensor_copy(recs[0:PI, 96:144], recs[0:PI, 24:72]).then_inc(W.im_stat, 1)
                dve.wait_ge(W.im_stat, 5 * g + 5)
                V.bn_aggr(mvi[0:PI, :], recs[0:PI, :]).then_inc(W.im_aggr, 1)
                wait(dve, W.im_pad_act, g)

            def image_squares(g):
                dve.wait_ge(W.im_aggr, g + 1)
                dve.wait_ge(W.im_mean, g + 1)
                V.tensor_copy(ims[0:PI, 0:1], avg_ps[0:PI, 0:1]).then_inc(W.im_dev, 1)
                dve.wait_ge(W.im_dev, 2 * g + 1)
                V.tensor_tensor(ims[0:PI, 1:2], mvi[0:PI, 0:1], ims[0:PI, 0:1], ALU.subtract).then_inc(W.im_dev, 1)
                dve.wait_ge(W.im_dev, 2 * g + 2)
                V.scalar_tensor_tensor(ims[0:PI, 2:3], ims[0:PI, 1:2], ims[0:PI, 1:2], mvi[0:PI, 1:2],
                                       ALU.mult, ALU.add).then_inc(W.im_sq, 1)

            def image_eps(g):
                dve.wait_ge(W.im_var, g + 1)
                V.tensor_scalar(ims[0:PI, 4:5], avg_ps[0:PI, 1:2], 1e-7, None, ALU.add).then_inc(W.im_eps, 1)

            def image_norm(g):
                dve.wait_ge(W.im_rstd, g + 1)
                V.scalar_tensor_tensor(ims[0:PI, 3:4], ims[0:PI, 0:1], -1.0, ims[0:PI, 5:6], ALU.mult, ALU.mult).then_inc(W.im_shift, 1)
                if g == 0:
                    dve.wait_ge(W.gbT, NSRC)
                else:
                    dve.wait_ge(W.im_tr, KG * NSRC)
                sc = (ims[0:PI, 0:1], ims[0:PI, 5:6], ALU.subtract, ALU.mult)
                V.tensor_scalar(patch5[0:PI, 0], xraw5[0:PI, 0].rearrange("p c r (x w) -> p (c r) x w", w=PATCH), *sc)
                for j in range(1, ACT_SOURCES[g]):
                    for dst, v in shifted(j):
                        last = V.tensor_scalar(dst, v, *sc)
                last.then_inc(W.im_pad, 1)

            def image_gamma(s):
                g, nx0, w = STEPS[s]
                wait(dve, W.im_conv, s - 1)
                for j in range(NSRC):
                    dve.wait_ge(W.im_tr, s * NSRC + j + 1)
                    V.tensor_tensor(xgT[s % 2][:, j * W4 * PI:(j * W4 + w) * PI].rearrange("p (x y b) -> p x y b", x=w, b=GB),
                                    quad[j][:, 0:w * PI].rearrange("p (x y b) -> p x y b", x=w, b=GB),
                                    gbT4[:, j, nx0:nx0 + w, 0:NY].unsqueeze(3).to_broadcast([P, w, NY, GB]),
                                    ALU.mult).then_inc(W.im_xg, 1)

            def image_tokens(s):
                g, nx0, w = STEPS[s]
                dve.wait_ge(W.im_conv, s + 1)
                hv = h_tiles[:, nx0:nx0 + w, g, :]
                V.tensor_tensor(hv, conv_ps[s % 2][0:PI, 0:w * D].rearrange("p (x d) -> p x d", d=D),
                                hv, ALU.add).then_inc(W.im_h, 1)
                dve.wait_ge(W.im_h, s + 1)
                for i in range(w):
                    last = V.bn_stats(rec1[0:PI, 6 * i:6 * i + 6], hv[:, i, :])
                last.then_inc(W.im_rec, 1)
                dve.wait_ge(W.im_rec, s + 1)
                wait(dve, W.im_neg, s)
                wait(dve, W.im_ve, s)
                for i in range(w):
                    last = V.bn_aggr(mv1[0:PI, 2 * i:2 * i + 2], rec1[0:PI, 6 * i:6 * i + 6])
                last.then_inc(W.im_mv, 1)
                dve.wait_ge(W.im_mv, s + 1)
                wait(dve, W.im_rs, s)
                V.tensor_scalar(ve1[0:PI, 0:w], mv1[0:PI, 1:2 * w:2], 1e-5, None, ALU.add).then_inc(W.im_ve, 1)
                wait(dve, W.im_sh, s)
                V.tensor_scalar(nm1[0:PI, 0:w], mv1[0:PI, 0:2 * w:2], -1.0, None, ALU.mult).then_inc(W.im_neg, 1)

            def image_decay(s):
                g, nx0, w = STEPS[s]
                dve.wait_ge(W.im_zT, s + 1)
                if s % KG == 0:
                    wait(dve, W.im_cum, g)
                V.tensor_tensor(zs_i.rearrange("p (b y x) -> p x y b", b=GB, y=NY)[:, nx0:nx0 + w],
                                tr_ps[:, 0:w * PI].rearrange("p (x y b) -> p x y b", x=w, b=GB),
                                pow_s[:, 0:T_IMG].rearrange("p (y x o) -> p x y o", o=1, y=NY)[:, nx0:nx0 + w]
                                .to_broadcast([P, w, NY, GB]), ALU.mult).then_inc(W.im_zs, 1)

            def image_sums(g):
                dve.wait_ge(W.im_zs, (g + 1) * KG)
                wait(dve, W.im_y, 3 * g)
                if g == 0:
                    dve.wait_ge(W.wsplit_lo, PIECES)
                    dve.wait_ge(W.bd3_ok, 1)
                for b in range(GB):
                    last = V.tensor_tensor_scan(cum_i[:, b * T_IMG:(b + 1) * T_IMG], one[:, :].to_broadcast([P, T_IMG]),
                                                zs_i[:, b * T_IMG:(b + 1) * T_IMG], 0.0, ALU.mult, ALU.add)
                last.then_inc(W.im_cum, 1)
                dve.wait_ge(W.im_cum, g + 1)
                V.tensor_copy(carry[:, g * GB:(g + 1) * GB], cum_i[:, T_IMG - 1:GB * T_IMG:T_IMG]).then_inc(W.im_carry, 1)

            def mixed(n, kind):
                p, w = tiles_of(kind)
                dve.wait_ge(W.mix_ok, n + 1)
                if kind == "txt":
                    dve.wait_ge(W.hb_ok, n - IMG_CHUNKS + 1)
                    skip = h_bias
                else:
                    dve.wait_ge(W.im_hI, needed(STEPS, n))
                    first = tiles_before(n)
                    skip = h_img[0:p, first * D:(first + w) * D]
                wait(dve, W.kept_ok, n)
                wait(dve, W.x2_ok, n)
                V.tensor_tensor(h1_new[0:p, 0:w * D], mx_ps[0:p, 0:w * D], skip, ALU.add).then_inc(W.h1_ok, 1)

            def mixed_stats(n, kind):
                p, w = tiles_of(kind)
                dve.wait_ge(W.h1_ok, n + 1)
                wait(dve, W.mv2_ok, n)
                for i in range(w):
                    last = V.bn_stats(rec2[0:p, 6 * i:6 * i + 6], h1_new[0:p, i * D:(i + 1) * D])
                last.then_inc(W.rec2_ok, 1)

            def mixed_var(n, kind):
                p, w = tiles_of(kind)
                dve.wait_ge(W.rec2_ok, n + 1)
                wait(dve, W.x2_ok, n)
                wait(dve, W.ve2_ok, n)
                dve.nop(nofuse=True)
                for i in range(w):
                    last = V.bn_aggr(mv2[0:p, 2 * i:2 * i + 2], rec2[0:p, 6 * i:6 * i + 6])
                last.then_inc(W.mv2_ok, 1)
                dve.wait_ge(W.mv2_ok, n + 1)
                wait(dve, W.rs2_ok, n)
                V.tensor_scalar(ve2[0:p, 0:w], mv2[0:p, 1:2 * w:2], 1e-5, None, ALU.add).then_inc(W.ve2_ok, 1)

            def norm_apply(n, kind):
                p, w = tiles_of(kind)
                dve.wait_ge(W.rs2_ok, n + 1)
                wait(dve, W.xT_ok, n)
                for i in range(w):
                    last = V.tensor_scalar(x2[0:p, i * D:(i + 1) * D], h1_new[0:p, i * D:(i + 1) * D],
                                           mv2[0:p, 2 * i:2 * i + 1], rs2[0:p, i:i + 1], ALU.subtract, ALU.mult)
                last.then_inc(W.x2_ok, 1)

            def x_low(n, buf, kind):
                cols = cols_of(kind)
                dve.wait_ge(W.xhi_ok, n + 1)
                V.tensor_tensor(x_lo[:, buf * 512:buf * 512 + cols], tr_ps[:, 0:cols],
                                x_hi[:, buf * 512:buf * 512 + cols].bitcast(F32), ALU.subtract).then_inc(W.xlo_ok, 1)

            def top_value(n, kind):
                p, w = tiles_of(kind)
                dve.wait_ge(W.lg_ok, n + 1)
                wait(dve, W.idx_ok, n)
                wait(dve, W.gap_ok, n)
                V.tensor_reduce(lg[0:p, 0:w * E], tr_ps[0:p, 0:w * 2 * E].rearrange("p (i k e) -> p i e k", k=2, e=E),
                                mybir.AxisListType.X, ALU.add).then_inc(W.lsum_ok, 1)
                dve.wait_ge(W.lsum_ok, n + 1)
                dve.nop(nofuse=True)
                for i in range(w):
                    last = V.max(top8[0:p, i * E:(i + 1) * E], lg[0:p, i * E:(i + 1) * E])
                last.then_inc(W.top_ok, 1)

            def top_index(n, kind):
                p, w = tiles_of(kind)
                dve.wait_ge(W.top_ok, n + 1)
                wait(dve, W.hit_ok, n)
                dve.nop(nofuse=True)
                for i in range(w):
                    last = V.max_index(idx8[0:p, i * E:(i + 1) * E], top8[0:p, i * E:(i + 1) * E],
                                       lg[0:p, i * E:(i + 1) * E])
                last.then_inc(W.idx_ok, 1)
                wait(dve, W.ex_ok, n)
                V.tensor_tensor(gap[0:p, 0:w], top8[0:p, 1:w * E:E], top8[0:p, 0:w * E:E], ALU.subtract).then_inc(W.gap_ok, 1)

            def routing(n, kind):
                p, w = tiles_of(kind)
                dve.wait_ge(W.idx_ok, n + 1)
                wait(dve, W.hitw_ok, n)
                top2 = idx8[0:p, 0:w * E].rearrange("p (i e) -> p i e", e=E)[:, :, 0:2]
                V.tensor_tensor(hit[0:p, 0:w * 2 * E].rearrange("p (i k e) -> p i k e", k=2, e=E),
                                iota[0:p].unsqueeze(1).unsqueeze(1).to_broadcast([p, w, 2, E]),
                                top2.unsqueeze(3).to_broadcast([p, w, 2, E]), ALU.is_equal).then_inc(W.hit_ok, 1)
                dve.wait_ge(W.ex_ok, n + 1)
                wait(dve, W.w0_ok, n)
                V.tensor_scalar(ex1[0:p, 0:w], ex[0:p, 0:w], 1.0, None, ALU.add).then_inc(W.ex1_ok, 1)
                dve.wait_ge(W.ex1_ok, n + 1)
                V.reciprocal(w2[0:p, 0:2 * w:2], ex1[0:p, 0:w]).then_inc(W.w0_ok, 1)
                dve.wait_ge(W.w0_ok, n + 1)
                V.tensor_tensor(w2[0:p, 1:2 * w:2], ex[0:p, 0:w], w2[0:p, 0:2 * w:2], ALU.mult).then_inc(W.w1_ok, 1)

            def routing_sum(n, kind):
                p, w = tiles_of(kind)
                dve.wait_ge(W.w1_ok, n + 1)
                dve.wait_ge(W.hit_ok, n + 1)
                wait(dve, W.comb_ok, n)
                V.tensor_tensor(hitw[0:p, 0:w * 2 * E].rearrange("p (i e) -> p i e", e=E),
                                hit[0:p, 0:w * 2 * E].rearrange("p (i e) -> p i e", e=E),
                                w2[0:p, 0:2 * w].unsqueeze(2).to_broadcast([p, 2 * w, E]), ALU.mult).then_inc(W.hitw_ok, 1)
                dve.wait_ge(W.hitw_ok, n + 1)
                wait(dve, W.combT_ok, n)
                hw = hitw[0:p, 0:w * 2 * E].rearrange("p (i k e) -> p i k e", k=2, e=E)
                V.tensor_tensor(comb[0:p, 0:w * 3 * E].rearrange("p (i r e) -> p i r e", r=3, e=E),
                                hw[:, :, 0:1, :].to_broadcast([p, w, 3, E]), hw[:, :, 1:2, :].to_broadcast([p, w, 3, E]),
                                ALU.add).then_inc(W.comb_ok, 1)

            for t in range(4):
                image_stats(0, t)
            image_moments(0)
            image_squares(0)
            image_eps(0)
            image_norm(0)
            dve.wait_ge(W.beta_tr, 1)
            image_gamma(0)
            for s in range(len(STEPS)):
                if s == KG - 2:
                    image_stats(1, 2)
                    image_stats(1, 3)
                    image_moments(1)
                if s == KG - 1:
                    image_norm(1)
                elif s < LAST:
                    image_gamma(s + 1)
                if s == KG - 2:
                    image_squares(1)
                    image_eps(1)
                if s == 0:
                    dve.wait_ge(W.pow_done, 2)
                    for dst, o in ((pow_s, 0), (pow_t, NA + NB)):
                        V.tensor_tensor(dst[:, :].rearrange("p (a b) -> p a b", a=NA),
                                        pows[:, o:o + NA].unsqueeze(2).to_broadcast([P, NA, NB]),
                                        pows[:, o + NA:o + NA + NB].unsqueeze(1).to_broadcast([P, NA, NB]),
                                        ALU.mult).then_inc(W.powers, 1)
                    dve.wait_ge(W.bias_done, 4)
                    dve.wait_ge(W.powers, 2)
                if s == 1:
                    image_stats(1, 0)
                    image_stats(1, 1)
                if s == LAST:
                    norm_apply(0, "img")
                    image_decay(s - 2)
                    x_low(0, 0, "img")
                if s == KG + 1:
                    image_decay(s - 2)
                    image_sums(0)
                if s > 0:
                    image_tokens(s - 1)
                if 1 < s < LAST and s != KG + 1:
                    image_decay(s - 2)
                if s == LAST - 1:
                    dve.wait_ge(W.im_pad, G)
                    dve.wait_ge(W.im_pad_act, G)
                    mixed(0, "img")
                    mixed_stats(0, "img")
                    mixed_var(0, "img")
                if s == KG - 1:
                    image_gamma(s + 1)
            top_value(0, "img")
            top_index(0, "img")
            image_tokens(LAST)
            routing(0, "img")
            routing_sum(0, "img")
            image_decay(LAST - 1)
            image_decay(LAST)
            image_sums(1)
            dve.wait_ge(W.im_carry, G)

            def text_stats(n):
                b = n - IMG_CHUNKS
                dve.wait_ge(W.xt, (b + 1) * 16)
                wait(dve, W.mv1_ok, b)
                for i in range(W4):
                    last = V.bn_stats(rec1[:, 6 * i:6 * i + 6], xt[:, i * D:(i + 1) * D])
                last.then_inc(W.rec1_ok, 1)

            def text_var(n):
                b = n - IMG_CHUNKS
                dve.wait_ge(W.rec1_ok, b + 1)
                wait(dve, W.z_ok, b)
                wait(dve, W.ve1_ok, b)
                dve.nop(nofuse=True)
                for i in range(W4):
                    last = V.bn_aggr(mv1[:, 2 * i:2 * i + 2], rec1[:, 6 * i:6 * i + 6])
                last.then_inc(W.mv1_ok, 1)
                dve.wait_ge(W.mv1_ok, b + 1)
                wait(dve, W.rs1_ok, b)
                V.tensor_scalar(ve1[:, :], mv1[:, 1:2 * W4:2], 1e-5, None, ALU.add).then_inc(W.ve1_ok, 1)

            def text_norm(n):
                b = n - IMG_CHUNKS
                dve.wait_ge(W.rs1_ok, b + 1)
                wait(dve, W.zT_ok, b)
                for i in range(W4):
                    last = V.tensor_scalar(z[:, i * D:(i + 1) * D], xt[:, i * D:(i + 1) * D], mv1[:, 2 * i:2 * i + 1],
                                           rs1[:, i:i + 1], ALU.subtract, ALU.mult)
                last.then_inc(W.z_ok, 1)

            def text_decay(n):
                b = n - IMG_CHUNKS
                dve.wait_ge(W.zT_ok, b + 1)
                wait(dve, W.cum_ok, b)
                V.tensor_tensor(zs.rearrange("p (q j) -> p q j", j=W4), tr_ps[:, :].rearrange("p (j q) -> p q j", j=W4),
                                pow_s[:, T_IMG:T].rearrange("p (q j) -> p q j", j=W4), ALU.mult).then_inc(W.zs_ok, 1)

            def text_sums(n):
                b = n - IMG_CHUNKS
                dve.wait_ge(W.zs_ok, b + 1)
                dve.wait_ge(W.y_ok, n)
                V.tensor_tensor_scan(cum, one[:, :].to_broadcast([P, T_TXT]), zs, carry[:, bass.ds(b, 1)],
                                     ALU.mult, ALU.add).then_inc(W.cum_ok, 1)

            def hidden(c, u, kind):
                q = c * UN + u
                e, t = divmod(u, HT)
                cols = cols_of(kind)
                dve.wait_ge(W.up_ok, q + 1)
                dve.wait_ge(W.silc_ok, q + 1)
                wait(dve, W.hhi_ok, q - 3)
                wait(dve, W.hlo_ok, q - 3)
                k = 4 * e + HT + t
                V.scalar_tensor_tensor(h_f[u % 4][:, 0:cols], up_ps[UP_BANK[u]][:, 0:cols], bguT[:, k:k + 1],
                                       silc[u % 4][:, 0:cols], ALU.add, ALU.mult).then_inc(W.h_ok, 1)

            def hidden_low(c, u, kind):
                q = c * UN + u
                cols = cols_of(kind)
                dve.wait_ge(W.hhi_ok, q + 1)
                wait(dve, W.down_ok, q - RING + 1)
                r = u % RING
                V.tensor_tensor(h_lo[:, r * 512:r * 512 + cols], h_f[u % 4][:, 0:cols],
                                h_hi[:, r * 512:r * 512 + cols].bitcast(F32), ALU.subtract).then_inc(W.hlo_ok, 1)

            def result(n, buf, kind):
                p, w = tiles_of(kind)
                dve.wait_ge(W.outT_ok, n + 1)
                dve.wait_ge(W.kept_ok, n + 1)
                wait(dve, W.store, stores_before(n, kind) * 16)
                V.tensor_tensor(o_sb[0:p, 0:w * D], mx_ps[0:p, 0:w * D], h1[buf][0:p, 0:w * D], ALU.add).then_inc(W.o_ok, 1)

            def chunk(c, buf, kind, before, after, after2, load):
                for u in range(UN):
                    hidden(c, u, kind)
                    if u >= SPLIT:
                        hidden_low(c, u - SPLIT, kind)
                    elif before:
                        hidden_low(c - 1, UN + u - SPLIT, before)
                    if after:
                        for name, step in (("mixed", mixed), ("mixed_stats", mixed_stats), ("mixed_var", mixed_var),
                                           ("norm_apply", norm_apply), ("top_value", top_value), ("top_index", top_index),
                                           ("routing", routing), ("routing_sum", routing_sum)):
                            if u == DVE_AT[name]:
                                step(c + 1, after)
                        if u == DVE_AT["x_low"]:
                            x_low(c + 1, 1 - buf, after)
                    if u == DVE_AT["result"] and before:
                        result(c - 1, 1 - buf, before)
                    if after2 == "txt":
                        for name, step in (("text_stats", text_stats), ("text_var", text_var), ("text_norm", text_norm),
                                           ("text_decay", text_decay), ("text_sums", text_sums)):
                            if u == DVE_AT[name]:
                                step(c + 2)

            run(chunk, dve)
            for u in range(UN - SPLIT, UN):
                hidden_low(LAST_CHUNK, u, "short")
            result(LAST_CHUNK, LAST_CHUNK % 2, "short")


_INS = ["x", "txt", "L0_tok_gamma", "L0_tok_beta", "L0_tok_W", "L0_tok_b", "L0_attn_log_decay", "L0_attn_mix_w",
        "L0_attn_mix_b", "L0_ffn_Wg", "L0_ffn_Wgu", "L0_ffn_bgu", "L0_ffn_Wd", "L0_ffn_bd"]


def shape_constants():
    import numpy as np
    c = np.zeros((P, C_W), np.float32)
    c[:, C_ID:C_ID + P] = np.eye(P)
    q = np.arange(PI)
    c[0:PI, C_AVG:C_AVG + PI] = (q[:, None] % GB == q[None, :] % GB) / NY
    c[:, C_IOTA:C_IOTA + E] = np.arange(E)
    c[E:2 * E, C_LOW] = 1
    c[2 * E:3 * E, C_LOW + 1] = 1
    c[:, C_EXP:C_LOW] = np.concatenate([NB * np.arange(NA), np.arange(NB), NB * np.arange(NA)[::-1], np.arange(NB)[::-1]])
    return c


def kernel(**inputs):
    import numpy as _np
    import concourse.bacc as _bacc
    from concourse import mybir as _mybir
    from concourse.bass_utils import run_bass_kernel_spmd as _run

    nc = _bacc.Bacc("TRN2", target_bir_lowering=False, num_devices=1)
    arrays, args = {}, []
    for name in _INS:
        a = _np.ascontiguousarray(inputs[name])
        if name == "L0_tok_W":
            a = a.reshape(D, -1)
        arrays[f"in_{name}_dram"] = a
        args.append(nc.dram_tensor(f"in_{name}_dram", a.shape, _mybir.dt.from_np(a.dtype), kind="ExternalInput").ap())
    c = shape_constants()
    arrays["in_const_dram"] = c
    args.append(nc.dram_tensor("in_const_dram", c.shape, _mybir.dt.from_np(c.dtype), kind="ExternalInput").ap())
    args.append(nc.dram_tensor("comb_dram", (2, E, 512), F32, kind="Internal").ap())
    args.append(nc.dram_tensor("out_0_dram", (B, T, D), F32, kind="ExternalOutput").ap())
    program(nc, *args)
    r = _run(nc, [arrays], core_ids=[0])
    return r.results[0]["out_0_dram"]
```
